# Optimizing a Trainium2 kernel written in Bass

```python
import numpy as np
import jax
import jax.numpy as jnp

def _softmax(x, axis=-1):
    return jax.nn.softmax(x, axis=axis)

def _gelu(x):
    return jax.nn.gelu(x, approximate=True)

def _silu(x):
    return jax.nn.silu(x)

def _sigmoid(x):
    return jax.nn.sigmoid(x)

def _layernorm(x, axis=-1, eps=1e-05):
    m = jnp.mean(x, axis=axis, keepdims=True)
    v = jnp.var(x, axis=axis, keepdims=True)
    return (x - m) / jnp.sqrt(v + eps)

def _scatter_add(tgt, idx, src, axis=0):
    return tgt.at[idx].add(src)

def _segment_sum(src, seg, n):
    return jax.ops.segment_sum(src, seg, n)
kernel_name = 'mk_cond_seq_d2_seqx_r4_13ce27'

def setup_inputs(seed: int=0):
    np.random.seed(seed)
    _w = jnp.asarray

    def _rec_inputs():
        import jax
        import jax.numpy as jnp
        _rk = jax.random.key(seed)
        x = 1.648e-05 + 1 * jax.random.normal(jax.random.fold_in(_rk, 1), (16, 256, 256), jnp.float32)
        _lenS = 256 - jax.random.randint(jax.random.fold_in(_rk, 7), (16,), 0, max(1, 256 // 4) + 1, jnp.int32)
        _lenS2 = 256 - jax.random.randint(jax.random.fold_in(_rk, 8), (16,), 0, max(1, 256 // 4) + 1, jnp.int32)
        cond_1024 = 0.00191187 + 0.999416 * jax.random.normal(jax.random.fold_in(_rk, 11), (16, 256), jnp.float32)
        _validS = jnp.arange(256)[None, :] < _lenS[:, None]
        _validS2 = jnp.arange(256)[None, :] < _lenS2[:, None]
        _causal = jnp.tril(jnp.ones((256, 256), dtype=bool))
        mask_BxSxSx11_ik0 = jnp.where(jnp.ones((16, 256, 256, 11), dtype=bool), 0, 1).astype(jnp.int32)
        return (x, cond_1024, mask_BxSxSx11_ik0)
    x, cond_1024, mask_BxSxSx11_ik0 = _rec_inputs()

    def _L0_cond_setup():
        import jax, jax.numpy as jnp
        import numpy as np
        NONGT = 20
        H = 16
        NEG = -9000000000000000.0

        def _gat_attention(self_feat, cond_adj, label_bias, Wq, bq, Wk, bk, Wout, bout):
            B, N, F = self_feat.shape
            ng = min(NONGT, N)
            dh = F // H
            kv = self_feat[:, :ng]
            qh = (self_feat @ Wq.T + bq).reshape(B, N, H, dh)
            kh = (kv @ Wk.T + bk).reshape(B, ng, H, dh)
            aff = jnp.einsum('bnhd,bmhd->bnhm', qh, kh) * (1.0 / np.sqrt(dh))
            mask = cond_adj[:, :, None, :] > 0
            aff = jnp.where(mask, aff, NEG) + label_bias[:, :, None, :]
            w = jax.nn.softmax(aff, axis=-1)
            out_t = jnp.einsum('bnhm,bmf->bnhf', w, kv)
            out = jnp.einsum('bnhf,hgf->bnhg', out_t, Wout) + bout.reshape(H, F // H)
            return out.reshape(B, N, F)

        def _forward(v, q, adj, W_self, b_self, w_bias, b_bias, Wq, bq, Wk, bk, Wout, bout):
            adj_f = adj.astype(jnp.float32)
            exp_v = v
            row_zero = exp_v.sum(-1) == 0
            q_exp = jnp.where(row_zero[..., None], 0.0, q[:, None, :])
            vcq = jnp.concatenate([exp_v, q_exp], axis=-1)
            self_feat = vcq @ W_self.T + b_self
            output = self_feat
            for d in range(2):
                A = adj_f if d == 0 else jnp.swapaxes(adj_f, 1, 2)
                A = A[:, :, :NONGT, :]
                cond = A.sum(-1)
                vb = A @ w_bias + b_bias
                output = output + _gat_attention(self_feat, cond, vb, Wq[d], bq[d], Wk[d], bk[d], Wout[d], bout[d])
            rel = jax.nn.relu(output)
            return exp_v + rel
        key = jax.random.key(seed)
        ks = jax.random.split(key, 8)
        B, N, L, F, Q = (64, 36, 11, 256, 256)
        IN = F + Q
        s = 0.02
        return {'v': jax.random.normal(ks[0], (B, N, F), jnp.float32), 'q': jax.random.normal(ks[1], (B, Q), jnp.float32), 'adj': jax.random.randint(ks[2], (B, N, N, L), 0, 2, jnp.int32), 'W_self': jax.random.normal(ks[3], (F, IN), jnp.float32) * s, 'b_self': jnp.zeros((F,), jnp.float32), 'w_bias': jax.random.normal(ks[4], (L,), jnp.float32) * s, 'b_bias': jnp.zeros((), jnp.float32), 'Wq': jax.random.normal(ks[5], (2, F, F), jnp.float32) * s, 'bq': jnp.zeros((2, F), jnp.float32), 'Wk': jax.random.normal(ks[6], (2, F, F), jnp.float32) * s, 'bk': jnp.zeros((2, F), jnp.float32), 'Wout': jax.random.normal(ks[7], (2, H, F // H, F), jnp.float32) * s, 'bout': jnp.zeros((2, F), jnp.float32)}
    _L0_cond_all = _L0_cond_setup()
    _L0_cond_in = {k: v for k, v in _L0_cond_all.items() if k in ('W_self', 'b_self', 'w_bias', 'b_bias', 'Wq', 'bq', 'Wk', 'bk', 'Wout', 'bout')}
    del _L0_cond_all

    def _L1_cond_setup():
        import jax, jax.numpy as jnp
        import numpy as np
        EPS_LN = 1e-06
        EPS_NORM = 1e-12
        MAX_SCALE_MUL = float(np.log(100.0))
        H = 16

        def _ln(x):
            mu = jnp.mean(x, axis=-1, keepdims=True)
            var = jnp.mean((x - mu) ** 2, axis=-1, keepdims=True)
            return (x - mu) / jnp.sqrt(var + EPS_LN)

        def _l2norm(x):
            n = jnp.sqrt(jnp.sum(x * x, axis=-1, keepdims=True))
            return x / jnp.maximum(n, EPS_NORM)
        key = jax.random.key(seed)
        ks = jax.random.split(key, 12)
        B, L, C = (4, 256, 256)
        Ccond, Dff = (256, 1024)
        s = lambda fan: 1.0 / np.sqrt(fan)
        return {'x': jax.random.normal(ks[0], (B, L, C), jnp.float32), 'cond': jax.random.normal(ks[1], (B, Ccond), jnp.float32), 'mat_qkv_w': jax.random.normal(ks[2], (3 * C, C), jnp.float32) * s(C), 'q_bias': jnp.zeros((C,), jnp.float32), 'v_bias': jnp.zeros((C,), jnp.float32), 'scale_mul': jnp.full((1, H, 1, 1), np.log(4.0), jnp.float32), 'proj_w': jax.random.normal(ks[3], (C, C), jnp.float32) * s(C), 'proj_b': jnp.zeros((C,), jnp.float32), 'ada_w': jax.random.normal(ks[4], (6 * C, Ccond), jnp.float32) * s(Ccond), 'ada_b': jnp.zeros((6 * C,), jnp.float32), 'fc1_w': jax.random.normal(ks[5], (Dff, C), jnp.float32) * s(C), 'fc1_b': jnp.zeros((Dff,), jnp.float32), 'fc2_w': jax.random.normal(ks[6], (C, Dff), jnp.float32) * s(Dff), 'fc2_b': jnp.zeros((C,), jnp.float32)}
    _L1_cond_all = _L1_cond_setup()
    _L1_cond_in = {k: v for k, v in _L1_cond_all.items() if k in ('mat_qkv_w', 'q_bias', 'v_bias', 'scale_mul', 'proj_w', 'proj_b', 'ada_w', 'ada_b', 'fc1_w', 'fc1_b', 'fc2_w', 'fc2_b')}
    del _L1_cond_all
    return {'x': x, 'cond_1024': cond_1024, 'mask_BxSxSx11_ik0': mask_BxSxSx11_ik0, 'L0_cond_W_self': _L0_cond_in['W_self'], 'L0_cond_b_self': _L0_cond_in['b_self'], 'L0_cond_w_bias': _L0_cond_in['w_bias'], 'L0_cond_b_bias': _L0_cond_in['b_bias'], 'L0_cond_Wq': _L0_cond_in['Wq'], 'L0_cond_bq': _L0_cond_in['bq'], 'L0_cond_Wk': _L0_cond_in['Wk'], 'L0_cond_bk': _L0_cond_in['bk'], 'L0_cond_Wout': _L0_cond_in['Wout'], 'L0_cond_bout': _L0_cond_in['bout'], 'L1_cond_mat_qkv_w': _L1_cond_in['mat_qkv_w'], 'L1_cond_q_bias': _L1_cond_in['q_bias'], 'L1_cond_v_bias': _L1_cond_in['v_bias'], 'L1_cond_scale_mul': _L1_cond_in['scale_mul'], 'L1_cond_proj_w': _L1_cond_in['proj_w'], 'L1_cond_proj_b': _L1_cond_in['proj_b'], 'L1_cond_ada_w': _L1_cond_in['ada_w'], 'L1_cond_ada_b': _L1_cond_in['ada_b'], 'L1_cond_fc1_w': _L1_cond_in['fc1_w'], 'L1_cond_fc1_b': _L1_cond_in['fc1_b'], 'L1_cond_fc2_w': _L1_cond_in['fc2_w'], 'L1_cond_fc2_b': _L1_cond_in['fc2_b']}

def reference(x, cond_1024, mask_BxSxSx11_ik0, L0_cond_W_self, L0_cond_b_self, L0_cond_w_bias, L0_cond_b_bias, L0_cond_Wq, L0_cond_bq, L0_cond_Wk, L0_cond_bk, L0_cond_Wout, L0_cond_bout, L1_cond_mat_qkv_w, L1_cond_q_bias, L1_cond_v_bias, L1_cond_scale_mul, L1_cond_proj_w, L1_cond_proj_b, L1_cond_ada_w, L1_cond_ada_b, L1_cond_fc1_w, L1_cond_fc1_b, L1_cond_fc2_w, L1_cond_fc2_b):
    import jax
    import jax.numpy as jnp

    def _L0_cond_ref(v, q, adj, W_self, b_self, w_bias, b_bias, Wq, bq, Wk, bk, Wout, bout):
        import jax, jax.numpy as jnp
        import numpy as np
        NONGT = 20
        H = 16
        NEG = -9000000000000000.0

        def _gat_attention(self_feat, cond_adj, label_bias, Wq, bq, Wk, bk, Wout, bout):
            B, N, F = self_feat.shape
            ng = min(NONGT, N)
            dh = F // H
            kv = self_feat[:, :ng]
            qh = (self_feat @ Wq.T + bq).reshape(B, N, H, dh)
            kh = (kv @ Wk.T + bk).reshape(B, ng, H, dh)
            aff = jnp.einsum('bnhd,bmhd->bnhm', qh, kh) * (1.0 / np.sqrt(dh))
            mask = cond_adj[:, :, None, :] > 0
            aff = jnp.where(mask, aff, NEG) + label_bias[:, :, None, :]
            w = jax.nn.softmax(aff, axis=-1)
            out_t = jnp.einsum('bnhm,bmf->bnhf', w, kv)
            out = jnp.einsum('bnhf,hgf->bnhg', out_t, Wout) + bout.reshape(H, F // H)
            return out.reshape(B, N, F)

        def _forward(v, q, adj, W_self, b_self, w_bias, b_bias, Wq, bq, Wk, bk, Wout, bout):
            adj_f = adj.astype(jnp.float32)
            exp_v = v
            row_zero = exp_v.sum(-1) == 0
            q_exp = jnp.where(row_zero[..., None], 0.0, q[:, None, :])
            vcq = jnp.concatenate([exp_v, q_exp], axis=-1)
            self_feat = vcq @ W_self.T + b_self
            output = self_feat
            for d in range(2):
                A = adj_f if d == 0 else jnp.swapaxes(adj_f, 1, 2)
                A = A[:, :, :NONGT, :]
                cond = A.sum(-1)
                vb = A @ w_bias + b_bias
                output = output + _gat_attention(self_feat, cond, vb, Wq[d], bq[d], Wk[d], bk[d], Wout[d], bout[d])
            rel = jax.nn.relu(output)
            return exp_v + rel
        return _forward(v, q, adj, W_self, b_self, w_bias, b_bias, Wq, bq, Wk, bk, Wout, bout)

    def _L1_cond_ref(x, cond, mat_qkv_w, q_bias, v_bias, scale_mul, proj_w, proj_b, ada_w, ada_b, fc1_w, fc1_b, fc2_w, fc2_b):
        import jax, jax.numpy as jnp
        import numpy as np
        EPS_LN = 1e-06
        EPS_NORM = 1e-12
        MAX_SCALE_MUL = float(np.log(100.0))
        H = 16

        def _ln(x):
            mu = jnp.mean(x, axis=-1, keepdims=True)
            var = jnp.mean((x - mu) ** 2, axis=-1, keepdims=True)
            return (x - mu) / jnp.sqrt(var + EPS_LN)

        def _l2norm(x):
            n = jnp.sqrt(jnp.sum(x * x, axis=-1, keepdims=True))
            return x / jnp.maximum(n, EPS_NORM)
        B, L, C = x.shape
        hd = C // H
        ada = jax.nn.silu(cond) @ ada_w.T + ada_b
        ada = ada.reshape(B, 1, 6, C)
        gamma1, gamma2, scale1, scale2, shift1, shift2 = [ada[:, :, i] for i in range(6)]
        x1 = _ln(x) * (scale1 + 1.0) + shift1
        qkv_bias = jnp.concatenate([q_bias, jnp.zeros_like(q_bias), v_bias])
        qkv = (x1 @ mat_qkv_w.T + qkv_bias).reshape(B, L, 3, H, hd)
        q, k, v = [jnp.transpose(qkv[:, :, i], (0, 2, 1, 3)) for i in range(3)]
        sm = jnp.exp(jnp.minimum(scale_mul, MAX_SCALE_MUL))
        q = _l2norm(q) * sm
        k = _l2norm(k)
        scores = jnp.einsum('bhqd,bhkd->bhqk', q, k)
        probs = jax.nn.softmax(scores, axis=-1)
        o = jnp.einsum('bhqk,bhkd->bhqd', probs, v)
        o = jnp.transpose(o, (0, 2, 1, 3)).reshape(B, L, C)
        attn_out = o @ proj_w.T + proj_b
        x = x + attn_out * gamma1
        x2 = _ln(x) * (scale2 + 1.0) + shift2
        h = jax.nn.gelu(x2 @ fc1_w.T + fc1_b, approximate=False)
        ffn_out = h @ fc2_w.T + fc2_b
        x = x + ffn_out * gamma2
        return x
    x = _L0_cond_ref(x, cond_1024, mask_BxSxSx11_ik0, L0_cond_W_self, L0_cond_b_self, L0_cond_w_bias, L0_cond_b_bias, L0_cond_Wq, L0_cond_bq, L0_cond_Wk, L0_cond_bk, L0_cond_Wout, L0_cond_bout)
    x = _L1_cond_ref(x, cond_1024, L1_cond_mat_qkv_w, L1_cond_q_bias, L1_cond_v_bias, L1_cond_scale_mul, L1_cond_proj_w, L1_cond_proj_b, L1_cond_ada_w, L1_cond_ada_b, L1_cond_fc1_w, L1_cond_fc1_b, L1_cond_fc2_w, L1_cond_fc2_b)
    return x

_drawn_inputs = setup_inputs


def setup_inputs(seed=0):
    import zlib

    import numpy as np

    out = dict(_drawn_inputs(seed))
    spreads = {'L0_cond_b_self': (0.0, 0.1),
     'L0_cond_bq': (0.0, 0.1),
     'L0_cond_bk': (0.0, 0.1),
     'L0_cond_bout': (0.0, 0.1),
     'L1_cond_q_bias': (0.0, 0.8),
     'L1_cond_v_bias': (0.0, 0.1),
     'L1_cond_scale_mul': (1.3862943649291992, 0.6),
     'L1_cond_proj_b': (0.0, 0.1),
     'L1_cond_ada_b': (0.0, 0.1),
     'L1_cond_fc1_b': (0.0, 0.1),
     'L1_cond_fc2_b': (0.0, 0.1)}
    factors = {}
    for name, (base, spread) in spreads.items():
        noise = np.random.default_rng([zlib.crc32(name.encode()), seed]).standard_normal(out[name].shape)
        drawn = base * np.exp(spread * noise) if base else spread * noise
        out[name] = jnp.asarray(drawn.astype(out[name].dtype))
    for name, factor in factors.items():
        out[name] = (out[name] * factor).astype(out[name].dtype)
    return out
```

```python
from contextlib import ExitStack

import concourse.bass as bass
from concourse import mybir
from concourse.alu_op_type import AluOpType as ALU

F32 = mybir.dt.float32
BF16 = mybir.dt.bfloat16
I32 = mybir.dt.int32
ACT = mybir.ActivationFunctionType
AX_X = mybir.AxisListType.X

P = 128
B, N, F = 16, 256, 256
T = N // P
C2 = F // P
H, HD = 16, 16
HT = P // HD
M, L = 20, 11
G4 = 4 * M
DFF = 1024
NEG = -9000000000000000.0
LN_EPS = 1e-06
NORM_EPS2 = 1e-24
MAX_SCALE_MUL = 4.605170185988092
SEED = 1597463007.0
SLOT = 16
NSLOT = 6
KROWS = NSLOT * SLOT
Q_PARTS = (0, 0, 0, 1, 1, 2)
K_PARTS = (0, 1, 2, 0, 1, 0)


def ge(eng, sem, value):
    if not isinstance(value, int) or value > 0:
        eng.wait_ge(sem, value)


def steps(turn, eng):
    turn(0, None, 0)
    turn(1, 0, 1)
    turn(2, 1, 0)
    with eng.Fori(0, (B - 4) // 2) as i:
        turn(i * 2 + 3, i * 2 + 2, 1)
        turn(i * 2 + 4, i * 2 + 3, 0)
    turn(B - 1, B - 2, 1)
    turn(None, B - 1, 0)


def loads(b, par):
    return (b - par) * 8 + 16


def following(f):
    return None if f is None or (isinstance(f, int) and f == B - 1) else f + 1


def build(nc, t):
    with ExitStack() as top:
        def alloc(scope, name, shape, dt=F32):
            return scope.enter_context(nc.sbuf_tensor(name, shape, dt))

        def sems(scope, *names):
            return [scope.enter_context(nc.semaphore(n)) for n in names]

        ps = top.enter_context(nc.psum_tensor("ps", [P, 8, 512], F32))

        x_res = alloc(top, "x_res", [P, B * T, F])
        ident = alloc(top, "ident", [P, P])
        ident_b = alloc(top, "ident_b", [P, P], BF16)
        ones = alloc(top, "ones", [P, P])
        neg_half = alloc(top, "neg_half", [P, T])
        ln_eps = alloc(top, "ln_eps", [P, T])
        zero = alloc(top, "zero", [P, 1])
        head_of_row = alloc(top, "head_of_row", [P, HT])
        w_qkv = alloc(top, "w_qkv", [P, C2, 3 * F])
        w_proj = alloc(top, "w_proj", [P, C2, F])
        w_fc1 = alloc(top, "w_fc1", [P, C2, DFF])
        w_fc2 = alloc(top, "w_fc2", [P, DFF // P, F])
        ada = alloc(top, "ada", [P, 6 * C2, B])
        bias_qk = alloc(top, "bias_qk", [P, 2 * F])
        b_v = alloc(top, "b_v", [P, C2])
        b_proj = alloc(top, "b_proj", [P, C2])
        b_fc1 = alloc(top, "b_fc1", [P, DFF // P])
        b_fc2 = alloc(top, "b_fc2", [P, C2])
        head_scale = alloc(top, "head_scale", [P, H])
        late_weights, = sems(top, "late_weights")
        LATE = 9 * 16

        with ExitStack() as graph:
            w_x = alloc(graph, "w_x", [P, C2, F])
            w_q = alloc(graph, "w_q", [P, 2, C2, F])
            b_self = alloc(graph, "b_self", [P, C2])
            b_q = alloc(graph, "b_q", [P, 2, C2])
            b_out = alloc(graph, "b_out", [P, 2, C2])
            b_out_sum = alloc(graph, "b_out_sum", [P, C2])
            w_label = alloc(graph, "w_label", [P, L])
            b_label = alloc(graph, "b_label", [P, 1])
            q_cond = alloc(graph, "q_cond", [P, C2, B])
            k_all = alloc(graph, "k_all", [P, 2 * C2, B * M])
            v_all = alloc(graph, "v_all", [P, 2 * C2, B * M])

            with ExitStack() as setup:
                w_c = alloc(setup, "w_c", [P, C2, F])
                w_k = alloc(setup, "w_k", [P, 2, C2, F])
                w_o = alloc(setup, "w_o", [P, 2, C2, F])
                b_k = alloc(setup, "b_k", [P, 2, C2])
                w_ada = alloc(setup, "w_ada", [P, C2, 6 * F])
                b_ada = alloc(setup, "b_ada", [P, 6 * C2])
                condT = alloc(setup, "condT", [P, C2, B])
                silu = alloc(setup, "silu", [P, C2, B])
                exp_neg = alloc(setup, "exp_neg", [P, C2, B])
                sig = alloc(setup, "sig", [P, C2, B])
                x20 = alloc(setup, "x20", [P, C2, B * M])
                nz20 = alloc(setup, "nz20", [P, B * M])
                cond20 = alloc(setup, "cond20", [P, C2, B * M])
                feat20 = alloc(setup, "feat20", [P, C2, B * M])
                scale_in = alloc(setup, "scale_in", [P, H])
                (consts_set, first_in, ada_in, kv_in, small_in, exp_made, sig_made, silu_made, cond_mm,
                 cond_out, sum20_mm, nz_made, cond20_made, feat20_mm, feat20_made, kv_mm, kv_out,
                 ada_mm, ada_out, chain) = sems(
                    setup, "consts_set", "first_in", "ada_in", "kv_in", "small_in", "exp_made", "sig_made",
                    "silu_made", "cond_mm", "cond_out", "sum20_mm", "nz_made", "cond20_made",
                    "feat20_mm", "feat20_made", "kv_mm", "kv_out", "ada_mm", "ada_out", "setup_chain")
                block = setup.enter_context(nc.Block())

                @block.sync
                def _(sp):
                    sp.dma_start(condT[:], t["condT"].rearrange("(k p) b -> p k b", p=P)).then_inc(first_in, 16)
                    sp.dma_start(w_c[:], t["w_selfT"][F:2 * F, :].rearrange("(k p) n -> p k n", p=P)).then_inc(first_in, 16)
                    sp.dma_start(w_x[:], t["w_selfT"][0:F, :].rearrange("(k p) n -> p k n", p=P)).then_inc(first_in, 16)
                    for k in range(C2):
                        sp.dma_start(x20[:, k, :].rearrange("p (b m) -> p b m", m=M),
                                     t["xT"][k * P:(k + 1) * P, :].rearrange("p (b n) -> p b n", b=B)[:, :, 0:M]
                                     ).then_inc(first_in, 16)
                    sp.dma_start(w_k[:], t["w_kT"].rearrange("d (k p) n -> p d k n", p=P)).then_inc(kv_in, 16)
                    sp.dma_start(w_o[:], t["w_oT"].rearrange("d (k p) n -> p d k n", p=P)).then_inc(kv_in, 16)
                    sp.dma_start(w_ada[:], t["w_adaT"].rearrange("(k p) n -> p k n", p=P)).then_inc(ada_in, 16)
                    sp.dma_start(w_q[:], t["w_qT"].rearrange("d (k p) n -> p d k n", p=P)).then_inc(kv_in, 16)
                    sp.wait_ge(kv_in, 48)
                    sp.wait_ge(small_in, 9 * 16)

                @block.gpsimd
                def _(pool):
                    nc.gpsimd.memset(ident[:], 0.0).then_inc(chain, 1)
                    nc.gpsimd.memset(head_of_row[:], 1.0).then_inc(chain, 1)
                    nc.gpsimd.memset(ones[:], 1.0).then_inc(consts_set, 1)
                    nc.gpsimd.memset(neg_half[:], -0.5).then_inc(consts_set, 1)
                    nc.gpsimd.memset(ln_eps[:], LN_EPS).then_inc(consts_set, 1)
                    nc.gpsimd.memset(zero[:], 0.0).then_inc(consts_set, 1)
                    pool.wait_ge(chain, 2)
                    nc.gpsimd.affine_select(out=ident[:], in_=ident[:], compare_op=ALU.not_equal, fill=1.0, base=0,
                                            pattern=[[-1, P]], channel_multiplier=1).then_inc(consts_set, 1)
                    nc.gpsimd.affine_select(out=head_of_row[:], in_=head_of_row[:], compare_op=ALU.is_ge, fill=0.0,
                                            base=0, pattern=[[-HD, HT]], channel_multiplier=1).then_inc(chain, 1)
                    pool.wait_ge(chain, 3)
                    nc.gpsimd.affine_select(out=head_of_row[:], in_=head_of_row[:], compare_op=ALU.is_ge, fill=0.0,
                                            base=HD - 1, pattern=[[HD, HT]], channel_multiplier=-1).then_inc(consts_set, 1)
                    pool.wait_ge(consts_set, 5)
                    nc.gpsimd.tensor_copy(ident_b[:], ident[:]).then_inc(consts_set, 1)

                @block.scalar
                def _(act):
                    for dst, src in ((b_self, t["b_self"]), (b_ada, t["b_ada"])):
                        act.dma_start(dst[:], src).then_inc(small_in, 16)
                    for dst, src in ((b_k, t["b_k"]), (b_q, t["b_q"]), (b_out, t["b_out"])):
                        act.dma_start(dst[:], src).then_inc(small_in, 16)
                    act.dma_start(w_label[:], t["w_label"].partition_broadcast(P)).then_inc(small_in, 16)
                    act.dma_start(b_label[:], t["b_label"].partition_broadcast(P)).then_inc(small_in, 16)
                    act.dma_start(scale_in[:], t["scale_mul"].partition_broadcast(P)).then_inc(small_in, 16)
                    act.dma_start(bias_qk[:, 0:F], t["b_qkv_q"].partition_broadcast(P)).then_inc(small_in, 16)
                    act.wait_ge(first_in, 80)
                    nc.scalar.activation(exp_neg[:], condT[:], ACT.Exp, scale=-1.0).then_inc(exp_made, 1)
                    for dst, src in ((w_qkv, t["w_qkvT"]), (w_proj, t["w_projT"]), (w_fc1, t["w_fc1T"]),
                                     (w_fc2, t["w_fc2T"])):
                        act.dma_start(dst[:], src.rearrange("(k p) n -> p k n", p=P)).then_inc(late_weights, 16)
                    for dst, src in ((b_v, t["b_v"]), (b_proj, t["b_proj"]), (b_fc1, t["b_fc1"]), (b_fc2, t["b_fc2"])):
                        act.dma_start(dst[:], src).then_inc(late_weights, 16)
                    act.wait_ge(small_in, 9 * 16)
                    act.wait_ge(chain, 4)
                    nc.scalar.activation(head_scale[:], scale_in[:], ACT.Exp).then_inc(exp_made, 1)
                    for c in range(2 * C2):
                        act.wait_ge(kv_mm, 2 * c + 1)
                        nc.scalar.activation(k_all[:, c, :], ps[:, 4, 0:B * M], ACT.Identity,
                                             bias=b_k[:, c // C2, c % C2:c % C2 + 1]).then_inc(kv_out, 1)
                        act.wait_ge(kv_mm, 2 * c + 2)
                        nc.scalar.activation(v_all[:, c, :], ps[:, 5, 0:B * M], ACT.Copy).then_inc(kv_out, 1)

                @block.vector
                def _(dve):
                    nc.vector.memset(bias_qk[:, F:2 * F], 0.0).then_inc(late_weights, 16)
                    dve.wait_ge(small_in, 9 * 16)
                    dve.wait_ge(chain, 3)
                    nc.vector.tensor_scalar(scale_in[:], scale_in[:], MAX_SCALE_MUL, None, ALU.min).then_inc(chain, 1)
                    nc.vector.tensor_scalar(b_q[:], b_q[:], float(HD) ** -0.5, None, ALU.mult).then_inc(chain, 1)
                    nc.vector.tensor_tensor(b_out_sum[:], b_out[:, 0, :], b_out[:, 1, :], ALU.add).then_inc(chain, 1)
                    dve.wait_ge(exp_made, 1)
                    nc.vector.tensor_scalar(sig[:], exp_neg[:], 1.0, None, ALU.add).then_inc(sig_made, 1)
                    dve.wait_ge(sig_made, 1)
                    nc.vector.reciprocal(sig[:], sig[:]).then_inc(sig_made, 1)
                    dve.wait_ge(sig_made, 2)
                    nc.vector.tensor_tensor(silu[:], condT[:], sig[:], ALU.mult).then_inc(silu_made, 1)
                    dve.wait_ge(cond_mm, 1)
                    nc.vector.tensor_copy(q_cond[:], ps[:, 0, 0:C2 * B].rearrange("p (k b) -> p k b", b=B)).then_inc(cond_out, 1)
                    dve.wait_ge(sum20_mm, 1)
                    nc.vector.tensor_scalar(nz20[:], ps[:, 1, 0:B * M], 0.0, None, ALU.not_equal).then_inc(nz_made, 1)
                    dve.wait_ge(nz_made, 1)
                    dve.wait_ge(cond_out, 1)
                    for k in range(C2):
                        nc.vector.tensor_tensor(cond20[:, k, :].rearrange("p (b m) -> p b m", m=M),
                                                nz20[:].rearrange("p (b m) -> p b m", m=M),
                                                q_cond[:, k, :].unsqueeze(2).broadcast_to([P, B, M]), ALU.mult).then_inc(cond20_made, 1)
                    dve.wait_ge(cond20_made, C2)
                    dve.wait_ge(feat20_mm, 1)
                    for k in range(C2):
                        nc.vector.scalar_tensor_tensor(out=feat20[:, k, :], in0=ps[:, 2 + k, 0:B * M], scalar=b_self[:, k:k + 1],
                                                       in1=cond20[:, k, :], op0=ALU.add, op1=ALU.add).then_inc(feat20_made, 1)
                    dve.wait_ge(ada_mm, 1)
                    for j in range(6 * C2):
                        scaled = 2 * C2 <= j < 4 * C2
                        nc.vector.tensor_scalar(ada[:, j, :], ps[:, 6, j * B:(j + 1) * B], b_ada[:, j:j + 1],
                                                1.0 if scaled else 0.0, ALU.add, ALU.add).then_inc(ada_out, 1)

                @block.tensor
                def _(pe):
                    pe.wait_ge(first_in, 80)
                    for f in range(C2):
                        for k in range(C2):
                            mm = nc.tensor.matmul(ps[:, 0, f * B:(f + 1) * B], w_c[:, k, f * P:(f + 1) * P], condT[:, k, :],
                                                  start=(k == 0), stop=(k == C2 - 1))
                    mm.then_inc(cond_mm, 1)
                    pe.wait_ge(consts_set, 7)
                    for k in range(C2):
                        mm = nc.tensor.matmul(ps[:, 1, 0:B * M], ones[:], x20[:, k, :], start=(k == 0), stop=(k == C2 - 1))
                    mm.then_inc(sum20_mm, 1)
                    for f in range(C2):
                        for k in range(C2):
                            mm = nc.tensor.matmul(ps[:, 2 + f, 0:B * M], w_x[:, k, f * P:(f + 1) * P], x20[:, k, :],
                                                  start=(k == 0), stop=(k == C2 - 1))
                    mm.then_inc(feat20_mm, 1)
                    pe.wait_ge(ada_in, 16)
                    pe.wait_ge(silu_made, 1)
                    for j in range(6 * C2):
                        for k in range(C2):
                            mm = nc.tensor.matmul(ps[:, 6, j * B:(j + 1) * B], w_ada[:, k, j * P:(j + 1) * P], silu[:, k, :],
                                                  start=(k == 0), stop=(k == C2 - 1))
                    mm.then_inc(ada_mm, 1)
                    pe.wait_ge(kv_in, 48)
                    pe.wait_ge(feat20_made, C2)
                    for c in range(2 * C2):
                        d, f = c // C2, c % C2
                        for bank, w in ((4, w_k), (5, w_o)):
                            ge(pe, kv_out, 2 * c + bank - 5)
                            for k in range(C2):
                                mm = nc.tensor.matmul(ps[:, bank, 0:B * M], w[:, d, k, f * P:(f + 1) * P], feat20[:, k, :],
                                                      start=(k == 0), stop=(k == C2 - 1))
                            mm.then_inc(kv_mm, 1)

            graph_block(nc, graph, t, alloc, sems, ps, dict(
                x_res=x_res, ident=ident, ones=ones, head_of_row=head_of_row, w_x=w_x, w_q=w_q, b_self=b_self, b_q=b_q,
                b_out_sum=b_out_sum, w_label=w_label, b_label=b_label, q_cond=q_cond, k_all=k_all, v_all=v_all))

        with ExitStack() as attention:
            attention_block(nc, attention, t, alloc, sems, ps, dict(
                x_res=x_res, ident=ident, ident_b=ident_b, neg_half=neg_half, ln_eps=ln_eps, zero=zero, w_qkv=w_qkv, w_proj=w_proj, ada=ada,
                bias_qk=bias_qk, b_v=b_v, b_proj=b_proj, head_scale=head_scale, late_weights=late_weights, LATE=LATE))

        with ExitStack() as ffn:
            ffn_block(nc, ffn, t, alloc, sems, ps, dict(
                x_res=x_res, ident=ident, neg_half=neg_half, ln_eps=ln_eps, zero=zero, w_fc1=w_fc1, w_fc2=w_fc2, ada=ada, b_fc1=b_fc1, b_fc2=b_fc2))


def halves(ps, bank):
    return ps[:, bank, :].rearrange("p (a n) -> p a n", a=2)


def graph_block(nc, scope, t, alloc, sems, ps, g):
    x_res, ident, ones, head_of_row = g["x_res"], g["ident"], g["ones"], g["head_of_row"]
    w_x, w_q, b_self, b_q, b_out_sum = g["w_x"], g["w_q"], g["b_self"], g["b_q"], g["b_out_sum"]
    w_label, b_label, q_cond, k_all, v_all = g["w_label"], g["b_label"], g["q_cond"], g["k_all"], g["v_all"]
    E2 = T * 2 * M
    xT = alloc(scope, "xT", [P, 2, C2, N])
    x_in = alloc(scope, "x_in", [P, 2, T, F])
    adj = alloc(scope, "adj", [P, 2, E2 * L], I32)
    weighted = alloc(scope, "weighted", [P, E2 * L])
    count = alloc(scope, "count", [P, E2])
    no_edge = alloc(scope, "no_edge", [P, E2])
    label_bias = alloc(scope, "label_bias", [P, E2])
    edge_bias = alloc(scope, "edge_bias", [P, 2, T, 2, M])
    nz = alloc(scope, "nz", [P, N])
    cond = alloc(scope, "cond", [P, C2, N])
    featT = alloc(scope, "featT", [P, 2, C2, N])
    qT = alloc(scope, "qT", [P, 2, 2, C2, N])
    k_blocks = alloc(scope, "k_blocks", [P, 2, 2 * C2, HT, M])
    v_masked = alloc(scope, "v_masked", [P, 2 * C2, HT, M])
    v_blocks = alloc(scope, "v_blocks", [G4, 2, H // 2, 64])
    scores = alloc(scope, "scores", [P, 2, T, H, M])
    row_max = alloc(scope, "row_max", [P, 2, T, H])
    total = alloc(scope, "row_sum", [P, 2, T, H])
    inverse = alloc(scope, "row_inverse", [P, 2, T, H])
    weightT = alloc(scope, "weightT", [G4, 2, T, 4, P])
    outT = alloc(scope, "outT", [P, C2, N])
    xT_in, x_arrived, adj_in = (sems(scope, f"{n}_even", f"{n}_odd") for n in ("xT_in", "x_in_arrived", "adj_in"))
    (sums_mm, nz_made, cond_made, feat_mm, feat_out, q_mm, q_out, kb_made, vm_made, vt_mm,
     vb_made, cnt_made, lab_w, lab_made, neg_made, edge_made, aff_mm, aff_out, max_made, shifted, exp_made,
     sum_made, rec_made, norm_made, wT_mm, wT_out, pv_mm, outT_made, out_mm, x_made) = sems(
        scope, "sums_mm", "nz_made_g", "cond_made", "feat_mm", "feat_out", "q_mm", "q_out",
        "kb_made", "vm_made", "vt_mm", "vb_made", "cnt_made", "lab_w", "lab_made", "neg_made", "edge_made",
        "aff_mm", "aff_out", "max_made", "shifted", "exp_made_g", "sum_made", "rec_made", "norm_made", "wT_mm", "wT_out",
        "pv_mm", "outT_made", "out_mm", "x_made")
    block = scope.enter_context(nc.Block())

    @block.sync
    def _(sp):
        def turn(f, b, par):
            if f is None:
                return
            ge(sp, feat_mm, f - 1)
            sp.dma_start(xT[:, par], t["xT"][:, bass.ds(f * N, N)].rearrange("(k p) n -> p k n", p=P)).then_inc(xT_in[par], 16)
            ge(sp, lab_w, f - 1)
            ge(sp, cnt_made, f - 1)
            sp.dma_start(adj[:, par].rearrange("p (t e) -> p t e", t=T),
                         t["adj"][bass.ds(f * N, N), :].rearrange("(t p) e -> p t e", p=P)).then_inc(adj_in[par], 16)
            ge(sp, x_made, f - 1)
            sp.dma_start(x_in[:, par], t["x"][bass.ds(f * N, N), :].rearrange("(t p) f -> p t f", p=P)).then_inc(x_arrived[par], 16)

        steps(turn, sp)

    @block.gpsimd
    def _(pool):
        own = head_of_row[:].unsqueeze(2).broadcast_to([P, HT, M])

        def turn(f, b, par):
            if b is not None:
                for d in range(2):
                    pool.wait_ge(max_made, 2 * b + d + 1)
                    nc.gpsimd.tensor_tensor(scores[:, d], scores[:, d], row_max[:, d].unsqueeze(3).broadcast_to([P, T, H, M]),
                                            ALU.subtract).then_inc(shifted, 1)
            if f is not None:
                ge(pool, aff_mm, 2 * (f - 1))
                for c in range(2 * C2):
                    nc.gpsimd.tensor_tensor(k_blocks[:, par, c], k_all[:, c, bass.ds(f * M, M)].unsqueeze(1).broadcast_to([P, HT, M]),
                                            own, ALU.mult).then_inc(kb_made, 1)
                ge(pool, vt_mm, 2 * f)
                for c in range(2 * C2):
                    nc.gpsimd.tensor_tensor(v_masked[:, c], v_all[:, c, bass.ds(f * M, M)].unsqueeze(1).broadcast_to([P, HT, M]),
                                            own, ALU.mult).then_inc(vm_made, 1)
            if b is not None:
                for d in range(2):
                    pool.wait_ge(rec_made, 2 * b + d + 1)
                    nc.gpsimd.tensor_tensor(scores[:, d], scores[:, d], inverse[:, d].unsqueeze(3).broadcast_to([P, T, H, M]),
                                            ALU.mult).then_inc(norm_made, 1)

        steps(turn, pool)

    @block.scalar
    def _(act):
        def turn(f, b, par):
            if b is not None:
                for d in range(2):
                    act.wait_ge(shifted, 2 * b + d + 1)
                    nc.scalar.activation(scores[:, d], scores[:, d], ACT.Exp).then_inc(exp_made, 1)
            if f is not None:
                ge(act, aff_mm, 2 * (f - 1))
                for d in range(2):
                    act.wait_ge(q_mm, 2 * f + d + 1)
                    for c in range(C2):
                        nc.scalar.activation(qT[:, par, d, c, :], halves(ps, 2 + d)[:, c, :], ACT.Identity,
                                             bias=b_q[:, d, c:c + 1], scale=float(HD) ** -0.5).then_inc(q_out, 1)
                act.wait_ge(vt_mm, 2 * f + 2)
                ge(act, pv_mm, f - 1)
                nc.scalar.activation(v_blocks[:, par], ps[0:G4, 0, :].rearrange("p (c v) -> p c v", v=64),
                                     ACT.Copy).then_inc(vb_made, 1)
            if b is not None:
                for d in range(2):
                    act.wait_ge(wT_mm, 2 * b + d + 1)
                    ge(act, pv_mm, b)
                    nc.scalar.activation(weightT[:, d], ps[0:G4, 6:8, :].rearrange("p t (c n) -> p t c n", c=4),
                                         ACT.Copy).then_inc(wT_out, 1)

        steps(turn, act)

    @block.vector
    def _(dve):
        def raw_scores(b, par):
            dve.wait_ge(edge_made, b + 1)
            for d in range(2):
                dve.wait_ge(aff_mm, 2 * b + d + 1)
                ge(dve, wT_mm, 2 * (b - 1) + d + 1)
                for tt in range(T):
                    nc.vector.tensor_tensor(
                        scores[:, d, tt], ps[:, 4 + tt, 0:H * M].rearrange("p (h m) -> p h m", m=M),
                        edge_bias[:, par, tt, d, :].unsqueeze(1).broadcast_to([P, H, M]), ALU.add).then_inc(aff_out, 1)
                dve.wait_ge(aff_out, T * (2 * b + d + 1))
                nc.vector.tensor_reduce(row_max[:, d], scores[:, d], AX_X, ALU.max).then_inc(max_made, 1)

        def features(f, par):
            dve.wait_ge(sums_mm, f + 1)
            nc.vector.tensor_scalar(nz[:], halves(ps, 0)[:, 0, :], 0.0, None, ALU.not_equal).then_inc(nz_made, 1)
            dve.wait_ge(nz_made, f + 1)
            for c in range(C2):
                nc.vector.tensor_scalar(cond[:, c, :], nz[:], q_cond[:, c, bass.ds(f, 1)], b_self[:, c:c + 1],
                                        ALU.mult, ALU.add).then_inc(cond_made, 1)
            dve.wait_ge(cond_made, C2 * (f + 1))
            dve.wait_ge(feat_mm, f + 1)
            ge(dve, q_mm, 2 * (f - 1))
            nc.vector.tensor_tensor(featT[:, par], halves(ps, 1), cond[:], ALU.add).then_inc(feat_out, 1)

        def edges_of(f, par):
            dve.wait_ge(adj_in[par], loads(f, par))
            edges = adj[:, par].rearrange("p (e l) -> p e l", l=L)
            nc.vector.tensor_reduce(count[:], edges, AX_X, ALU.add).then_inc(cnt_made, 1)
            nc.vector.tensor_tensor(weighted[:].rearrange("p (e l) -> p e l", l=L), edges,
                                    w_label[:].unsqueeze(1).broadcast_to([P, E2, L]), ALU.mult).then_inc(lab_w, 1)
            dve.wait_ge(cnt_made, f + 1)
            nc.vector.tensor_scalar(no_edge[:], count[:], 0.0, NEG, ALU.is_le, ALU.mult).then_inc(neg_made, 1)
            dve.wait_ge(lab_w, f + 1)
            nc.vector.tensor_reduce(label_bias[:], weighted[:].rearrange("p (e l) -> p e l", l=L), AX_X,
                                    ALU.add).then_inc(lab_made, 1)
            dve.wait_ge(neg_made, f + 1)
            dve.wait_ge(lab_made, f + 1)
            nc.vector.scalar_tensor_tensor(out=edge_bias[:, par].rearrange("p t d m -> p (t d m)"), in0=label_bias[:],
                                           scalar=b_label[:, 0:1], in1=no_edge[:], op0=ALU.add, op1=ALU.add).then_inc(edge_made, 1)

        def sums(b):
            for d in range(2):
                dve.wait_ge(exp_made, 2 * b + d + 1)
                nc.vector.tensor_reduce(total[:, d], scores[:, d], AX_X, ALU.add).then_inc(sum_made, 1)
                dve.wait_ge(sum_made, 2 * b + d + 1)
                nc.vector.reciprocal(inverse[:, d], total[:, d]).then_inc(rec_made, 1)

        def output(b, par):
            dve.wait_ge(pv_mm, b + 1)
            ge(dve, out_mm, b)
            for c in range(C2):
                nc.vector.scalar_tensor_tensor(out=outT[:, c, :], in0=halves(ps, 1)[:, c, :], scalar=b_out_sum[:, c:c + 1],
                                               in1=featT[:, par, c, :], op0=ALU.add, op1=ALU.add).then_inc(outT_made, 1)
            dve.wait_ge(out_mm, b + 1)
            dve.wait_ge(x_arrived[par], loads(b, par))
            nc.vector.scalar_tensor_tensor(
                out=x_res[:, bass.ds(b * T, T), :].rearrange("p t f -> p (t f)"), in0=ps[:, 0, :], scalar=0.0,
                in1=x_in[:, par].rearrange("p t f -> p (t f)"), op0=ALU.max, op1=ALU.add).then_inc(x_made, 1)

        def turn(f, b, par):
            if b is not None:
                raw_scores(b, 1 - par)
            if f is not None:
                features(f, par)
                edges_of(f, par)
            if b is not None:
                sums(b)
                output(b, 1 - par)

        steps(turn, dve)

    @block.tensor
    def _(pe):
        def raw_scores(b, par, d):
            pe.wait_ge(q_out, 4 * b + 2 * d + 2)
            pe.wait_ge(kb_made, 2 * C2 * (b + 1))
            ge(pe, aff_out, T * (2 * b + d))
            for tt in range(T):
                for c in range(C2):
                    mm = nc.tensor.matmul(ps[:, 4 + tt, c * HT * M:(c + 1) * HT * M], qT[:, par, d, c, tt * P:(tt + 1) * P],
                                          k_blocks[:, par, C2 * d + c].rearrange("p h m -> p (h m)"), start=True, stop=True)
            mm.then_inc(aff_mm, 1)

        def features(f, par):
            pe.wait_ge(xT_in[par], loads(f, par))
            ge(pe, x_made, f - 1)
            ge(pe, vb_made, f)
            for k in range(C2):
                mm = nc.tensor.matmul(halves(ps, 0)[:, 0, :], ones[:], xT[:, par, k, :], start=(k == 0), stop=(k == C2 - 1))
            mm.then_inc(sums_mm, 1)
            ge(pe, outT_made, C2 * (f - 1))
            for c in range(C2):
                for k in range(C2):
                    mm = nc.tensor.matmul(halves(ps, 1)[:, c, :], w_x[:, k, c * P:(c + 1) * P], xT[:, par, k, :],
                                          start=(k == 0), stop=(k == C2 - 1))
            mm.then_inc(feat_mm, 1)

        def queries(f, par):
            pe.wait_ge(feat_out, f + 1)
            ge(pe, q_out, 2 * C2 * f)
            pe.wait_ge(vm_made, 2 * C2 * (f + 1))
            pe.wait_ge(nz_made, f + 1)
            for d in range(2):
                for c in range(C2):
                    for k in range(C2):
                        mm = nc.tensor.matmul(halves(ps, 2 + d)[:, c, :], w_q[:, d, k, c * P:(c + 1) * P], featT[:, par, k, :],
                                              start=(k == 0), stop=(k == C2 - 1))
                mm.then_inc(q_mm, 1)
                j = d
                for c in range(2 * C2):
                    o = (2 * c + j) * 64
                    mm = nc.tensor.transpose(ps[0:G4, 0, o:o + 64],
                                             v_masked[64 * j:64 * j + 64, c, 4 * j:4 * j + 4].rearrange("p h m -> p (h m)"),
                                             ident[64 * j:64 * j + 64, 64 * j:64 * j + 64])
                mm.then_inc(vt_mm, 1)
                if j == 0:
                    pe.wait_ge(vt_mm, 2 * f + 1)

        def weights_of(b, d):
            pe.wait_ge(norm_made, 2 * b + d + 1)
            ge(pe, wT_out, 2 * b + d)
            for tt in range(T):
                for c in range(4):
                    mm = nc.tensor.transpose(ps[0:G4, 6 + tt, c * P:(c + 1) * P],
                                             scores[:, d, tt, 4 * c:4 * c + 4].rearrange("p h m -> p (h m)"), ident[:])
            mm.then_inc(wT_mm, 1)

        def output(b, par, fronts):
            pe.wait_ge(wT_out, 2 * b + 2)
            pe.wait_ge(feat_out, fronts)
            pe.wait_ge(vb_made, fronts)
            for c in range(C2):
                for j in range(2):
                    for d in range(2):
                        mm = nc.tensor.matmul(halves(ps, 1)[64 * j:64 * j + 64, c, :], v_blocks[:, par, 2 * (C2 * d + c) + j, :],
                                              weightT[:, d, :, 2 * c + j, :], start=(d == 0), stop=(d == 1))
            mm.then_inc(pv_mm, 1)
            pe.wait_ge(outT_made, C2 * (b + 1))
            for tt in range(T):
                for c in range(C2):
                    mm = nc.tensor.transpose(ps[:, 0, (C2 * tt + c) * P:(C2 * tt + c + 1) * P], outT[:, c, tt * P:(tt + 1) * P],
                                             ident[:])
            mm.then_inc(out_mm, 1)

        def turn(f, b, par):
            if b is not None:
                raw_scores(b, 1 - par, 0)
            if f is not None:
                features(f, par)
            if b is not None:
                raw_scores(b, 1 - par, 1)
            if f is not None:
                queries(f, par)
            if b is not None:
                weights_of(b, 0)
                weights_of(b, 1)
                output(b, 1 - par, B if f is None else f + 1)

        steps(turn, pe)


def norm_stats(nc, x_res, b, stats, stats_made):
    for tt in range(T):
        nc.vector.bn_stats(stats[:, tt, :], x_res[:, bass.ds(b * T + tt, 1), :].rearrange("p a f -> p (a f)")).then_inc(stats_made, 1)


def norm_moments(nc, stats, mean_var, mv_made):
    for tt in range(T):
        nc.vector.bn_aggr(mean_var[:, tt, :], stats[:, tt, :]).then_inc(mv_made, 1)


def norm_root(pool, nc, b, mean_var, g, var_eps, rstd, mv_made, eps_made, rstd_made):
    pool.wait_ge(mv_made, T * (b + 1))
    nc.gpsimd.tensor_tensor(var_eps[:], mean_var[:, :, 1], g["ln_eps"][:], ALU.add).then_inc(eps_made, 1)
    pool.wait_ge(eps_made, b + 1)
    nc.gpsimd.tensor_tensor(rstd[:], var_eps[:], g["neg_half"][:], ALU.pow).then_inc(rstd_made, 1)


def attention_block(nc, scope, t, alloc, sems, ps, g):
    x_res, ident, ident_b = g["x_res"], g["ident"], g["ident_b"]
    w_qkv, w_proj, ada, bias_qk = g["w_qkv"], g["w_proj"], g["ada"], g["bias_qk"]
    b_v, b_proj, head_scale = g["b_v"], g["b_proj"], g["head_scale"]
    HH = T * 2 * H
    parts_dram = nc.dram_tensor("parts_dram", (2, 3, HD, C2, HT, N), BF16, kind="Internal").ap()
    stats = alloc(scope, "stats", [P, T, 6])
    mean_var = alloc(scope, "mean_var", [P, T, 2])
    var_eps = alloc(scope, "var_eps", [P, T])
    rstd = alloc(scope, "rstd", [P, T])
    x_hat = alloc(scope, "x_hat", [P, T, F])
    x1T = alloc(scope, "x1T", [P, C2, N])
    qk = alloc(scope, "qk", [P, T, 2 * F])
    squares = alloc(scope, "squares", [P, T, 2 * F])
    sum_sq = alloc(scope, "sum_sq", [P, HH])
    minus_half = alloc(scope, "minus_half", [P, HH])
    root = [alloc(scope, f"root{i}", [P, HH]) for i in range(2)]
    root_sq = alloc(scope, "root_sq", [P, HH])
    root_err = alloc(scope, "root_err", [P, HH])
    qkn = alloc(scope, "qkn", [P, T, 2 * F])
    parts = alloc(scope, "parts", [P, 2, 3, C2 * N], BF16)
    rest = alloc(scope, "rest", [P, 2, C2 * N])
    q_stack = alloc(scope, "q_stack", [KROWS + 1, 2, H, N], BF16)
    k_stack = alloc(scope, "k_stack", [KROWS + 1, 2, H, N], BF16)
    v_ones = alloc(scope, "v_ones", [P, 2, T, H, 2 * HD])
    neg_max = alloc(scope, "neg_max", [P, T, H], BF16)
    neg_maxT = alloc(scope, "neg_maxT", [H, N], BF16)
    probsT = alloc(scope, "probsT", [P, 4, 1024])
    o_sumsT = alloc(scope, "o_sumsT", [P, 2, 2 * N])
    denom = alloc(scope, "denom", [P, T, H])
    o_tok = alloc(scope, "o_tok", [P, T, F])
    oT = alloc(scope, "oT", [P, C2, N])
    projT = alloc(scope, "projT", [P, C2, N])
    (stats_made, mv_made, eps_made, rstd_made, xhat_made, xt_mm, x1_out, qk_mm, qk_out, v_mm, v_out, sq_made, ss_made,
     root_step, qkn_made, qkt_mm, high_made, rest_made, mid_made, low_made, parts_out, stack_in, s_mm, max_made, m_mm, m_out,
     m_row_in, st_mm, exp_made, pv_mm, os_out, otok_mm, den_made, otok_made, ot_mm, ot_out, proj_mm, proj_out, res_mm,
     res_made, consts) = sems(
        scope, "stats_made", "mv_made", "eps_made", "rstd_made", "xhat_made", "xt_mm", "x1_out", "qk_mm", "qk_out", "v_mm",
        "v_out", "sq_made", "ss_made", "root_step", "qkn_made", "qkt_mm", "high_made", "rest_made", "mid_made", "low_made",
        "parts_out", "stack_in", "s_mm", "max_made_a", "m_mm", "m_out", "m_row_in", "st_mm", "exp_made_a", "pv_mm_a", "os_out",
        "otok_mm", "den_made", "otok_made", "ot_mm", "ot_out", "proj_mm", "proj_out", "res_mm", "res_made", "consts")
    block = scope.enter_context(nc.Block())

    def region(r):
        return ps[:, 4 + 2 * r:6 + 2 * r, :]

    @block.sync
    def _(sp):
        def turn(f, b, par):
            if f is None:
                return
            ge(sp, stack_in, f * (9 * 16))
            ge(sp, st_mm, f * 8 - 8)
            sp.wait_ge(low_made, 2 * (f + 1))
            for w in range(2):
                for part in range(3):
                    for c in range(C2):
                        sp.dma_start(parts_dram[w, part, :, c].rearrange("d h n -> h d n"),
                                     parts[:, w, part, c * N:(c + 1) * N]).then_inc(parts_out, 16)
            sp.wait_ge(parts_out, 12 * 16 * (f + 1))
            whole = parts_dram.rearrange("w p d c h n -> w (p d) (c h n)")

            def rows(stack, at, n):
                return stack[at * SLOT:(at + n) * SLOT, par].rearrange("p h n -> p (h n)")

            for slot, part in enumerate(Q_PARTS):
                sp.dma_start(rows(q_stack, slot, 1), whole[0, part * HD:(part + 1) * HD, :]).then_inc(stack_in, 16)
            for slot, n in ((0, 3), (3, 2), (5, 1)):
                sp.dma_start(rows(k_stack, slot, n), whole[1, 0:n * HD, :]).then_inc(stack_in, 16)

        steps(turn, sp)

    @block.gpsimd
    def _(pool):
        nc.gpsimd.memset(v_ones[:], 1.0).then_inc(consts, 1)
        pool.wait_ge(consts, 1)
        nc.gpsimd.memset(k_stack[KROWS:KROWS + 1], 1.0).then_inc(consts, 1)
        pool.wait_ge(consts, 2)
        norm_root(pool, nc, 0, mean_var, g, var_eps, rstd, mv_made, eps_made, rstd_made)

        def turn(f, b, par):
            ahead = following(f)
            if ahead is not None:
                norm_root(pool, nc, ahead, mean_var, g, var_eps, rstd, mv_made, eps_made, rstd_made)
            if f is not None:
                for w in range(2):
                    pool.wait_ge(rest_made, 2 * f + w + 1)
                    nc.gpsimd.tensor_tensor(parts[:, w, 1, :], rest[:, w, :], g["zero"][:].broadcast_to([P, C2 * N]), ALU.add).then_inc(mid_made, 1)
                    pool.wait_ge(mid_made, 2 * f + w + 1)
                    nc.gpsimd.tensor_tensor(parts[:, w, 2, :], rest[:, w, :], parts[:, w, 1, :], ALU.subtract).then_inc(low_made, 1)

        steps(turn, pool)

    @block.scalar
    def _(act):
        def turn(f, b, par):
            if f is not None:
                act.wait_ge(xt_mm, f + 1)
                ge(act, v_mm, f)
                for c in range(C2):
                    nc.scalar.activation(x1T[:, c, :], halves(ps, 0)[:, c, :], ACT.Identity,
                                         bias=ada[:, 4 * C2 + c, bass.ds(f, 1)],
                                         scale=ada[:, 2 * C2 + c, bass.ds(f, 1)]).then_inc(x1_out, 1)
                for tt in range(T):
                    act.wait_ge(qk_out, T * f + tt + 1)
                    ge(act, ss_made, f)
                    nc.scalar.activation(squares[:, tt, :], qk[:, tt, :], ACT.Square).then_inc(sq_made, 1)
                act.wait_ge(v_mm, f + 1)
                ge(act, pv_mm, 4 * (f - 1))
                if isinstance(f, int):
                    ge(act, consts, 2)
                nc.scalar.activation(v_ones[:, par, :, :, 0:HD], halves(ps, 1).rearrange("p t (h d) -> p t h d", d=HD),
                                     ACT.Copy).then_inc(v_out, 1)
            if b is not None:
                act.wait_ge(m_mm, b + 1)
                ge(act, m_row_in, 16 * b)
                nc.scalar.activation(neg_maxT[:], ps[0:H, 3, 0:N // 2].bitcast(BF16), ACT.Copy).then_inc(m_out, 1)
                act.wait_ge(m_out, b + 1)
                act.dma_start(q_stack[KROWS:KROWS + 1, 1 - par], neg_maxT[:]).then_inc(m_row_in, 16)
            if f is not None:
                ge(act, parts_out, 12 * 16 * f)
                for w in range(2):
                    act.wait_ge(qkt_mm, 2 * f + w + 1)
                    nc.scalar.activation(parts[:, w, 0, :], ps[:, w, :], ACT.Copy).then_inc(high_made, 1)
            if b is not None:
                for s in range(8):
                    act.wait_ge(st_mm, 8 * b + s + 1)
                    ge(act, pv_mm, 4 * b + s // 2 - 1)
                    nc.scalar.activation(probsT[:, s % 4, :], region(s % 2).rearrange("p a n -> p (a n)"),
                                         ACT.Exp).then_inc(exp_made, 1)
                    if s == 6:
                        take_sums(b, 0)
                take_sums(b, 1)
                act.wait_ge(ot_mm, b + 1)
                ge(act, proj_mm, b)
                for c in range(C2):
                    nc.scalar.activation(oT[:, c, :], halves(ps, 2)[:, c, :], ACT.Identity,
                                         bias=b_v[:, c:c + 1]).then_inc(ot_out, 1)

        def take_sums(b, i):
            act.wait_ge(pv_mm, 4 * b + 2 * i + 2)
            ge(act, otok_mm, b)
            nc.scalar.activation(o_sumsT[:, i, :], ps[:, 2 + i, :], ACT.Copy).then_inc(os_out, 1)

        steps(turn, act)

    @block.vector
    def _(dve):
        def normalise(f):
            dve.wait_ge(rstd_made, f + 1)
            ge(dve, xt_mm, f)
            for tt in range(T):
                nc.vector.tensor_scalar(x_hat[:, tt, :], x_res[:, bass.ds(f * T + tt, 1), :].rearrange("p a f -> p (a f)"),
                                        mean_var[:, tt, 0:1], rstd[:, tt:tt + 1], ALU.subtract, ALU.mult).then_inc(xhat_made, 1)

        def unit_qk(f):
            if following(f) is not None:
                norm_stats(nc, x_res, following(f), stats, stats_made)
                dve.wait_ge(stats_made, T * (f + 2))
            for tt in range(T):
                dve.wait_ge(qk_mm, T * f + tt + 1)
                ge(dve, sq_made, T * f)
                nc.vector.tensor_tensor(qk[:, tt, :], ps[:, 1 - tt, :], bias_qk[:], ALU.add).then_inc(qk_out, 1)
            if following(f) is not None:
                norm_moments(nc, stats, mean_var, mv_made)
            dve.wait_ge(sq_made, T * (f + 1))
            nc.vector.tensor_reduce(sum_sq[:], squares[:].rearrange("p t (h d) -> p (t h) d", d=HD), AX_X,
                                    ALU.add).then_inc(ss_made, 1)
            count = [0]
            STEPS = 14

            def link(ins):
                count[0] += 1
                ins.then_inc(root_step, 1)
                dve.wait_ge(root_step, f * STEPS + count[0])

            dve.wait_ge(ss_made, f + 1)
            link(nc.vector.tensor_scalar(sum_sq[:], sum_sq[:], NORM_EPS2, None, ALU.max))
            nc.vector.tensor_scalar(minus_half[:], sum_sq[:], -0.5, None, ALU.mult).then_inc(root_step, 1)
            count[0] += 1
            link(nc.vector.tensor_scalar(root[0][:].bitcast(I32), sum_sq[:].bitcast(I32), 1, None, ALU.arith_shift_right))
            link(nc.vector.tensor_scalar(root[1][:].bitcast(I32), root[0][:].bitcast(I32), -1.0, SEED, ALU.mult, ALU.add))
            for n in range(3):
                old, new = root[(n + 1) % 2], root[n % 2]
                link(nc.vector.tensor_tensor(root_sq[:], old[:], old[:], ALU.mult))
                link(nc.vector.tensor_tensor(root_err[:], root_sq[:], minus_half[:], ALU.mult))
                link(nc.vector.scalar_tensor_tensor(out=new[:], in0=root_err[:], scalar=1.5, in1=old[:], op0=ALU.add, op1=ALU.mult))
            norm = root[0]
            by = norm[:].rearrange("p (t w h) -> p t w h", t=T, w=2)
            link(nc.vector.tensor_tensor(by[:, :, 0, :], by[:, :, 0, :], head_scale[:].unsqueeze(1).broadcast_to([P, T, H]), ALU.mult))
            assert count[0] == STEPS
            ge(dve, qkt_mm, 2 * f)
            nc.vector.tensor_tensor(qkn[:].rearrange("p t (h d) -> p (t h) d", d=HD), qk[:].rearrange("p t (h d) -> p (t h) d", d=HD),
                                    norm[:].unsqueeze(2).broadcast_to([P, HH, HD]), ALU.mult).then_inc(qkn_made, 1)

        def maxima(b):
            ge(dve, m_mm, b)
            for s in range(8):
                dve.wait_ge(s_mm, 8 * b + s + 1)
                nc.vector.tensor_reduce(neg_max[:, s // 4, 4 * (s % 4):4 * (s % 4) + 4],
                                        region(s % 2).rearrange("p a (h n) -> p (a h) n", h=2), AX_X, ALU.max,
                                        negate=True).then_inc(max_made, 1)

        def rests(f):
            for w in range(2):
                dve.wait_ge(high_made, 2 * f + w + 1)
                ge(dve, low_made, 2 * f)
                nc.vector.tensor_tensor(rest[:, w, :], ps[:, w, :], parts[:, w, 0, :], ALU.subtract).then_inc(rest_made, 1)

        def output(b):
            dve.wait_ge(otok_mm, b + 1)
            heads = ps[:, 2:4, :].rearrange("p t (h d) -> p t h d", d=2 * HD)
            nc.vector.reciprocal(denom[:], heads[:, :, :, HD]).then_inc(den_made, 1)
            dve.wait_ge(den_made, b + 1)
            ge(dve, ot_mm, b)
            for tt in range(T):
                nc.vector.tensor_tensor(o_tok[:, tt, :].rearrange("p (h d) -> p h d", d=HD), heads[:, tt, :, 0:HD],
                                        denom[:, tt, :].unsqueeze(2).broadcast_to([P, H, HD]), ALU.mult).then_inc(otok_made, 1)
            dve.wait_ge(proj_mm, b + 1)
            ge(dve, res_mm, b)
            for c in range(C2):
                nc.vector.tensor_scalar(projT[:, c, :], halves(ps, 3)[:, c, :], b_proj[:, c:c + 1], ada[:, c, bass.ds(b, 1)],
                                        ALU.add, ALU.mult).then_inc(proj_out, 1)
            dve.wait_ge(res_mm, b + 1)
            x = x_res[:, bass.ds(b * T, T), :].rearrange("p t f -> p (t f)")
            nc.vector.tensor_tensor(x, ps[:, 2, :], x, ALU.add).then_inc(res_made, 1)

        norm_stats(nc, x_res, 0, stats, stats_made)
        dve.wait_ge(stats_made, T)
        norm_moments(nc, stats, mean_var, mv_made)

        def turn(f, b, par):
            if f is not None:
                normalise(f)
                unit_qk(f)
            if b is not None:
                maxima(b)
            if f is not None:
                rests(f)
            if b is not None:
                output(b)

        steps(turn, dve)

    @block.tensor
    def _(pe):
        pe.wait_ge(g["late_weights"], g["LATE"])

        def project(f, par):
            pe.wait_ge(xhat_made, T * (f + 1))
            ge(pe, rest_made, 2 * f)
            for tt in range(T):
                for c in range(C2):
                    mm = nc.tensor.transpose(halves(ps, 0)[:, c, tt * P:(tt + 1) * P], x_hat[:, tt, c * P:(c + 1) * P], ident[:])
            mm.then_inc(xt_mm, 1)
            pe.wait_ge(x1_out, C2 * (f + 1))
            for tt in range(T):
                for k in range(C2):
                    mm = nc.tensor.matmul(ps[:, 1 - tt, :], x1T[:, k, tt * P:(tt + 1) * P], w_qkv[:, k, 0:2 * F],
                                          start=(k == 0), stop=(k == C2 - 1))
                mm.then_inc(qk_mm, 1)
            pe.wait_ge(qk_out, T * f + 1)
            for tt in range(T):
                for k in range(C2):
                    mm = nc.tensor.matmul(halves(ps, 1)[:, tt, :], x1T[:, k, tt * P:(tt + 1) * P], w_qkv[:, k, 2 * F:3 * F],
                                          start=(k == 0), stop=(k == C2 - 1))
            mm.then_inc(v_mm, 1)

        def row_scores(b, par):
            pe.wait_ge(stack_in, 9 * 16 * (b + 1))
            for s in range(8):
                tt, h0 = s // 4, 4 * (s % 4)
                if s < 2:
                    ge(pe, exp_made, 8 * b)
                else:
                    pe.wait_ge(max_made, 8 * b + s - 1)
                for j in range(4):
                    mm = nc.tensor.matmul(region(s % 2)[:, j // 2, (j % 2) * N:(j % 2 + 1) * N],
                                          q_stack[0:KROWS, par, h0 + j, tt * P:(tt + 1) * P], k_stack[0:KROWS, par, h0 + j, :],
                                          start=True, stop=True)
                mm.then_inc(s_mm, 1)
            pe.wait_ge(max_made, 8 * (b + 1))
            ge(pe, proj_out, C2 * b)
            for tt in range(T):
                mm = nc.tensor.transpose(ps[0:H, 3, tt * P // 2:(tt + 1) * P // 2].bitcast(BF16), neg_max[:, tt, :], ident_b[:])
            mm.then_inc(m_mm, 1)

        def split_qk(f):
            pe.wait_ge(qkn_made, f + 1)
            pe.wait_ge(v_out, f + 1)
            for w in range(2):
                for tt in range(T):
                    for c in range(C2):
                        mm = nc.tensor.transpose(halves(ps, w)[:, c, tt * P:(tt + 1) * P],
                                                 qkn[:, tt, w * F + c * P:w * F + (c + 1) * P], ident[:])
                mm.then_inc(qkt_mm, 1)

        def col_scores(b, par, s):
            if s == 0:
                pe.wait_ge(m_row_in, 16 * (b + 1))
            if s >= 2:
                pe.wait_ge(exp_made, 8 * b + s - 1)
            for j in range(2):
                h = 2 * s + j
                for kt in range(T):
                    mm = nc.tensor.matmul(region(s % 2)[:, j, kt * N:(kt + 1) * N], k_stack[:, par, h, kt * P:(kt + 1) * P],
                                          q_stack[:, par, h, :], start=True, stop=True)
            mm.then_inc(st_mm, 1)

        def values(b, par, hg):
            if hg == 0:
                ge(pe, res_made, b)
            if hg == 2:
                pe.wait_ge(m_out, b + 1)
            pe.wait_ge(exp_made, 8 * b + 2 * hg + 2)
            for kt in range(T):
                for j in range(4):
                    mm = nc.tensor.matmul(halves(ps, 2 + hg // 2)[32 * j:32 * j + 32, hg % 2, :], v_ones[:, par, kt, 4 * hg + j, :],
                                          probsT[:, (2 * hg + j // 2) % 4, (j % 2) * 2 * N + kt * N:(j % 2) * 2 * N + (kt + 1) * N],
                                          start=(kt == 0), stop=(kt == T - 1))
            mm.then_inc(pv_mm, 1)

        def output(b):
            pe.wait_ge(os_out, 2 * (b + 1))
            for tt in range(T):
                for hg in range(4):
                    o = (hg % 2) * N + tt * P
                    mm = nc.tensor.transpose(ps[:, 2 + tt, hg * P:(hg + 1) * P], o_sumsT[:, hg // 2, o:o + P], ident[:])
            mm.then_inc(otok_mm, 1)
            pe.wait_ge(otok_made, T * (b + 1))
            for tt in range(T):
                for c in range(C2):
                    mm = nc.tensor.transpose(halves(ps, 2)[:, c, tt * P:(tt + 1) * P], o_tok[:, tt, c * P:(c + 1) * P], ident[:])
            mm.then_inc(ot_mm, 1)
            pe.wait_ge(ot_out, C2 * (b + 1))
            for c in range(C2):
                for k in range(C2):
                    mm = nc.tensor.matmul(halves(ps, 3)[:, c, :], w_proj[:, k, c * P:(c + 1) * P], oT[:, k, :],
                                          start=(k == 0), stop=(k == C2 - 1))
            mm.then_inc(proj_mm, 1)
            pe.wait_ge(proj_out, C2 * (b + 1))
            for tt in range(T):
                for c in range(C2):
                    mm = nc.tensor.transpose(ps[:, 2, (C2 * tt + c) * P:(C2 * tt + c + 1) * P], projT[:, c, tt * P:(tt + 1) * P],
                                             ident[:])
            mm.then_inc(res_mm, 1)

        def turn(f, b, par):
            if f is not None:
                project(f, par)
            if b is not None:
                row_scores(b, 1 - par)
            if f is not None:
                split_qk(f)
            if b is not None:
                for s in range(8):
                    col_scores(b, 1 - par, s)
                    if s >= 2 and s % 2 == 0:
                        values(b, 1 - par, s // 2 - 1)
                values(b, 1 - par, 3)
                output(b)

        steps(turn, pe)


def ffn_block(nc, scope, t, alloc, sems, ps, g):
    x_res, ident, ada = g["x_res"], g["ident"], g["ada"]
    w_fc1, w_fc2, b_fc1, b_fc2 = g["w_fc1"], g["w_fc2"], g["b_fc1"], g["b_fc2"]
    DT = DFF // P
    stats = alloc(scope, "stats_f", [P, T, 6])
    mean_var = alloc(scope, "mean_var_f", [P, T, 2])
    var_eps = alloc(scope, "var_eps_f", [P, T])
    rstd = alloc(scope, "rstd_f", [P, T])
    x_hat = alloc(scope, "x_hat_f", [P, T, F])
    x2T = alloc(scope, "x2T", [P, C2, N])
    hidden = alloc(scope, "hidden", [P, 2, DT, N])
    outT = alloc(scope, "outT_f", [P, C2, N])
    result = alloc(scope, "result", [P, 2, T * F])
    (stats_made, mv_made, eps_made, rstd_made, xhat_made, xt_mm, x2_out, fc1_mm, gelu_made, fc2_mm, outT_made, out_mm,
     result_made) = sems(
        scope, "stats_made_f", "mv_made_f", "eps_made_f", "rstd_made_f", "xhat_made_f", "xt_mm_f", "x2_out", "fc1_mm",
        "gelu_made", "fc2_mm", "outT_made_f", "out_mm_f", "result_made")
    stored = sems(scope, "stored_even", "stored_odd")
    block = scope.enter_context(nc.Block())

    @block.sync
    def _(sp):
        def turn(f, b, par):
            if b is not None:
                sp.wait_ge(result_made, b + 1)
                sp.dma_start(t["out"][bass.ds(b * N, N), :].rearrange("(t p) f -> p t f", p=P),
                             result[:, 1 - par, :].rearrange("p (t f) -> p t f", t=T)).then_inc(stored[1 - par], 16)

        steps(turn, sp)
        for par in range(2):
            sp.wait_ge(stored[par], 16 * (B // 2))

    @block.gpsimd
    def _(pool):
        norm_root(pool, nc, 0, mean_var, g, var_eps, rstd, mv_made, eps_made, rstd_made)

        def turn(f, b, par):
            if following(f) is not None:
                norm_root(pool, nc, following(f), mean_var, g, var_eps, rstd, mv_made, eps_made, rstd_made)

        steps(turn, pool)

    @block.scalar
    def _(act):
        def turn(f, b, par):
            if f is None:
                return
            act.wait_ge(xt_mm, f + 1)
            ge(act, fc1_mm, DT // 2 * f)
            for c in range(C2):
                nc.scalar.activation(x2T[:, c, :], halves(ps, 0)[:, c, :], ACT.Identity, bias=ada[:, 5 * C2 + c, bass.ds(f, 1)],
                                     scale=ada[:, 3 * C2 + c, bass.ds(f, 1)]).then_inc(x2_out, 1)
            ge(act, fc2_mm, f - 1)
            for m in range(DT):
                if m % 2 == 0:
                    act.wait_ge(fc1_mm, DT // 2 * f + m // 2 + 1)
                nc.scalar.activation(hidden[:, par, m, :], halves(ps, 1 + m // 2)[:, m % 2, :], ACT.Gelu,
                                     bias=b_fc1[:, m:m + 1]).then_inc(gelu_made, 1)

        steps(turn, act)

    @block.vector
    def _(dve):
        def turn(f, b, par):
            if f is not None:
                dve.wait_ge(rstd_made, f + 1)
                ge(dve, xt_mm, f)
                for tt in range(T):
                    nc.vector.tensor_scalar(x_hat[:, tt, :], x_res[:, bass.ds(f * T + tt, 1), :].rearrange("p a f -> p (a f)"),
                                            mean_var[:, tt, 0:1], rstd[:, tt:tt + 1], ALU.subtract, ALU.mult).then_inc(xhat_made, 1)
                if following(f) is not None:
                    norm_stats(nc, x_res, following(f), stats, stats_made)
                    dve.wait_ge(stats_made, T * (f + 2))
            if b is not None:
                dve.wait_ge(fc2_mm, b + 1)
                ge(dve, out_mm, b)
                for c in range(C2):
                    nc.vector.tensor_scalar(outT[:, c, :], halves(ps, 5)[:, c, :], b_fc2[:, c:c + 1],
                                            ada[:, C2 + c, bass.ds(b, 1)], ALU.add, ALU.mult).then_inc(outT_made, 1)
                if following(f) is not None:
                    norm_moments(nc, stats, mean_var, mv_made)
                dve.wait_ge(out_mm, b + 1)
                ge(dve, stored[1 - par], loads(b, 1 - par) - 16)
                nc.vector.tensor_tensor(result[:, 1 - par, :], ps[:, 6, :],
                                        x_res[:, bass.ds(b * T, T), :].rearrange("p t f -> p (t f)"), ALU.add).then_inc(result_made, 1)
            elif following(f) is not None:
                norm_moments(nc, stats, mean_var, mv_made)

        norm_stats(nc, x_res, 0, stats, stats_made)
        dve.wait_ge(stats_made, T)
        norm_moments(nc, stats, mean_var, mv_made)
        steps(turn, dve)

    @block.tensor
    def _(pe):
        def hidden_of(f):
            pe.wait_ge(xhat_made, T * (f + 1))
            ge(pe, x2_out, C2 * f)
            for tt in range(T):
                for c in range(C2):
                    mm = nc.tensor.transpose(halves(ps, 0)[:, c, tt * P:(tt + 1) * P], x_hat[:, tt, c * P:(c + 1) * P], ident[:])
            mm.then_inc(xt_mm, 1)
            pe.wait_ge(x2_out, C2 * (f + 1))
            for m in range(DT):
                if m % 2 == 0:
                    ge(pe, gelu_made, DT * (f - 1) + m + 2)
                for k in range(C2):
                    mm = nc.tensor.matmul(halves(ps, 1 + m // 2)[:, m % 2, :], w_fc1[:, k, m * P:(m + 1) * P], x2T[:, k, :],
                                          start=(k == 0), stop=(k == C2 - 1))
                if m % 2 == 1:
                    mm.then_inc(fc1_mm, 1)

        def output(b, par):
            pe.wait_ge(gelu_made, DT * (b + 1))
            ge(pe, outT_made, C2 * b)
            for c in range(C2):
                for m in range(DT):
                    mm = nc.tensor.matmul(halves(ps, 5)[:, c, :], w_fc2[:, m, c * P:(c + 1) * P], hidden[:, par, m, :],
                                          start=(m == 0), stop=(m == DT - 1))
            mm.then_inc(fc2_mm, 1)

        def back_to_tokens(b):
            pe.wait_ge(outT_made, C2 * (b + 1))
            ge(pe, result_made, b)
            for tt in range(T):
                for c in range(C2):
                    mm = nc.tensor.transpose(ps[:, 6, (C2 * tt + c) * P:(C2 * tt + c + 1) * P], outT[:, c, tt * P:(tt + 1) * P],
                                             ident[:])
            mm.then_inc(out_mm, 1)

        def turn(f, b, par):
            if f is not None:
                hidden_of(f)
            if b is not None:
                output(b, 1 - par)
                back_to_tokens(b)

        steps(turn, pe)


def kernel(x, cond_1024, mask_BxSxSx11_ik0, L0_cond_W_self, L0_cond_b_self, L0_cond_w_bias, L0_cond_b_bias, L0_cond_Wq,
           L0_cond_bq, L0_cond_Wk, L0_cond_bk, L0_cond_Wout, L0_cond_bout, L1_cond_mat_qkv_w, L1_cond_q_bias,
           L1_cond_v_bias, L1_cond_scale_mul, L1_cond_proj_w, L1_cond_proj_b, L1_cond_ada_w, L1_cond_ada_b, L1_cond_fc1_w,
           L1_cond_fc1_b, L1_cond_fc2_w, L1_cond_fc2_b):
    import numpy as np
    import concourse.bacc as bacc
    from concourse.bass_utils import run_bass_kernel_spmd

    def columns(a):
        a = np.asarray(a)
        return np.moveaxis(a.reshape(*a.shape[:-1], a.shape[-1] // P, P), -1, 0)

    flat = np.asarray(x).reshape(B * N, F)
    mask = np.asarray(mask_BxSxSx11_ik0)
    adj = np.stack([mask[:, :, :M, :], np.swapaxes(mask[:, :M, :, :], 1, 2)], axis=2)
    arrays = {
        "x": flat, "xT": flat.T, "adj": adj.reshape(B * N, 2 * M * L), "condT": np.asarray(cond_1024).T,
        "w_selfT": np.asarray(L0_cond_W_self).T, "b_self": columns(L0_cond_b_self),
        "w_label": L0_cond_w_bias, "b_label": np.asarray(L0_cond_b_bias).reshape(1),
        "w_qT": np.swapaxes(L0_cond_Wq, 1, 2), "b_q": columns(L0_cond_bq), "w_kT": np.swapaxes(L0_cond_Wk, 1, 2), "b_k": columns(L0_cond_bk),
        "w_oT": np.swapaxes(np.asarray(L0_cond_Wout).reshape(2, F, F), 1, 2), "b_out": columns(L0_cond_bout),
        "w_qkvT": np.asarray(L1_cond_mat_qkv_w).T, "b_qkv_q": L1_cond_q_bias, "b_v": columns(L1_cond_v_bias),
        "scale_mul": np.asarray(L1_cond_scale_mul).reshape(H), "w_projT": np.asarray(L1_cond_proj_w).T,
        "b_proj": columns(L1_cond_proj_b), "w_adaT": np.asarray(L1_cond_ada_w).T, "b_ada": columns(L1_cond_ada_b),
        "w_fc1T": np.asarray(L1_cond_fc1_w).T, "b_fc1": columns(L1_cond_fc1_b), "w_fc2T": np.asarray(L1_cond_fc2_w).T,
        "b_fc2": columns(L1_cond_fc2_b),
    }
    nc = bacc.Bacc("TRN2", target_bir_lowering=False, num_devices=1)
    sent, tensors = {}, {}
    for name, a in arrays.items():
        a = np.ascontiguousarray(a)
        sent[f"in_{name}"] = a
        tensors[name] = nc.dram_tensor(f"in_{name}", a.shape, mybir.dt.from_np(a.dtype), kind="ExternalInput").ap()
    tensors["out"] = nc.dram_tensor("out_x", (B * N, F), F32, kind="ExternalOutput").ap()
    build(nc, tensors)
    ran = run_bass_kernel_spmd(nc, [sent], core_ids=[0])
    return ran.results[0]["out_x"].reshape(B, N, F)
```

```python
from contextlib import ExitStack

import concourse.bass as bass
from concourse import mybir
from concourse.alu_op_type import AluOpType as ALU

F32 = mybir.dt.float32
BF16 = mybir.dt.bfloat16
I32 = mybir.dt.int32
ACT = mybir.ActivationFunctionType
AX_X = mybir.AxisListType.X

P = 128
B, N, F = 16, 256, 256
T = N // P
C2 = F // P
H, HD = 16, 16
HT = P // HD
M, L = 20, 11
G4 = 4 * M
DFF = 1024
NEG = -9000000000000000.0
LN_EPS = 1e-06
NORM_EPS2 = 1e-24
MAX_SCALE_MUL = 4.605170185988092
SEED = 1597463007.0
SLOT = 16
NSLOT = 6
KROWS = NSLOT * SLOT
Q_PARTS = (0, 0, 0, 1, 1, 2)
K_PARTS = (0, 1, 2, 0, 1, 0)


def ge(eng, sem, value):
    if not isinstance(value, int) or value > 0:
        eng.wait_ge(sem, value)


def turns(turn, eng, stages):
    def peeled(i):
        turn(*(i - back if 0 <= i - back < B else None for back in range(stages)), i % 2)

    for i in range(5):
        peeled(i)
    with eng.Fori(0, (B - 6) // 2) as i:
        turn(*(i * 2 + 5 - back for back in range(stages)), 1)
        turn(*(i * 2 + 6 - back for back in range(stages)), 0)
    for i in range(B - 1, B + stages - 1):
        peeled(i)


def loads(b, par):
    return (b - par) * 8 + 16


def following(f):
    return None if f is None or (isinstance(f, int) and f == B - 1) else f + 1


def build(nc, t):
    with ExitStack() as top:
        def alloc(scope, name, shape, dt=F32):
            return scope.enter_context(nc.sbuf_tensor(name, shape, dt))

        def sems(scope, *names):
            return [scope.enter_context(nc.semaphore(n)) for n in names]

        ps = top.enter_context(nc.psum_tensor("ps", [P, 8, 512], F32))

        x_res = alloc(top, "x_res", [P, B * T, F])
        ident = alloc(top, "ident", [P, P])
        ident_b = alloc(top, "ident_b", [P, P], BF16)
        ones = alloc(top, "ones", [P, P])
        neg_half = alloc(top, "neg_half", [P, T])
        ln_eps = alloc(top, "ln_eps", [P, T])
        zero = alloc(top, "zero", [P, 1])
        head_of_row = alloc(top, "head_of_row", [P, HT])
        w_qkv = alloc(top, "w_qkv", [P, C2, 3 * F])
        w_proj = alloc(top, "w_proj", [P, C2, F])
        w_fc1 = alloc(top, "w_fc1", [P, C2, DFF])
        w_fc2 = alloc(top, "w_fc2", [P, DFF // P, F])
        ada = alloc(top, "ada", [P, 6 * C2, B])
        bias_qk = alloc(top, "bias_qk", [P, 2 * F])
        b_v = alloc(top, "b_v", [P, C2])
        b_proj = alloc(top, "b_proj", [P, C2])
        b_fc1 = alloc(top, "b_fc1", [P, DFF // P])
        b_fc2 = alloc(top, "b_fc2", [P, C2])
        head_scale = alloc(top, "head_scale", [P, H])
        late_weights, = sems(top, "late_weights")
        LATE = 9 * 16

        with ExitStack() as graph:
            w_x = alloc(graph, "w_x", [P, C2, F])
            w_q = alloc(graph, "w_q", [P, 2, C2, F])
            b_self = alloc(graph, "b_self", [P, C2])
            b_q = alloc(graph, "b_q", [P, 2, C2])
            b_out = alloc(graph, "b_out", [P, 2, C2])
            b_out_sum = alloc(graph, "b_out_sum", [P, C2])
            w_label = alloc(graph, "w_label", [P, L])
            b_label = alloc(graph, "b_label", [P, 1])
            q_cond = alloc(graph, "q_cond", [P, C2, B])
            k_all = alloc(graph, "k_all", [P, 2 * C2, B * M])
            v_all = alloc(graph, "v_all", [P, 2 * C2, B * M])

            with ExitStack() as setup:
                w_c = alloc(setup, "w_c", [P, C2, F])
                w_k = alloc(setup, "w_k", [P, 2, C2, F])
                w_o = alloc(setup, "w_o", [P, 2, C2, F])
                b_k = alloc(setup, "b_k", [P, 2, C2])
                w_ada = alloc(setup, "w_ada", [P, C2, 6 * F])
                b_ada = alloc(setup, "b_ada", [P, 6 * C2])
                condT = alloc(setup, "condT", [P, C2, B])
                silu = alloc(setup, "silu", [P, C2, B])
                exp_neg = alloc(setup, "exp_neg", [P, C2, B])
                sig = alloc(setup, "sig", [P, C2, B])
                x20 = alloc(setup, "x20", [P, C2, B * M])
                nz20 = alloc(setup, "nz20", [P, B * M])
                cond20 = alloc(setup, "cond20", [P, C2, B * M])
                feat20 = alloc(setup, "feat20", [P, C2, B * M])
                scale_in = alloc(setup, "scale_in", [P, H])
                (consts_set, first_in, ada_in, kv_in, small_in, exp_made, sig_made, silu_made, cond_mm,
                 cond_out, sum20_mm, nz_made, cond20_made, feat20_mm, feat20_made, kv_mm, kv_out,
                 ada_mm, ada_out, chain) = sems(
                    setup, "consts_set", "first_in", "ada_in", "kv_in", "small_in", "exp_made", "sig_made",
                    "silu_made", "cond_mm", "cond_out", "sum20_mm", "nz_made", "cond20_made",
                    "feat20_mm", "feat20_made", "kv_mm", "kv_out", "ada_mm", "ada_out", "setup_chain")
                block = setup.enter_context(nc.Block())

                @block.sync
                def _(sp):
                    sp.dma_start(condT[:], t["condT"].rearrange("(k p) b -> p k b", p=P)).then_inc(first_in, 16)
                    sp.dma_start(w_c[:], t["w_selfT"][F:2 * F, :].rearrange("(k p) n -> p k n", p=P)).then_inc(first_in, 16)
                    sp.dma_start(w_x[:], t["w_selfT"][0:F, :].rearrange("(k p) n -> p k n", p=P)).then_inc(first_in, 16)
                    for k in range(C2):
                        sp.dma_start(x20[:, k, :].rearrange("p (b m) -> p b m", m=M),
                                     t["xT"][k * P:(k + 1) * P, :].rearrange("p (b n) -> p b n", b=B)[:, :, 0:M]
                                     ).then_inc(first_in, 16)
                    sp.dma_start(w_k[:], t["w_kT"].rearrange("d (k p) n -> p d k n", p=P)).then_inc(kv_in, 16)
                    sp.dma_start(w_o[:], t["w_oT"].rearrange("d (k p) n -> p d k n", p=P)).then_inc(kv_in, 16)
                    sp.dma_start(w_ada[:], t["w_adaT"].rearrange("(k p) n -> p k n", p=P)).then_inc(ada_in, 16)
                    sp.dma_start(w_q[:], t["w_qT"].rearrange("d (k p) n -> p d k n", p=P)).then_inc(kv_in, 16)
                    sp.wait_ge(kv_in, 48)
                    sp.wait_ge(small_in, 9 * 16)

                @block.gpsimd
                def _(pool):
                    nc.gpsimd.memset(ident[:], 0.0).then_inc(chain, 1)
                    nc.gpsimd.memset(head_of_row[:], 1.0).then_inc(chain, 1)
                    nc.gpsimd.memset(ones[:], 1.0).then_inc(consts_set, 1)
                    nc.gpsimd.memset(neg_half[:], -0.5).then_inc(consts_set, 1)
                    nc.gpsimd.memset(ln_eps[:], LN_EPS).then_inc(consts_set, 1)
                    nc.gpsimd.memset(zero[:], 0.0).then_inc(consts_set, 1)
                    pool.wait_ge(chain, 2)
                    nc.gpsimd.affine_select(out=ident[:], in_=ident[:], compare_op=ALU.not_equal, fill=1.0, base=0,
                                            pattern=[[-1, P]], channel_multiplier=1).then_inc(consts_set, 1)
                    nc.gpsimd.affine_select(out=head_of_row[:], in_=head_of_row[:], compare_op=ALU.is_ge, fill=0.0,
                                            base=0, pattern=[[-HD, HT]], channel_multiplier=1).then_inc(chain, 1)
                    pool.wait_ge(chain, 3)
                    nc.gpsimd.affine_select(out=head_of_row[:], in_=head_of_row[:], compare_op=ALU.is_ge, fill=0.0,
                                            base=HD - 1, pattern=[[HD, HT]], channel_multiplier=-1).then_inc(consts_set, 1)
                    pool.wait_ge(consts_set, 5)
                    nc.gpsimd.tensor_copy(ident_b[:], ident[:]).then_inc(consts_set, 1)

                @block.scalar
                def _(act):
                    for dst, src in ((b_self, t["b_self"]), (b_ada, t["b_ada"])):
                        act.dma_start(dst[:], src).then_inc(small_in, 16)
                    for dst, src in ((b_k, t["b_k"]), (b_q, t["b_q"]), (b_out, t["b_out"])):
                        act.dma_start(dst[:], src).then_inc(small_in, 16)
                    act.dma_start(w_label[:], t["w_label"].partition_broadcast(P)).then_inc(small_in, 16)
                    act.dma_start(b_label[:], t["b_label"].partition_broadcast(P)).then_inc(small_in, 16)
                    act.dma_start(scale_in[:], t["scale_mul"].partition_broadcast(P)).then_inc(small_in, 16)
                    act.dma_start(bias_qk[:, 0:F], t["b_qkv_q"].partition_broadcast(P)).then_inc(small_in, 16)
                    act.wait_ge(first_in, 80)
                    nc.scalar.activation(exp_neg[:], condT[:], ACT.Exp, scale=-1.0).then_inc(exp_made, 1)
                    for dst, src in ((w_qkv, t["w_qkvT"]), (w_proj, t["w_projT"]), (w_fc1, t["w_fc1T"]),
                                     (w_fc2, t["w_fc2T"])):
                        act.dma_start(dst[:], src.rearrange("(k p) n -> p k n", p=P)).then_inc(late_weights, 16)
                    for dst, src in ((b_v, t["b_v"]), (b_proj, t["b_proj"]), (b_fc1, t["b_fc1"]), (b_fc2, t["b_fc2"])):
                        act.dma_start(dst[:], src).then_inc(late_weights, 16)
                    act.wait_ge(small_in, 9 * 16)
                    act.wait_ge(chain, 4)
                    nc.scalar.activation(head_scale[:], scale_in[:], ACT.Exp).then_inc(exp_made, 1)
                    for c in range(2 * C2):
                        act.wait_ge(kv_mm, 2 * c + 1)
                        nc.scalar.activation(k_all[:, c, :], ps[:, 4, 0:B * M], ACT.Identity,
                                             bias=b_k[:, c // C2, c % C2:c % C2 + 1]).then_inc(kv_out, 1)
                        act.wait_ge(kv_mm, 2 * c + 2)
                        nc.scalar.activation(v_all[:, c, :], ps[:, 5, 0:B * M], ACT.Copy).then_inc(kv_out, 1)

                @block.vector
                def _(dve):
                    nc.vector.memset(bias_qk[:, F:2 * F], 0.0).then_inc(late_weights, 16)
                    dve.wait_ge(small_in, 9 * 16)
                    dve.wait_ge(chain, 3)
                    nc.vector.tensor_scalar(scale_in[:], scale_in[:], MAX_SCALE_MUL, None, ALU.min).then_inc(chain, 1)
                    nc.vector.tensor_scalar(b_q[:], b_q[:], float(HD) ** -0.5, None, ALU.mult).then_inc(chain, 1)
                    nc.vector.tensor_tensor(b_out_sum[:], b_out[:, 0, :], b_out[:, 1, :], ALU.add).then_inc(chain, 1)
                    dve.wait_ge(exp_made, 1)
                    nc.vector.tensor_scalar(sig[:], exp_neg[:], 1.0, None, ALU.add).then_inc(sig_made, 1)
                    dve.wait_ge(sig_made, 1)
                    nc.vector.reciprocal(sig[:], sig[:]).then_inc(sig_made, 1)
                    dve.wait_ge(sig_made, 2)
                    nc.vector.tensor_tensor(silu[:], condT[:], sig[:], ALU.mult).then_inc(silu_made, 1)
                    dve.wait_ge(cond_mm, 1)
                    nc.vector.tensor_copy(q_cond[:], ps[:, 0, 0:C2 * B].rearrange("p (k b) -> p k b", b=B)).then_inc(cond_out, 1)
                    dve.wait_ge(sum20_mm, 1)
                    nc.vector.tensor_scalar(nz20[:], ps[:, 1, 0:B * M], 0.0, None, ALU.not_equal).then_inc(nz_made, 1)
                    dve.wait_ge(nz_made, 1)
                    dve.wait_ge(cond_out, 1)
                    for k in range(C2):
                        nc.vector.tensor_tensor(cond20[:, k, :].rearrange("p (b m) -> p b m", m=M),
                                                nz20[:].rearrange("p (b m) -> p b m", m=M),
                                                q_cond[:, k, :].unsqueeze(2).broadcast_to([P, B, M]), ALU.mult).then_inc(cond20_made, 1)
                    dve.wait_ge(cond20_made, C2)
                    dve.wait_ge(feat20_mm, 1)
                    for k in range(C2):
                        nc.vector.scalar_tensor_tensor(out=feat20[:, k, :], in0=ps[:, 2 + k, 0:B * M], scalar=b_self[:, k:k + 1],
                                                       in1=cond20[:, k, :], op0=ALU.add, op1=ALU.add).then_inc(feat20_made, 1)
                    dve.wait_ge(ada_mm, 1)
                    for j in range(6 * C2):
                        scaled = 2 * C2 <= j < 4 * C2
                        nc.vector.tensor_scalar(ada[:, j, :], ps[:, 6, j * B:(j + 1) * B], b_ada[:, j:j + 1],
                                                1.0 if scaled else 0.0, ALU.add, ALU.add).then_inc(ada_out, 1)

                @block.tensor
                def _(pe):
                    pe.wait_ge(first_in, 80)
                    for f in range(C2):
                        for k in range(C2):
                            mm = nc.tensor.matmul(ps[:, 0, f * B:(f + 1) * B], w_c[:, k, f * P:(f + 1) * P], condT[:, k, :],
                                                  start=(k == 0), stop=(k == C2 - 1))
                    mm.then_inc(cond_mm, 1)
                    pe.wait_ge(consts_set, 7)
                    for k in range(C2):
                        mm = nc.tensor.matmul(ps[:, 1, 0:B * M], ones[:], x20[:, k, :], start=(k == 0), stop=(k == C2 - 1))
                    mm.then_inc(sum20_mm, 1)
                    for f in range(C2):
                        for k in range(C2):
                            mm = nc.tensor.matmul(ps[:, 2 + f, 0:B * M], w_x[:, k, f * P:(f + 1) * P], x20[:, k, :],
                                                  start=(k == 0), stop=(k == C2 - 1))
                    mm.then_inc(feat20_mm, 1)
                    pe.wait_ge(ada_in, 16)
                    pe.wait_ge(silu_made, 1)
                    for j in range(6 * C2):
                        for k in range(C2):
                            mm = nc.tensor.matmul(ps[:, 6, j * B:(j + 1) * B], w_ada[:, k, j * P:(j + 1) * P], silu[:, k, :],
                                                  start=(k == 0), stop=(k == C2 - 1))
                    mm.then_inc(ada_mm, 1)
                    pe.wait_ge(kv_in, 48)
                    pe.wait_ge(feat20_made, C2)
                    for c in range(2 * C2):
                        d, f = c // C2, c % C2
                        for bank, w in ((4, w_k), (5, w_o)):
                            ge(pe, kv_out, 2 * c + bank - 5)
                            for k in range(C2):
                                mm = nc.tensor.matmul(ps[:, bank, 0:B * M], w[:, d, k, f * P:(f + 1) * P], feat20[:, k, :],
                                                      start=(k == 0), stop=(k == C2 - 1))
                            mm.then_inc(kv_mm, 1)

            graph_block(nc, graph, t, alloc, sems, ps, dict(
                x_res=x_res, ident=ident, ones=ones, head_of_row=head_of_row, w_x=w_x, w_q=w_q, b_self=b_self, b_q=b_q,
                b_out_sum=b_out_sum, w_label=w_label, b_label=b_label, q_cond=q_cond, k_all=k_all, v_all=v_all))

        with ExitStack() as attention:
            attention_block(nc, attention, t, alloc, sems, ps, dict(
                x_res=x_res, ident=ident, ident_b=ident_b, neg_half=neg_half, ln_eps=ln_eps, zero=zero, w_qkv=w_qkv, w_proj=w_proj, ada=ada,
                bias_qk=bias_qk, b_v=b_v, b_proj=b_proj, head_scale=head_scale, late_weights=late_weights, LATE=LATE))

        with ExitStack() as ffn:
            ffn_block(nc, ffn, t, alloc, sems, ps, dict(
                x_res=x_res, ident=ident, neg_half=neg_half, ln_eps=ln_eps, zero=zero, w_fc1=w_fc1, w_fc2=w_fc2, ada=ada, b_fc1=b_fc1, b_fc2=b_fc2))


def halves(ps, bank):
    return ps[:, bank, :].rearrange("p (a n) -> p a n", a=2)


def graph_block(nc, scope, t, alloc, sems, ps, g):
    x_res, ident, ones, head_of_row = g["x_res"], g["ident"], g["ones"], g["head_of_row"]
    w_x, w_q, b_self, b_q, b_out_sum = g["w_x"], g["w_q"], g["b_self"], g["b_q"], g["b_out_sum"]
    w_label, b_label, q_cond, k_all, v_all = g["w_label"], g["b_label"], g["q_cond"], g["k_all"], g["v_all"]
    E2 = T * 2 * M
    xT = alloc(scope, "xT", [P, 2, C2, N])
    x_in = alloc(scope, "x_in", [P, 2, T, F])
    adj = alloc(scope, "adj", [P, 2, E2 * L], I32)
    weighted = alloc(scope, "weighted", [P, E2 * L])
    count = alloc(scope, "count", [P, E2])
    no_edge = alloc(scope, "no_edge", [P, E2])
    label_bias = alloc(scope, "label_bias", [P, E2])
    edge_bias = alloc(scope, "edge_bias", [P, 2, T, 2, M])
    nz = alloc(scope, "nz", [P, N])
    cond = alloc(scope, "cond", [P, C2, N])
    qT = alloc(scope, "qT", [P, 2, 2, C2, N])
    k_blocks = alloc(scope, "k_blocks", [P, 2, 2 * C2, HT, M])
    v_masked = alloc(scope, "v_masked", [P, 2 * C2, HT, M])
    v_blocks = alloc(scope, "v_blocks", [G4, 2, H // 2, 64])
    scores = alloc(scope, "scores", [P, 2, 2, T, H, M])
    row_max = alloc(scope, "row_max", [P, 2, T, H])
    total = alloc(scope, "row_sum", [P, 2, T, H])
    inverse = alloc(scope, "row_inverse", [P, 2, T, H])
    weightT = alloc(scope, "weightT", [G4, 2, T, 4, P])
    outT = alloc(scope, "outT", [P, C2, N])
    xT_in, x_arrived, adj_in = (sems(scope, f"{n}_even", f"{n}_odd") for n in ("xT_in", "x_in_arrived", "adj_in"))
    (sums_mm, nz_made, cond_made, feat_mm, feat_out, q_mm, q_out, kb_made, vm_made, vt_mm,
     vb_made, cnt_made, lab_w, lab_made, neg_made, edge_made, aff_mm, aff_out, max_made, shifted, exp_made,
     sum_made, rec_made, norm_made, wT_mm, wT_out, pv_mm, outT_made, out_mm, x_made) = sems(
        scope, "sums_mm", "nz_made_g", "cond_made", "feat_mm", "feat_out", "q_mm", "q_out",
        "kb_made", "vm_made", "vt_mm", "vb_made", "cnt_made", "lab_w", "lab_made", "neg_made", "edge_made",
        "aff_mm", "aff_out", "max_made", "shifted", "exp_made_g", "sum_made", "rec_made", "norm_made", "wT_mm", "wT_out",
        "pv_mm", "outT_made", "out_mm", "x_made")
    block = scope.enter_context(nc.Block())

    def feat_at(b):
        return x_res[:, bass.ds(b * T, T), :]

    @block.sync
    def _(sp):
        def turn(f, b, c, par):
            if f is not None:
                ge(sp, feat_mm, f - 1)
                sp.dma_start(xT[:, par], t["xT"][:, bass.ds(f * N, N)].rearrange("(k p) n -> p k n", p=P)).then_inc(xT_in[par], 16)
                ge(sp, lab_w, f - 1)
                ge(sp, cnt_made, f - 1)
                sp.dma_start(adj[:, par].rearrange("p (t e) -> p t e", t=T),
                             t["adj"][bass.ds(f * N, N), :].rearrange("(t p) e -> p t e", p=P)).then_inc(adj_in[par], 16)
            if b is not None:
                ge(sp, x_made, b - 1)
                sp.dma_start(x_in[:, 1 - par], t["x"][bass.ds(b * N, N), :].rearrange("(t p) f -> p t f", p=P)
                             ).then_inc(x_arrived[1 - par], 16)

        turns(turn, sp, 3)

    @block.gpsimd
    def _(pool):
        own = head_of_row[:].unsqueeze(2).broadcast_to([P, HT, M])

        def shift(b, par, d):
            pool.wait_ge(max_made, 2 * b + d + 1)
            nc.gpsimd.tensor_tensor(scores[:, par, d], scores[:, par, d], row_max[:, d].unsqueeze(3).broadcast_to([P, T, H, M]),
                                    ALU.subtract).then_inc(shifted, 1)

        def normalise(b, par, d):
            pool.wait_ge(rec_made, 2 * b + d + 1)
            nc.gpsimd.tensor_tensor(scores[:, par, d], scores[:, par, d], inverse[:, d].unsqueeze(3).broadcast_to([P, T, H, M]),
                                    ALU.mult).then_inc(norm_made, 1)

        def turn(f, b, c, par):
            if b is not None:
                ge(pool, vt_mm, 2 * b)
                for k in range(2 * C2):
                    nc.gpsimd.tensor_tensor(v_masked[:, k], v_all[:, k, bass.ds(b * M, M)].unsqueeze(1).broadcast_to([P, HT, M]),
                                            own, ALU.mult).then_inc(vm_made, 1)
                shift(b, 1 - par, 0)
            if f is not None:
                ge(pool, aff_mm, 2 * (f - 1))
                for k in range(2 * C2):
                    nc.gpsimd.tensor_tensor(k_blocks[:, par, k], k_all[:, k, bass.ds(f * M, M)].unsqueeze(1).broadcast_to([P, HT, M]),
                                            own, ALU.mult).then_inc(kb_made, 1)
            if b is not None:
                shift(b, 1 - par, 1)
                normalise(b, 1 - par, 0)
                normalise(b, 1 - par, 1)

        turns(turn, pool, 3)

    @block.scalar
    def _(act):
        def exponentials(b, par, d):
            act.wait_ge(shifted, 2 * b + d + 1)
            nc.scalar.activation(scores[:, par, d], scores[:, par, d], ACT.Exp).then_inc(exp_made, 1)

        def take_queries(f, par, d):
            act.wait_ge(q_mm, 2 * f + d + 1)
            for k in range(C2):
                nc.scalar.activation(qT[:, par, d, k, :], halves(ps, 2 + d)[:, k, :], ACT.Identity,
                                     bias=b_q[:, d, k:k + 1], scale=float(HD) ** -0.5).then_inc(q_out, 1)

        def take_weights(c, d):
            act.wait_ge(wT_mm, 2 * c + d + 1)
            ge(act, pv_mm, c)
            nc.scalar.activation(weightT[:, d], ps[0:G4, 6:8, :].rearrange("p t (c n) -> p t c n", c=4),
                                 ACT.Copy).then_inc(wT_out, 1)

        def turn(f, b, c, par):
            if f is not None:
                act.wait_ge(nz_made, f + 1)
                ge(act, feat_out, f)
                for k in range(C2):
                    nc.scalar.activation(cond[:, k, :], nz[:], ACT.Identity, bias=b_self[:, k:k + 1],
                                         scale=q_cond[:, k, bass.ds(f, 1)]).then_inc(cond_made, 1)
            if c is not None:
                take_weights(c, 0)
                take_weights(c, 1)
            if f is not None:
                take_queries(f, par, 0)
            if b is not None:
                exponentials(b, 1 - par, 0)
                act.wait_ge(vt_mm, 2 * b + 2)
                ge(act, pv_mm, b - 1)
                nc.scalar.activation(v_blocks[:, 1 - par], ps[0:G4, 0, :].rearrange("p (c v) -> p c v", v=64),
                                     ACT.Copy).then_inc(vb_made, 1)
                exponentials(b, 1 - par, 1)
            if f is not None:
                ge(act, aff_mm, 2 * (f - 1))
                take_queries(f, par, 1)

        turns(turn, act, 3)

    @block.vector
    def _(dve):
        def raw_scores(b, par, d):
            dve.wait_ge(edge_made, b + 1)
            dve.wait_ge(aff_mm, 2 * b + d + 1)
            ge(dve, wT_mm, 2 * (b - 2) + d + 1)
            for tt in range(T):
                nc.vector.tensor_tensor(
                    scores[:, par, d, tt], ps[:, 4 + tt, 0:H * M].rearrange("p (h m) -> p h m", m=M),
                    edge_bias[:, par, tt, d, :].unsqueeze(1).broadcast_to([P, H, M]), ALU.add).then_inc(aff_out, 1)
            dve.wait_ge(aff_out, T * (2 * b + d + 1))
            nc.vector.tensor_reduce(row_max[:, d], scores[:, par, d], AX_X, ALU.max).then_inc(max_made, 1)

        def nonzero(f):
            dve.wait_ge(sums_mm, f + 1)
            ge(dve, cond_made, C2 * f)
            nc.vector.tensor_scalar(nz[:], halves(ps, 4)[:, 0, :], 0.0, None, ALU.not_equal).then_inc(nz_made, 1)

        def features(f):
            dve.wait_ge(feat_mm, f + 1)
            dve.wait_ge(cond_made, C2 * (f + 1))
            nc.vector.tensor_tensor(feat_at(f), halves(ps, 1), cond[:], ALU.add).then_inc(feat_out, 1)

        def label_products(f, par):
            dve.wait_ge(adj_in[par], loads(f, par))
            edges = adj[:, par].rearrange("p (e l) -> p e l", l=L)
            nc.vector.tensor_reduce(count[:], edges, AX_X, ALU.add).then_inc(cnt_made, 1)
            nc.vector.tensor_tensor(weighted[:].rearrange("p (e l) -> p e l", l=L), edges,
                                    w_label[:].unsqueeze(1).broadcast_to([P, E2, L]), ALU.mult).then_inc(lab_w, 1)

        def label_sums(f, par):
            dve.wait_ge(cnt_made, f + 1)
            nc.vector.tensor_scalar(no_edge[:], count[:], 0.0, NEG, ALU.is_le, ALU.mult).then_inc(neg_made, 1)
            dve.wait_ge(lab_w, f + 1)
            nc.vector.tensor_reduce(label_bias[:], weighted[:].rearrange("p (e l) -> p e l", l=L), AX_X,
                                    ALU.add).then_inc(lab_made, 1)

        def edge_biases(f, par):
            dve.wait_ge(neg_made, f + 1)
            dve.wait_ge(lab_made, f + 1)
            nc.vector.scalar_tensor_tensor(out=edge_bias[:, par].rearrange("p t d m -> p (t d m)"), in0=label_bias[:],
                                           scalar=b_label[:, 0:1], in1=no_edge[:], op0=ALU.add, op1=ALU.add).then_inc(edge_made, 1)

        def sums(b, par, d):
            dve.wait_ge(exp_made, 2 * b + d + 1)
            nc.vector.tensor_reduce(total[:, d], scores[:, par, d], AX_X, ALU.add).then_inc(sum_made, 1)
            dve.wait_ge(sum_made, 2 * b + d + 1)
            nc.vector.reciprocal(inverse[:, d], total[:, d]).then_inc(rec_made, 1)

        def take_output(c):
            dve.wait_ge(pv_mm, c + 1)
            ge(dve, out_mm, c)
            for k in range(C2):
                nc.vector.scalar_tensor_tensor(out=outT[:, k, :], in0=halves(ps, 1)[:, k, :], scalar=b_out_sum[:, k:k + 1],
                                               in1=feat_at(c)[:, k, :], op0=ALU.add, op1=ALU.add).then_inc(outT_made, 1)

        def residual(c, par):
            dve.wait_ge(out_mm, c + 1)
            dve.wait_ge(x_arrived[par], loads(c, par))
            dve.wait_ge(outT_made, C2 * (c + 1))
            nc.vector.scalar_tensor_tensor(
                out=x_res[:, bass.ds(c * T, T), :].rearrange("p t f -> p (t f)"), in0=ps[:, 0, :], scalar=0.0,
                in1=x_in[:, par].rearrange("p t f -> p (t f)"), op0=ALU.max, op1=ALU.add).then_inc(x_made, 1)

        def turn(f, b, c, par):
            if f is not None:
                nonzero(f)
                features(f)
            if b is not None:
                raw_scores(b, 1 - par, 0)
            if f is not None:
                label_products(f, par)
            if b is not None:
                raw_scores(b, 1 - par, 1)
            if c is not None:
                take_output(c)
            if b is not None:
                sums(b, 1 - par, 0)
            if f is not None:
                label_sums(f, par)
            if b is not None:
                sums(b, 1 - par, 1)
            if f is not None:
                edge_biases(f, par)
            if c is not None:
                residual(c, par)

        turns(turn, dve, 3)

    @block.tensor
    def _(pe):
        def raw_scores(b, par, d):
            pe.wait_ge(q_out, 4 * b + 2 * d + 2)
            pe.wait_ge(kb_made, 2 * C2 * (b + 1))
            ge(pe, aff_out, T * (2 * b + d))
            if d == 0:
                pe.wait_ge(nz_made, B if following(b) is None else b + 2)
                pe.wait_ge(vm_made, 2 * C2 * (b + 1))
                ge(pe, x_made, b - 1)
            else:
                pe.wait_ge(vt_mm, 2 * b + 1)
            for tt in range(T):
                for k in range(C2):
                    mm = nc.tensor.matmul(ps[:, 4 + tt, k * HT * M:(k + 1) * HT * M], qT[:, par, d, k, tt * P:(tt + 1) * P],
                                          k_blocks[:, par, C2 * d + k].rearrange("p h m -> p (h m)"), start=True, stop=True)
            mm.then_inc(aff_mm, 1)

        def row_sums(f, par):
            pe.wait_ge(xT_in[par], loads(f, par))
            ge(pe, aff_out, 2 * T * (f - 1))
            for k in range(C2):
                mm = nc.tensor.matmul(halves(ps, 4)[:, 0, :], ones[:], xT[:, par, k, :], start=(k == 0), stop=(k == C2 - 1))
            mm.then_inc(sums_mm, 1)

        def features(f, par):
            ge(pe, outT_made, C2 * (f - 2))
            for m in range(C2):
                for k in range(C2):
                    mm = nc.tensor.matmul(halves(ps, 1)[:, m, :], w_x[:, k, m * P:(m + 1) * P], xT[:, par, k, :],
                                          start=(k == 0), stop=(k == C2 - 1))
            mm.then_inc(feat_mm, 1)

        def queries(f, d):
            pe.wait_ge(feat_out, f + 1)
            ge(pe, q_out, 2 * C2 * f)
            for m in range(C2):
                for k in range(C2):
                    mm = nc.tensor.matmul(halves(ps, 2 + d)[:, m, :], w_q[:, d, k, m * P:(m + 1) * P], feat_at(f)[:, k, :],
                                          start=(k == 0), stop=(k == C2 - 1))
            mm.then_inc(q_mm, 1)

        def values_transposed(b, j):
            for k in range(2 * C2):
                o = (2 * k + j) * 64
                mm = nc.tensor.transpose(ps[0:G4, 0, o:o + 64],
                                         v_masked[64 * j:64 * j + 64, k, 4 * j:4 * j + 4].rearrange("p h m -> p (h m)"),
                                         ident[64 * j:64 * j + 64, 64 * j:64 * j + 64])
            mm.then_inc(vt_mm, 1)

        def weights_of(c, par, d):
            pe.wait_ge(norm_made, 2 * c + d + 1)
            ge(pe, wT_out, 2 * c + d)
            for tt in range(T):
                for k in range(4):
                    mm = nc.tensor.transpose(ps[0:G4, 6 + tt, k * P:(k + 1) * P],
                                             scores[:, par, d, tt, 4 * k:4 * k + 4].rearrange("p h m -> p (h m)"), ident[:])
            mm.then_inc(wT_mm, 1)

        def output_channels(c, par, fronts):
            pe.wait_ge(wT_out, 2 * c + 2)
            pe.wait_ge(feat_out, fronts)
            pe.wait_ge(vb_made, c + 1)
            for m in range(C2):
                for d in range(2):
                    for j in range(2):
                        mm = nc.tensor.matmul(halves(ps, 1)[64 * j:64 * j + 64, m, :], v_blocks[:, par, 2 * (C2 * d + m) + j, :],
                                              weightT[:, d, :, 2 * m + j, :], start=(d == 0), stop=(d == 1))
            mm.then_inc(pv_mm, 1)

        def output_tokens(c, backs):
            pe.wait_ge(outT_made, C2 * (c + 1))
            pe.wait_ge(vb_made, backs)
            for tt in range(T):
                for k in range(C2):
                    mm = nc.tensor.transpose(ps[:, 0, (C2 * tt + k) * P:(C2 * tt + k + 1) * P], outT[:, k, tt * P:(tt + 1) * P],
                                             ident[:])
            mm.then_inc(out_mm, 1)

        def turn(f, b, c, par):
            if f is not None:
                row_sums(f, par)
                features(f, par)
            if c is not None:
                weights_of(c, par, 0)
            if b is not None:
                raw_scores(b, 1 - par, 0)
                values_transposed(b, 0)
            if c is not None:
                weights_of(c, par, 1)
            if f is not None:
                queries(f, 0)
            if b is not None:
                raw_scores(b, 1 - par, 1)
                values_transposed(b, 1)
            if c is not None:
                output_channels(c, par, B if f is None else f + 1)
            if f is not None:
                queries(f, 1)
            if c is not None:
                output_tokens(c, B if b is None else b + 1)

        turns(turn, pe, 3)


def norm_stats(nc, x_res, b, stats, stats_made):
    for tt in range(T):
        nc.vector.bn_stats(stats[:, tt, :], x_res[:, bass.ds(b * T + tt, 1), :].rearrange("p a f -> p (a f)")).then_inc(stats_made, 1)


def norm_moments(nc, stats, mean_var, mv_made):
    for tt in range(T):
        nc.vector.bn_aggr(mean_var[:, tt, :], stats[:, tt, :]).then_inc(mv_made, 1)


def norm_root(pool, nc, b, mean_var, g, var_eps, rstd, mv_made, eps_made, rstd_made):
    pool.wait_ge(mv_made, T * (b + 1))
    nc.gpsimd.tensor_tensor(var_eps[:], mean_var[:, :, 1], g["ln_eps"][:], ALU.add).then_inc(eps_made, 1)
    pool.wait_ge(eps_made, b + 1)
    nc.gpsimd.tensor_tensor(rstd[:], var_eps[:], g["neg_half"][:], ALU.pow).then_inc(rstd_made, 1)


def attention_block(nc, scope, t, alloc, sems, ps, g):
    x_res, ident, ident_b = g["x_res"], g["ident"], g["ident_b"]
    w_qkv, w_proj, ada, bias_qk = g["w_qkv"], g["w_proj"], g["ada"], g["bias_qk"]
    b_v, b_proj, head_scale = g["b_v"], g["b_proj"], g["head_scale"]
    HH = T * 2 * H
    parts_dram = nc.dram_tensor("parts_dram", (2, HT, 3, HD, C2 * N), BF16, kind="Internal").ap()
    stats = alloc(scope, "stats", [P, T, 6])
    mean_var = alloc(scope, "mean_var", [P, T, 2])
    var_eps = alloc(scope, "var_eps", [P, T])
    rstd = alloc(scope, "rstd", [P, T])
    x_hat = alloc(scope, "x_hat", [P, T, F])
    x1T = alloc(scope, "x1T", [P, 2, C2, N])
    qk = alloc(scope, "qk", [P, T, 2 * F])
    squares = alloc(scope, "squares", [P, T, 2 * F])
    sum_sq = alloc(scope, "sum_sq", [P, HH])
    minus_half = alloc(scope, "minus_half", [P, HH])
    root = [alloc(scope, f"root{i}", [P, HH]) for i in range(2)]
    root_sq = alloc(scope, "root_sq", [P, HH])
    root_err = alloc(scope, "root_err", [P, HH])
    qkn = alloc(scope, "qkn", [P, T, 2 * F])
    parts = alloc(scope, "parts", [P, 2, 3, C2 * N], BF16)
    rest = alloc(scope, "rest", [P, 2, C2 * N])
    q_stack = alloc(scope, "q_stack", [KROWS + 1, 2, H, N], BF16)
    k_stack = alloc(scope, "k_stack", [KROWS + 1, 2, H, N], BF16)
    v_ones = alloc(scope, "v_ones", [P, 2, T, H, 2 * HD])
    neg_max = alloc(scope, "neg_max", [P, T, H], BF16)
    neg_maxT = alloc(scope, "neg_maxT", [HT, 2, N], BF16)
    probsT = alloc(scope, "probsT", [P, 4, 1024])
    o_sumsT = alloc(scope, "o_sumsT", [P, 2, 2 * N])
    denom = alloc(scope, "denom", [P, T, H])
    o_tok = alloc(scope, "o_tok", [P, T, F])
    oT = alloc(scope, "oT", [P, C2, N])
    projT = alloc(scope, "projT", [P, C2, N])
    (stats_made, mv_made, eps_made, rstd_made, xhat_made, xt_mm, x1_out, qk_mm, qk_out, v_mm, v_out, sq_made, ss_made,
     root_step, qkn_made, qkt_mm, high_made, rest_made, mid_made, low_made, parts_out, stack_in, s_mm, max_made, m_mm, m_out,
     m_low_in, m_high_in, st_mm, exp_made, pv_mm, os_out, otok_mm, den_made, otok_made, ot_mm, ot_out, proj_mm, proj_out,
     res_mm, res_made, consts) = sems(
        scope, "stats_made", "mv_made", "eps_made", "rstd_made", "xhat_made", "xt_mm", "x1_out", "qk_mm", "qk_out", "v_mm",
        "v_out", "sq_made", "ss_made", "root_step", "qkn_made", "qkt_mm", "high_made", "rest_made", "mid_made", "low_made",
        "parts_out", "stack_in", "s_mm", "max_made_a", "m_mm", "m_out", "m_low_in", "m_high_in", "st_mm", "exp_made_a",
        "pv_mm_a", "os_out", "otok_mm", "den_made", "otok_made", "ot_mm", "ot_out", "proj_mm", "proj_out", "res_mm",
        "res_made", "consts")
    m_row_in = (m_low_in, m_high_in)
    block = scope.enter_context(nc.Block())
    SLOTS = 10

    @block.sync
    def _(sp):
        def turn(f, b, c, d, par):
            if f is None:
                return
            ge(sp, stack_in, f * (9 * 16))
            for part, made in enumerate((high_made, mid_made, low_made)):
                for w in range(2):
                    sp.wait_ge(made, 2 * f + w + 1)
                    sp.dma_start(parts_dram[w, :, part], parts[:, w, part]).then_inc(parts_out, 16)
            sp.wait_ge(parts_out, 6 * 16 * (f + 1))
            ge(sp, st_mm, f * 8 - 8)

            def rows(stack, at, n):
                return stack[at * SLOT:(at + n) * SLOT, par].rearrange("p (h c) n -> p h (c n)", c=C2)

            def whole(w, part, n):
                return parts_dram[w, :, part:part + n].rearrange("h a d x -> (a d) h x")

            for slot, part in enumerate(Q_PARTS):
                sp.dma_start(rows(q_stack, slot, 1), whole(0, part, 1)).then_inc(stack_in, 16)
            for slot, n in ((0, 3), (3, 2), (5, 1)):
                sp.dma_start(rows(k_stack, slot, n), whole(1, 0, n)).then_inc(stack_in, 16)

        turns(turn, sp, 4)

    @block.gpsimd
    def _(pool):
        nc.gpsimd.memset(v_ones[:], 1.0).then_inc(consts, 1)
        pool.wait_ge(consts, 1)
        nc.gpsimd.memset(k_stack[KROWS:KROWS + 1], 1.0).then_inc(consts, 1)
        pool.wait_ge(consts, 2)
        norm_root(pool, nc, 0, mean_var, g, var_eps, rstd, mv_made, eps_made, rstd_made)

        def turn(f, b, c, d, par):
            ahead = following(f)
            if ahead is not None:
                norm_root(pool, nc, ahead, mean_var, g, var_eps, rstd, mv_made, eps_made, rstd_made)
            if f is not None:
                for w in range(2):
                    pool.wait_ge(mid_made, 2 * f + w + 1)
                    nc.gpsimd.tensor_tensor(parts[:, w, 2, :], rest[:, w, :], parts[:, w, 1, :], ALU.subtract).then_inc(low_made, 1)

        turns(turn, pool, 4)

    @block.scalar
    def _(act):
        def shift_scale(n, par):
            act.wait_ge(xt_mm, n + 1)
            ge(act, v_mm, n - 1)
            for k in range(C2):
                nc.scalar.activation(x1T[:, par, k, :], halves(ps, 1)[:, k, :], ACT.Identity,
                                     bias=ada[:, 4 * C2 + k, bass.ds(n, 1)],
                                     scale=ada[:, 2 * C2 + k, bass.ds(n, 1)]).then_inc(x1_out, 1)

        def square(f, tt):
            act.wait_ge(qk_out, T * f + tt + 1)
            ge(act, ss_made, f)
            nc.scalar.activation(squares[:, tt, :], qk[:, tt, :], ACT.Square).then_inc(sq_made, 1)

        def take_v(b, par):
            act.wait_ge(v_mm, b + 1)
            ge(act, pv_mm, 4 * (b - 1))
            if isinstance(b, int):
                ge(act, consts, 2)
            nc.scalar.activation(v_ones[:, par, :, :, 0:HD], halves(ps, 0).rearrange("p t (h d) -> p t h d", d=HD),
                                 ACT.Copy).then_inc(v_out, 1)

        def take_maxima(b, par, i):
            act.wait_ge(m_mm, 2 * b + i + 1)
            ge(act, m_row_in[i], 16 * b)
            nc.scalar.activation(neg_maxT[:, i, :], ps[0:HT, 3 + i, 0:N // 2].bitcast(BF16), ACT.Copy).then_inc(m_out, 1)
            act.wait_ge(m_out, 2 * b + i + 1)
            act.dma_start(q_stack[KROWS:KROWS + 1, par, HT * i:HT * (i + 1)], neg_maxT[:, i, :]).then_inc(m_row_in[i], 16)

        def probabilities(c, s):
            act.wait_ge(st_mm, 8 * c + s + 1)
            ge(act, pv_mm, 4 * c + s // 2 - 1)
            nc.scalar.activation(probsT[:, s % 4, :], ps[:, 6:8, :].rearrange("p a n -> p (a n)"),
                                 ACT.Exp).then_inc(exp_made, 1)

        def take_sums(c, i):
            act.wait_ge(pv_mm, 4 * c + 2 * i + 2)
            ge(act, otok_mm, c)
            nc.scalar.activation(o_sumsT[:, i, :], ps[:, 2 + i, :], ACT.Copy).then_inc(os_out, 1)

        def add_bias_v(d):
            act.wait_ge(ot_mm, d + 1)
            ge(act, proj_mm, d)
            for k in range(C2):
                nc.scalar.activation(oT[:, k, :], halves(ps, 0)[:, k, :], ACT.Identity, bias=b_v[:, k:k + 1]).then_inc(ot_out, 1)

        def turn(f, b, c, d, par):
            for s in range(SLOTS):
                if f is not None and s == 2:
                    square(f, 1)
                if c is not None and s < 8:
                    probabilities(c, s)
                if f is not None and s == 1:
                    square(f, 0)
                if b is not None and s == 2:
                    take_v(b, 1 - par)
                if f is not None and s == 4:
                    ge(act, parts_out, 6 * 16 * f)
                    for w in range(2):
                        act.wait_ge(qkt_mm, 2 * f + w + 1)
                        nc.scalar.activation(parts[:, w, 0, :], ps[:, w, :], ACT.Copy).then_inc(high_made, 1)
                if f is not None and s == 5:
                    for w in range(2):
                        act.wait_ge(rest_made, 2 * f + w + 1)
                        nc.scalar.activation(parts[:, w, 1, :], rest[:, w, :], ACT.Copy).then_inc(mid_made, 1)
                if b is not None and s == 6:
                    take_maxima(b, 1 - par, 0)
                if d is not None and s == 7:
                    add_bias_v(d)
                if c is not None and s == 7:
                    take_sums(c, 0)
            if following(f) is not None:
                shift_scale(following(f), 1 - par)
            if c is not None:
                take_sums(c, 1)
            if b is not None:
                take_maxima(b, 1 - par, 1)

        shift_scale(0, 0)
        turns(turn, act, 4)

    @block.vector
    def _(dve):
        def normalise(n):
            dve.wait_ge(rstd_made, n + 1)
            ge(dve, xt_mm, n)
            for tt in range(T):
                nc.vector.tensor_scalar(x_hat[:, tt, :], x_res[:, bass.ds(n * T + tt, 1), :].rearrange("p a f -> p (a f)"),
                                        mean_var[:, tt, 0:1], rstd[:, tt:tt + 1], ALU.subtract, ALU.mult).then_inc(xhat_made, 1)

        def take_qk(f, tt):
            dve.wait_ge(qk_mm, T * f + tt + 1)
            ge(dve, sq_made, T * f)
            nc.vector.tensor_tensor(qk[:, tt, :], ps[:, tt, :], bias_qk[:], ALU.add).then_inc(qk_out, 1)

        def unit_qk(f):
            dve.wait_ge(sq_made, T * (f + 1))
            nc.vector.tensor_reduce(sum_sq[:], squares[:].rearrange("p t (h d) -> p (t h) d", d=HD), AX_X,
                                    ALU.add).then_inc(ss_made, 1)
            count = [0]
            STEPS = 14

            def link(ins):
                count[0] += 1
                ins.then_inc(root_step, 1)
                dve.wait_ge(root_step, f * STEPS + count[0])

            dve.wait_ge(ss_made, f + 1)
            link(nc.vector.tensor_scalar(sum_sq[:], sum_sq[:], NORM_EPS2, None, ALU.max))
            nc.vector.tensor_scalar(minus_half[:], sum_sq[:], -0.5, None, ALU.mult).then_inc(root_step, 1)
            count[0] += 1
            link(nc.vector.tensor_scalar(root[0][:].bitcast(I32), sum_sq[:].bitcast(I32), 1, None, ALU.arith_shift_right))
            link(nc.vector.tensor_scalar(root[1][:].bitcast(I32), root[0][:].bitcast(I32), -1.0, SEED, ALU.mult, ALU.add))
            for n in range(3):
                old, new = root[(n + 1) % 2], root[n % 2]
                link(nc.vector.tensor_tensor(root_sq[:], old[:], old[:], ALU.mult))
                link(nc.vector.tensor_tensor(root_err[:], root_sq[:], minus_half[:], ALU.mult))
                link(nc.vector.scalar_tensor_tensor(out=new[:], in0=root_err[:], scalar=1.5, in1=old[:], op0=ALU.add, op1=ALU.mult))
            norm = root[0]
            by = norm[:].rearrange("p (t w h) -> p t w h", t=T, w=2)
            link(nc.vector.tensor_tensor(by[:, :, 0, :], by[:, :, 0, :], head_scale[:].unsqueeze(1).broadcast_to([P, T, H]), ALU.mult))
            assert count[0] == STEPS
            ge(dve, qkt_mm, 2 * f)
            nc.vector.tensor_tensor(qkn[:].rearrange("p t (h d) -> p (t h) d", d=HD), qk[:].rearrange("p t (h d) -> p (t h) d", d=HD),
                                    norm[:].unsqueeze(2).broadcast_to([P, HH, HD]), ALU.mult).then_inc(qkn_made, 1)

        def maxima(b, s):
            if s == 0:
                ge(dve, m_mm, 2 * b)
            dve.wait_ge(s_mm, 8 * b + s + 1)
            hg, tt = s // 2, s % 2
            nc.vector.tensor_reduce(neg_max[:, tt, 4 * hg:4 * hg + 4],
                                    ps[:, 4:6, :].rearrange("p a (h n) -> p (a h) n", h=2), AX_X, ALU.max,
                                    negate=True).then_inc(max_made, 1)

        def rests(f):
            for w in range(2):
                dve.wait_ge(high_made, 2 * f + w + 1)
                ge(dve, low_made, 2 * f)
                nc.vector.tensor_tensor(rest[:, w, :], ps[:, w, :], parts[:, w, 0, :], ALU.subtract).then_inc(rest_made, 1)

        def divide(d):
            dve.wait_ge(otok_mm, d + 1)
            places = ps[:, 0:2, :].rearrange("p t (g d) -> p t g d", d=2 * HD)
            nc.vector.reciprocal(denom[:], places[:, :, :, HD]).then_inc(den_made, 1)
            dve.wait_ge(den_made, d + 1)
            ge(dve, ot_mm, d)
            for tt in range(T):
                nc.vector.tensor_tensor(o_tok[:, tt, :].rearrange("p (c h d) -> p h c d", c=C2, d=HD),
                                        places[:, tt, :, 0:HD].rearrange("p (h c) d -> p h c d", c=C2),
                                        denom[:, tt, :].rearrange("p (h c) -> p h c", c=C2).unsqueeze(3).broadcast_to([P, HT, C2, HD]),
                                        ALU.mult).then_inc(otok_made, 1)

        def gate(d):
            dve.wait_ge(proj_mm, d + 1)
            ge(dve, res_mm, d)
            for k in range(C2):
                nc.vector.tensor_scalar(projT[:, k, :], halves(ps, 1)[:, k, :], b_proj[:, k:k + 1], ada[:, k, bass.ds(d, 1)],
                                        ALU.add, ALU.mult).then_inc(proj_out, 1)

        def residual(d):
            dve.wait_ge(res_mm, d + 1)
            x = x_res[:, bass.ds(d * T, T), :].rearrange("p t f -> p (t f)")
            nc.vector.tensor_tensor(x, ps[:, 0, :], x, ALU.add).then_inc(res_made, 1)

        norm_stats(nc, x_res, 0, stats, stats_made)
        dve.wait_ge(stats_made, T)
        norm_moments(nc, stats, mean_var, mv_made)
        normalise(0)

        def turn(f, b, c, d, par):
            ahead = following(f)
            for s in range(SLOTS):
                if b is not None and s >= 2 and s != 5:
                    maxima(b, s - 2)
                if f is not None and s < 2:
                    take_qk(f, s)
                if ahead is not None and s == 1:
                    norm_stats(nc, x_res, ahead, stats, stats_made)
                if f is not None and s == 2:
                    if ahead is not None:
                        dve.wait_ge(stats_made, T * (f + 2))
                    unit_qk(f)
                    if ahead is not None:
                        norm_moments(nc, stats, mean_var, mv_made)
                if f is not None and s == 5:
                    rests(f)
                if b is not None and s == 5:
                    maxima(b, s - 2)
                if d is not None and s == 6:
                    divide(d)
                if ahead is not None and s == 7:
                    normalise(ahead)
                if d is not None and s == 8:
                    gate(d)
            if d is not None:
                residual(d)

        turns(turn, dve, 4)

    @block.tensor
    def _(pe):
        pe.wait_ge(g["late_weights"], g["LATE"])

        def norm_transposed(n, d):
            pe.wait_ge(xhat_made, T * (n + 1))
            if d is not None:
                pe.wait_ge(proj_out, C2 * (d + 1))
            else:
                ge(pe, rest_made, 2 * n)
            for tt in range(T):
                for k in range(C2):
                    mm = nc.tensor.transpose(halves(ps, 1)[:, k, tt * P:(tt + 1) * P], x_hat[:, tt, k * P:(k + 1) * P], ident[:])
            mm.then_inc(xt_mm, 1)

        def make_qk(f, par, tt):
            pe.wait_ge(x1_out, C2 * (f + 1))
            if tt == 0:
                ge(pe, res_made, f - 3)
                if isinstance(f, int):
                    ge(pe, rest_made, 2 * f)
            for k in range(C2):
                mm = nc.tensor.matmul(ps[:, tt, :], x1T[:, par, k, tt * P:(tt + 1) * P], w_qkv[:, k, 0:2 * F],
                                      start=(k == 0), stop=(k == C2 - 1))
            mm.then_inc(qk_mm, 1)

        def make_v(b, par, f):
            if f is not None:
                pe.wait_ge(qk_out, T * f + 1)
            else:
                ge(pe, res_made, b - 2)
            for tt in range(T):
                for k in range(C2):
                    mm = nc.tensor.matmul(halves(ps, 0)[:, tt, :], x1T[:, par, k, tt * P:(tt + 1) * P], w_qkv[:, k, 2 * F:3 * F],
                                          start=(k == 0), stop=(k == C2 - 1))
            mm.then_inc(v_mm, 1)

        def row_scores(b, par, s):
            if s == 0:
                pe.wait_ge(stack_in, 9 * 16 * (b + 1))
                ge(pe, m_out, 2 * b)
            ge(pe, max_made, 8 * b + s)
            hg, tt = s // 2, s % 2
            for j in range(4):
                mm = nc.tensor.matmul(ps[:, 4 + j // 2, (j % 2) * N:(j % 2 + 1) * N],
                                      q_stack[0:KROWS, par, 4 * hg + j, tt * P:(tt + 1) * P], k_stack[0:KROWS, par, 4 * hg + j, :],
                                      start=True, stop=True)
            mm.then_inc(s_mm, 1)

        def max_transposed(b, i):
            pe.wait_ge(max_made, 8 * b + 4 * (i + 1))
            if i == 0:
                ge(pe, os_out, 2 * (b - 1))
            for tt in range(T):
                mm = nc.tensor.transpose(ps[0:HT, 3 + i, tt * P // 2:(tt + 1) * P // 2].bitcast(BF16),
                                         neg_max[:, tt, HT * i:HT * (i + 1)], ident_b[:])
            mm.then_inc(m_mm, 1)

        def split_qk(f):
            pe.wait_ge(qkn_made, f + 1)
            ge(pe, v_out, f)
            for w in range(2):
                for tt in range(T):
                    for k in range(C2):
                        mm = nc.tensor.transpose(halves(ps, w)[:, k, tt * P:(tt + 1) * P],
                                                 qkn[:, tt, w * F + k * P:w * F + (k + 1) * P], ident[:])
                mm.then_inc(qkt_mm, 1)

        def col_scores(c, par, s):
            if s % 4 == 0:
                pe.wait_ge(m_row_in[s // 4], 16 * (c + 1))
            ge(pe, exp_made, 8 * c + s)
            for j in range(2):
                place = 2 * s + j
                for kt in range(T):
                    mm = nc.tensor.matmul(ps[:, 6 + j, kt * N:(kt + 1) * N], k_stack[:, par, place, kt * P:(kt + 1) * P],
                                          q_stack[:, par, place, :], start=True, stop=True)
            mm.then_inc(st_mm, 1)

        def values(c, par, hg, b):
            if hg == 0:
                ge(pe, os_out, 2 * c - 1)
            if hg == 2:
                ge(pe, os_out, 2 * c)
                if b is not None:
                    pe.wait_ge(m_out, 2 * b + 1)
            pe.wait_ge(exp_made, 8 * c + 2 * hg + 2)
            for kt in range(T):
                for j in range(4):
                    place = 4 * hg + j
                    mm = nc.tensor.matmul(halves(ps, 2 + hg // 2)[32 * j:32 * j + 32, hg % 2, :],
                                          v_ones[:, par, kt, HT * (place % 2) + place // 2, :],
                                          probsT[:, (2 * hg + j // 2) % 4, (j % 2) * 2 * N + kt * N:(j % 2) * 2 * N + (kt + 1) * N],
                                          start=(kt == 0), stop=(kt == T - 1))
            mm.then_inc(pv_mm, 1)

        def output_tokens(d, f):
            pe.wait_ge(os_out, 2 * (d + 1))
            if f is not None:
                pe.wait_ge(rest_made, 2 * (f + 1))
            else:
                pe.wait_ge(v_out, B)
                ge(pe, res_made, d)
                ge(pe, proj_out, C2 * d)
            for tt in range(T):
                for hg in range(4):
                    o = (hg % 2) * N + tt * P
                    mm = nc.tensor.transpose(ps[:, tt, hg * P:(hg + 1) * P], o_sumsT[:, hg // 2, o:o + P], ident[:])
            mm.then_inc(otok_mm, 1)

        def output_channels(d):
            pe.wait_ge(otok_made, T * (d + 1))
            for tt in range(T):
                for k in range(C2):
                    mm = nc.tensor.transpose(halves(ps, 0)[:, k, tt * P:(tt + 1) * P], o_tok[:, tt, k * P:(k + 1) * P], ident[:])
            mm.then_inc(ot_mm, 1)

        def project(d):
            pe.wait_ge(ot_out, C2 * (d + 1))
            for m in range(C2):
                for k in range(C2):
                    mm = nc.tensor.matmul(halves(ps, 1)[:, m, :], w_proj[:, k, m * P:(m + 1) * P], oT[:, k, :],
                                          start=(k == 0), stop=(k == C2 - 1))
            mm.then_inc(proj_mm, 1)

        def residual(d):
            pe.wait_ge(proj_out, C2 * (d + 1))
            for tt in range(T):
                for k in range(C2):
                    mm = nc.tensor.transpose(ps[:, 0, (C2 * tt + k) * P:(C2 * tt + k + 1) * P], projT[:, k, tt * P:(tt + 1) * P],
                                             ident[:])
            mm.then_inc(res_mm, 1)

        def turn(f, b, c, d, par):
            for s in range(SLOTS):
                if c is not None and s < 8:
                    col_scores(c, par, s)
                if b is not None and s >= 2:
                    row_scores(b, 1 - par, s - 2)
                if f is not None and s < 2:
                    make_qk(f, par, s)
                if b is not None and s == 2:
                    make_v(b, 1 - par, f)
                if f is not None and s == 4:
                    split_qk(f)
                if b is not None and s == 6:
                    max_transposed(b, 0)
                if d is not None and s == 6:
                    output_tokens(d, f)
                if d is not None and s == 7:
                    output_channels(d)
                if c is not None and s % 2 == 1 and s > 1:
                    values(c, par, s // 2 - 1, b)
                if d is not None and s == 8:
                    project(d)
                if d is not None and s == 9:
                    residual(d)
                if following(f) is not None and s == 9:
                    norm_transposed(following(f), d)
            if b is not None:
                max_transposed(b, 1)

        norm_transposed(0, None)
        turns(turn, pe, 4)


def ffn_block(nc, scope, t, alloc, sems, ps, g):
    x_res, ident, ada = g["x_res"], g["ident"], g["ada"]
    w_fc1, w_fc2, b_fc1, b_fc2 = g["w_fc1"], g["w_fc2"], g["b_fc1"], g["b_fc2"]
    DT = DFF // P
    stats = alloc(scope, "stats_f", [P, T, 6])
    mean_var = alloc(scope, "mean_var_f", [P, T, 2])
    var_eps = alloc(scope, "var_eps_f", [P, T])
    rstd = alloc(scope, "rstd_f", [P, T])
    x_hat = alloc(scope, "x_hat_f", [P, T, F])
    x2T = alloc(scope, "x2T", [P, C2, N])
    hidden = alloc(scope, "hidden", [P, 2, DT, N])
    outT = alloc(scope, "outT_f", [P, C2, N])
    result = alloc(scope, "result", [P, 2, T * F])
    (stats_made, mv_made, eps_made, rstd_made, xhat_made, xt_mm, x2_out, fc1_mm, gelu_made, fc2_mm, outT_made, out_mm,
     result_made) = sems(
        scope, "stats_made_f", "mv_made_f", "eps_made_f", "rstd_made_f", "xhat_made_f", "xt_mm_f", "x2_out", "fc1_mm",
        "gelu_made", "fc2_mm", "outT_made_f", "out_mm_f", "result_made")
    stored = sems(scope, "stored_even", "stored_odd")
    block = scope.enter_context(nc.Block())

    @block.sync
    def _(sp):
        def turn(f, b, c, par):
            if c is not None:
                sp.wait_ge(result_made, c + 1)
                sp.dma_start(t["out"][bass.ds(c * N, N), :].rearrange("(t p) f -> p t f", p=P),
                             result[:, par, :].rearrange("p (t f) -> p t f", t=T)).then_inc(stored[par], 16)

        turns(turn, sp, 3)
        for par in range(2):
            sp.wait_ge(stored[par], 16 * (B // 2))

    @block.gpsimd
    def _(pool):
        norm_root(pool, nc, 0, mean_var, g, var_eps, rstd, mv_made, eps_made, rstd_made)

        def turn(f, b, c, par):
            if following(f) is not None:
                norm_root(pool, nc, following(f), mean_var, g, var_eps, rstd, mv_made, eps_made, rstd_made)

        turns(turn, pool, 3)

    @block.scalar
    def _(act):
        def shift_scale(n):
            act.wait_ge(xt_mm, n + 1)
            ge(act, fc1_mm, DT // 2 * n)
            for k in range(C2):
                nc.scalar.activation(x2T[:, k, :], halves(ps, 0)[:, k, :], ACT.Identity, bias=ada[:, 5 * C2 + k, bass.ds(n, 1)],
                                     scale=ada[:, 3 * C2 + k, bass.ds(n, 1)]).then_inc(x2_out, 1)

        def turn(f, b, c, par):
            if f is None:
                return
            ge(act, fc2_mm, f - 1)
            for m in range(DT):
                if m == DT - 2 and following(f) is not None:
                    shift_scale(following(f))
                if m % 2 == 0:
                    act.wait_ge(fc1_mm, DT // 2 * f + m // 2 + 1)
                nc.scalar.activation(hidden[:, par, m, :], halves(ps, 1 + m // 2)[:, m % 2, :], ACT.Gelu,
                                     bias=b_fc1[:, m:m + 1]).then_inc(gelu_made, 1)

        shift_scale(0)
        turns(turn, act, 3)

    @block.vector
    def _(dve):
        def normalise(n):
            dve.wait_ge(rstd_made, n + 1)
            ge(dve, xt_mm, n)
            for tt in range(T):
                nc.vector.tensor_scalar(x_hat[:, tt, :], x_res[:, bass.ds(n * T + tt, 1), :].rearrange("p a f -> p (a f)"),
                                        mean_var[:, tt, 0:1], rstd[:, tt:tt + 1], ALU.subtract, ALU.mult).then_inc(xhat_made, 1)

        def turn(f, b, c, par):
            ahead = following(f)
            if ahead is not None:
                norm_stats(nc, x_res, ahead, stats, stats_made)
                dve.wait_ge(stats_made, T * (f + 2))
            if c is not None:
                dve.wait_ge(fc2_mm, c + 1)
                ge(dve, out_mm, c)
                for k in range(C2):
                    nc.vector.tensor_scalar(outT[:, k, :], halves(ps, 5)[:, k, :], b_fc2[:, k:k + 1],
                                            ada[:, C2 + k, bass.ds(c, 1)], ALU.add, ALU.mult).then_inc(outT_made, 1)
            if ahead is not None:
                norm_moments(nc, stats, mean_var, mv_made)
            if c is not None:
                dve.wait_ge(out_mm, c + 1)
                ge(dve, stored[par], loads(c, par) - 16)
                nc.vector.tensor_tensor(result[:, par, :], ps[:, 6, :],
                                        x_res[:, bass.ds(c * T, T), :].rearrange("p t f -> p (t f)"), ALU.add).then_inc(result_made, 1)
            if ahead is not None:
                normalise(ahead)

        norm_stats(nc, x_res, 0, stats, stats_made)
        dve.wait_ge(stats_made, T)
        norm_moments(nc, stats, mean_var, mv_made)
        normalise(0)
        turns(turn, dve, 3)

    @block.tensor
    def _(pe):
        def norm_transposed(n):
            pe.wait_ge(xhat_made, T * (n + 1))
            ge(pe, x2_out, C2 * n)
            for tt in range(T):
                for k in range(C2):
                    mm = nc.tensor.transpose(halves(ps, 0)[:, k, tt * P:(tt + 1) * P], x_hat[:, tt, k * P:(k + 1) * P], ident[:])
            mm.then_inc(xt_mm, 1)

        def hidden_of(f, m):
            if m == 0:
                pe.wait_ge(x2_out, C2 * (f + 1))
            if m % 2 == 0:
                ge(pe, gelu_made, DT * (f - 1) + m + 2)
            for k in range(C2):
                mm = nc.tensor.matmul(halves(ps, 1 + m // 2)[:, m % 2, :], w_fc1[:, k, m * P:(m + 1) * P], x2T[:, k, :],
                                      start=(k == 0), stop=(k == C2 - 1))
            if m % 2 == 1:
                mm.then_inc(fc1_mm, 1)

        def output(b, par):
            pe.wait_ge(gelu_made, DT * (b + 1))
            ge(pe, outT_made, C2 * b)
            for k in range(C2):
                for m in range(DT):
                    mm = nc.tensor.matmul(halves(ps, 5)[:, k, :], w_fc2[:, m, k * P:(k + 1) * P], hidden[:, par, m, :],
                                          start=(m == 0), stop=(m == DT - 1))
            mm.then_inc(fc2_mm, 1)

        def back_to_tokens(c):
            pe.wait_ge(outT_made, C2 * (c + 1))
            ge(pe, result_made, c)
            for tt in range(T):
                for k in range(C2):
                    mm = nc.tensor.transpose(ps[:, 6, (C2 * tt + k) * P:(C2 * tt + k + 1) * P], outT[:, k, tt * P:(tt + 1) * P],
                                             ident[:])
            mm.then_inc(out_mm, 1)

        def turn(f, b, c, par):
            for m in range(DT):
                if f is not None:
                    hidden_of(f, m)
                if c is not None and m == 3:
                    back_to_tokens(c)
            if following(f) is not None:
                norm_transposed(following(f))
            if b is not None:
                output(b, 1 - par)

        norm_transposed(0)
        turns(turn, pe, 3)


def kernel(x, cond_1024, mask_BxSxSx11_ik0, L0_cond_W_self, L0_cond_b_self, L0_cond_w_bias, L0_cond_b_bias, L0_cond_Wq,
           L0_cond_bq, L0_cond_Wk, L0_cond_bk, L0_cond_Wout, L0_cond_bout, L1_cond_mat_qkv_w, L1_cond_q_bias,
           L1_cond_v_bias, L1_cond_scale_mul, L1_cond_proj_w, L1_cond_proj_b, L1_cond_ada_w, L1_cond_ada_b, L1_cond_fc1_w,
           L1_cond_fc1_b, L1_cond_fc2_w, L1_cond_fc2_b):
    import numpy as np
    import concourse.bacc as bacc
    from concourse.bass_utils import run_bass_kernel_spmd

    def columns(a):
        a = np.asarray(a)
        return np.moveaxis(a.reshape(*a.shape[:-1], a.shape[-1] // P, P), -1, 0)

    flat = np.asarray(x).reshape(B * N, F)
    mask = np.asarray(mask_BxSxSx11_ik0)
    adj = np.stack([mask[:, :, :M, :], np.swapaxes(mask[:, :M, :, :], 1, 2)], axis=2)
    arrays = {
        "x": flat, "xT": flat.T, "adj": adj.reshape(B * N, 2 * M * L), "condT": np.asarray(cond_1024).T,
        "w_selfT": np.asarray(L0_cond_W_self).T, "b_self": columns(L0_cond_b_self),
        "w_label": L0_cond_w_bias, "b_label": np.asarray(L0_cond_b_bias).reshape(1),
        "w_qT": np.swapaxes(L0_cond_Wq, 1, 2), "b_q": columns(L0_cond_bq), "w_kT": np.swapaxes(L0_cond_Wk, 1, 2), "b_k": columns(L0_cond_bk),
        "w_oT": np.swapaxes(np.asarray(L0_cond_Wout).reshape(2, F, F), 1, 2), "b_out": columns(L0_cond_bout),
        "w_qkvT": np.asarray(L1_cond_mat_qkv_w).T, "b_qkv_q": L1_cond_q_bias, "b_v": columns(L1_cond_v_bias),
        "scale_mul": np.asarray(L1_cond_scale_mul).reshape(H), "w_projT": np.asarray(L1_cond_proj_w).T,
        "b_proj": columns(L1_cond_proj_b), "w_adaT": np.asarray(L1_cond_ada_w).T, "b_ada": columns(L1_cond_ada_b),
        "w_fc1T": np.asarray(L1_cond_fc1_w).T, "b_fc1": columns(L1_cond_fc1_b), "w_fc2T": np.asarray(L1_cond_fc2_w).T,
        "b_fc2": columns(L1_cond_fc2_b),
    }
    nc = bacc.Bacc("TRN2", target_bir_lowering=False, num_devices=1)
    sent, tensors = {}, {}
    for name, a in arrays.items():
        a = np.ascontiguousarray(a)
        sent[f"in_{name}"] = a
        tensors[name] = nc.dram_tensor(f"in_{name}", a.shape, mybir.dt.from_np(a.dtype), kind="ExternalInput").ap()
    tensors["out"] = nc.dram_tensor("out_x", (B * N, F), F32, kind="ExternalOutput").ap()
    build(nc, tensors)
    ran = run_bass_kernel_spmd(nc, [sent], core_ids=[0])
    return ran.results[0]["out_x"].reshape(B, N, F)
```

```python
from contextlib import ExitStack

import concourse.bass as bass
from concourse import mybir
from concourse.alu_op_type import AluOpType as ALU

F32 = mybir.dt.float32
BF16 = mybir.dt.bfloat16
F32R = mybir.dt.float32r
I32 = mybir.dt.int32
ACT = mybir.ActivationFunctionType
AX_X = mybir.AxisListType.X

P = 128
B, N, F = 16, 256, 256
T = N // P
C2 = F // P
H, HD = 16, 16
HT = P // HD
M, L = 20, 11
G4 = 4 * M
DFF = 1024
NEG = -9000000000000000.0
LN_EPS = 1e-06
NORM_EPS2 = 1e-24
MAX_SCALE_MUL = 4.605170185988092
LOW_BITS = 12
SEED = 1597463007.0
SLOT = 16
NSLOT = 6
KROWS = NSLOT * SLOT
Q_PARTS = (0, 0, 0, 1, 1, 2)
K_PARTS = (0, 1, 2, 0, 1, 0)


def ge(eng, sem, value):
    if not isinstance(value, int) or value > 0:
        eng.wait_ge(sem, value)


def turns(turn, eng, stages):
    def peeled(i):
        turn(*(i - back if 0 <= i - back < B else None for back in range(stages)), i % 2)

    for i in range(5):
        peeled(i)
    with eng.Fori(0, (B - 6) // 2) as i:
        turn(*(i * 2 + 5 - back for back in range(stages)), 1)
        turn(*(i * 2 + 6 - back for back in range(stages)), 0)
    for i in range(B - 1, B + stages - 1):
        peeled(i)


def loads(b, par):
    return (b - par) * 8 + 16


def following(f):
    return None if f is None or (isinstance(f, int) and f == B - 1) else f + 1


def build(nc, t):
    with ExitStack() as top:
        def alloc(scope, name, shape, dt=F32):
            return scope.enter_context(nc.sbuf_tensor(name, shape, dt))

        def sems(scope, *names):
            return [scope.enter_context(nc.semaphore(n)) for n in names]

        ps = top.enter_context(nc.psum_tensor("ps", [P, 8, 512], F32))

        x_res = alloc(top, "x_res", [P, B * T, F])
        ident = alloc(top, "ident", [P, P])
        ident_b = alloc(top, "ident_b", [P, P], BF16)
        ones = alloc(top, "ones", [P, P])
        neg_half = alloc(top, "neg_half", [P, T])
        ln_eps = alloc(top, "ln_eps", [P, T])
        zero = alloc(top, "zero", [P, 1])
        head_of_row = alloc(top, "head_of_row", [P, HT])
        w_qkv = alloc(top, "w_qkv", [P, C2, 3 * F])
        w_proj = alloc(top, "w_proj", [P, C2, F])
        w_fc1 = alloc(top, "w_fc1", [P, C2, DFF])
        w_fc2 = alloc(top, "w_fc2", [P, DFF // P, F])
        ada = alloc(top, "ada", [P, 6 * C2, B])
        bias_qk = alloc(top, "bias_qk", [P, 2 * F])
        b_v = alloc(top, "b_v", [P, C2])
        b_proj = alloc(top, "b_proj", [P, C2])
        b_fc1 = alloc(top, "b_fc1", [P, DFF // P])
        b_fc2 = alloc(top, "b_fc2", [P, C2])
        head_scale = alloc(top, "head_scale", [P, H])
        late_weights, = sems(top, "late_weights")
        LATE = 9 * 16

        with ExitStack() as graph:
            w_x = alloc(graph, "w_x", [P, C2, F])
            w_q = alloc(graph, "w_q", [P, 2, C2, F])
            b_self = alloc(graph, "b_self", [P, C2])
            b_q = alloc(graph, "b_q", [P, 2, C2])
            b_out = alloc(graph, "b_out", [P, 2, C2])
            b_out_sum = alloc(graph, "b_out_sum", [P, C2])
            w_label = alloc(graph, "w_label", [P, L])
            b_label = alloc(graph, "b_label", [P, 1])
            q_cond = alloc(graph, "q_cond", [P, C2, B])
            k_all = alloc(graph, "k_all", [P, 2 * C2, B * M])
            v_all = alloc(graph, "v_all", [P, 2 * C2, B * M])

            xT = alloc(graph, "xT", [P, 2, C2, N])
            adj = alloc(graph, "adj", [P, 2, T * 2 * M * L], I32)
            xT_in, adj_in = (sems(graph, f"{n}_even", f"{n}_odd") for n in ("xT_in", "adj_in"))

            with ExitStack() as setup:
                w_c = alloc(setup, "w_c", [P, C2, F])
                w_k = alloc(setup, "w_k", [P, 2, C2, F])
                w_o = alloc(setup, "w_o", [P, 2, C2, F])
                b_k = alloc(setup, "b_k", [P, 2, C2])
                w_ada = alloc(setup, "w_ada", [P, C2, 6 * F])
                b_ada = alloc(setup, "b_ada", [P, 6 * C2])
                condT = alloc(setup, "condT", [P, C2, B])
                silu = alloc(setup, "silu", [P, C2, B])
                exp_neg = alloc(setup, "exp_neg", [P, C2, B])
                sig = alloc(setup, "sig", [P, C2, B])
                x20 = alloc(setup, "x20", [P, C2, B * M])
                nz20 = alloc(setup, "nz20", [P, B * M])
                cond20 = alloc(setup, "cond20", [P, C2, B * M])
                feat20 = alloc(setup, "feat20", [P, C2, B * M])
                scale_in = alloc(setup, "scale_in", [P, H])
                (consts_set, first_in, ada_in, kv_in, small_in, exp_made, sig_made, silu_made, cond_mm,
                 cond_out, sum20_mm, nz_made, cond20_made, feat20_mm, feat20_made, kv_mm, kv_out,
                 ada_mm, ada_out, chain) = sems(
                    setup, "consts_set", "first_in", "ada_in", "kv_in", "small_in", "exp_made", "sig_made",
                    "silu_made", "cond_mm", "cond_out", "sum20_mm", "nz_made", "cond20_made",
                    "feat20_mm", "feat20_made", "kv_mm", "kv_out", "ada_mm", "ada_out", "setup_chain")
                block = setup.enter_context(nc.Block())

                @block.sync
                def _(sp):
                    sp.dma_start(condT[:], t["condT"].rearrange("(k p) b -> p k b", p=P)).then_inc(first_in, 16)
                    sp.dma_start(w_c[:], t["w_selfT"][F:2 * F, :].rearrange("(k p) n -> p k n", p=P)).then_inc(first_in, 16)
                    sp.dma_start(w_x[:], t["w_selfT"][0:F, :].rearrange("(k p) n -> p k n", p=P)).then_inc(first_in, 16)
                    for k in range(C2):
                        sp.dma_start(x20[:, k, :].rearrange("p (b m) -> p b m", m=M),
                                     t["xT"][k * P:(k + 1) * P, :].rearrange("p (b n) -> p b n", b=B)[:, :, 0:M]
                                     ).then_inc(first_in, 16)
                    sp.dma_start(w_k[:], t["w_kT"].rearrange("d (k p) n -> p d k n", p=P)).then_inc(kv_in, 16)
                    sp.dma_start(w_o[:], t["w_oT"].rearrange("d (k p) n -> p d k n", p=P)).then_inc(kv_in, 16)
                    sp.dma_start(w_q[:], t["w_qT"].rearrange("d (k p) n -> p d k n", p=P)).then_inc(kv_in, 16)
                    sp.dma_start(w_ada[:], t["w_adaT"].rearrange("(k p) n -> p k n", p=P)).then_inc(ada_in, 16)
                    sp.dma_start(xT[:, 0], t["xT"][:, 0:N].rearrange("(k p) n -> p k n", p=P)).then_inc(xT_in[0], 16)
                    sp.dma_start(adj[:, 0].rearrange("p (t e) -> p t e", t=T),
                                 t["adj"][0:N, :].rearrange("(t p) e -> p t e", p=P)).then_inc(adj_in[0], 16)
                    sp.wait_ge(kv_in, 48)
                    sp.wait_ge(small_in, 9 * 16)

                @block.gpsimd
                def _(pool):
                    nc.gpsimd.memset(ident[:], 0.0).then_inc(chain, 1)
                    nc.gpsimd.memset(head_of_row[:], 1.0).then_inc(chain, 1)
                    nc.gpsimd.memset(ones[:], 1.0).then_inc(consts_set, 1)
                    nc.gpsimd.memset(neg_half[:], -0.5).then_inc(consts_set, 1)
                    nc.gpsimd.memset(ln_eps[:], LN_EPS).then_inc(consts_set, 1)
                    nc.gpsimd.memset(zero[:], 0.0).then_inc(consts_set, 1)
                    pool.wait_ge(chain, 2)
                    nc.gpsimd.affine_select(out=ident[:], in_=ident[:], compare_op=ALU.not_equal, fill=1.0, base=0,
                                            pattern=[[-1, P]], channel_multiplier=1).then_inc(consts_set, 1)
                    nc.gpsimd.affine_select(out=head_of_row[:], in_=head_of_row[:], compare_op=ALU.is_ge, fill=0.0,
                                            base=0, pattern=[[-HD, HT]], channel_multiplier=1).then_inc(chain, 1)
                    pool.wait_ge(chain, 3)
                    nc.gpsimd.affine_select(out=head_of_row[:], in_=head_of_row[:], compare_op=ALU.is_ge, fill=0.0,
                                            base=HD - 1, pattern=[[HD, HT]], channel_multiplier=-1).then_inc(consts_set, 1)
                    pool.wait_ge(consts_set, 5)
                    nc.gpsimd.tensor_copy(ident_b[:], ident[:]).then_inc(consts_set, 1)

                @block.scalar
                def _(act):
                    for dst, src in ((b_self, t["b_self"]), (b_ada, t["b_ada"])):
                        act.dma_start(dst[:], src).then_inc(small_in, 16)
                    for dst, src in ((b_k, t["b_k"]), (b_q, t["b_q"]), (b_out, t["b_out"])):
                        act.dma_start(dst[:], src).then_inc(small_in, 16)
                    act.dma_start(w_label[:], t["w_label"].partition_broadcast(P)).then_inc(small_in, 16)
                    act.dma_start(b_label[:], t["b_label"].partition_broadcast(P)).then_inc(small_in, 16)
                    act.dma_start(scale_in[:], t["scale_mul"].partition_broadcast(P)).then_inc(small_in, 16)
                    act.dma_start(bias_qk[:, 0:F], t["b_qkv_q"].partition_broadcast(P)).then_inc(small_in, 16)
                    act.wait_ge(first_in, 80)
                    nc.scalar.activation(exp_neg[:], condT[:], ACT.Exp, scale=-1.0).then_inc(exp_made, 1)
                    for dst, src in ((w_qkv, t["w_qkvT"]), (w_proj, t["w_projT"]), (w_fc1, t["w_fc1T"]),
                                     (w_fc2, t["w_fc2T"])):
                        act.dma_start(dst[:], src.rearrange("(k p) n -> p k n", p=P)).then_inc(late_weights, 16)
                    for dst, src in ((b_v, t["b_v"]), (b_proj, t["b_proj"]), (b_fc1, t["b_fc1"]), (b_fc2, t["b_fc2"])):
                        act.dma_start(dst[:], src).then_inc(late_weights, 16)
                    act.wait_ge(small_in, 9 * 16)
                    act.wait_ge(chain, 4)
                    nc.scalar.activation(head_scale[:], scale_in[:], ACT.Exp).then_inc(exp_made, 1)
                    for c in range(2 * C2):
                        act.wait_ge(kv_mm, 2 * c + 1)
                        nc.scalar.activation(k_all[:, c, :], ps[:, 4, 0:B * M], ACT.Identity,
                                             bias=b_k[:, c // C2, c % C2:c % C2 + 1]).then_inc(kv_out, 1)
                        act.wait_ge(kv_mm, 2 * c + 2)
                        nc.scalar.activation(v_all[:, c, :], ps[:, 5, 0:B * M], ACT.Copy).then_inc(kv_out, 1)

                @block.vector
                def _(dve):
                    nc.vector.memset(bias_qk[:, F:2 * F], 0.0).then_inc(late_weights, 16)
                    dve.wait_ge(small_in, 9 * 16)
                    dve.wait_ge(chain, 3)
                    nc.vector.tensor_scalar(scale_in[:], scale_in[:], MAX_SCALE_MUL, None, ALU.min).then_inc(chain, 1)
                    nc.vector.tensor_scalar(b_q[:], b_q[:], float(HD) ** -0.5, None, ALU.mult).then_inc(chain, 1)
                    nc.vector.tensor_tensor(b_out_sum[:], b_out[:, 0, :], b_out[:, 1, :], ALU.add).then_inc(chain, 1)
                    dve.wait_ge(exp_made, 1)
                    nc.vector.tensor_scalar(sig[:], exp_neg[:], 1.0, None, ALU.add).then_inc(sig_made, 1)
                    dve.wait_ge(sig_made, 1)
                    nc.vector.reciprocal(sig[:], sig[:]).then_inc(sig_made, 1)
                    dve.wait_ge(sig_made, 2)
                    nc.vector.tensor_tensor(silu[:], condT[:], sig[:], ALU.mult).then_inc(silu_made, 1)
                    dve.wait_ge(cond_mm, 1)
                    nc.vector.tensor_copy(q_cond[:], ps[:, 0, 0:C2 * B].rearrange("p (k b) -> p k b", b=B)).then_inc(cond_out, 1)
                    dve.wait_ge(sum20_mm, 1)
                    nc.vector.tensor_scalar(nz20[:], ps[:, 1, 0:B * M], 0.0, None, ALU.not_equal).then_inc(nz_made, 1)
                    dve.wait_ge(nz_made, 1)
                    dve.wait_ge(cond_out, 1)
                    for k in range(C2):
                        nc.vector.tensor_tensor(cond20[:, k, :].rearrange("p (b m) -> p b m", m=M),
                                                nz20[:].rearrange("p (b m) -> p b m", m=M),
                                                q_cond[:, k, :].unsqueeze(2).broadcast_to([P, B, M]), ALU.mult).then_inc(cond20_made, 1)
                    dve.wait_ge(cond20_made, C2)
                    dve.wait_ge(feat20_mm, 1)
                    for k in range(C2):
                        nc.vector.scalar_tensor_tensor(out=feat20[:, k, :], in0=ps[:, 2 + k, 0:B * M], scalar=b_self[:, k:k + 1],
                                                       in1=cond20[:, k, :], op0=ALU.add, op1=ALU.add).then_inc(feat20_made, 1)
                    dve.wait_ge(ada_mm, 1)
                    for j in range(6 * C2):
                        scaled = 2 * C2 <= j < 4 * C2
                        nc.vector.tensor_scalar(ada[:, j, :], ps[:, 6, j * B:(j + 1) * B], b_ada[:, j:j + 1],
                                                1.0 if scaled else 0.0, ALU.add, ALU.add).then_inc(ada_out, 1)

                @block.tensor
                def _(pe):
                    pe.wait_ge(first_in, 80)
                    for f in range(C2):
                        for k in range(C2):
                            mm = nc.tensor.matmul(ps[:, 0, f * B:(f + 1) * B], w_c[:, k, f * P:(f + 1) * P], condT[:, k, :],
                                                  start=(k == 0), stop=(k == C2 - 1))
                    mm.then_inc(cond_mm, 1)
                    pe.wait_ge(consts_set, 7)
                    for k in range(C2):
                        mm = nc.tensor.matmul(ps[:, 1, 0:B * M], ones[:], x20[:, k, :], start=(k == 0), stop=(k == C2 - 1))
                    mm.then_inc(sum20_mm, 1)
                    for f in range(C2):
                        for k in range(C2):
                            mm = nc.tensor.matmul(ps[:, 2 + f, 0:B * M], w_x[:, k, f * P:(f + 1) * P], x20[:, k, :],
                                                  start=(k == 0), stop=(k == C2 - 1))
                    mm.then_inc(feat20_mm, 1)
                    pe.wait_ge(kv_in, 48)
                    pe.wait_ge(feat20_made, C2)
                    for c in range(2 * C2):
                        d, f = c // C2, c % C2
                        for bank, w in ((4, w_k), (5, w_o)):
                            ge(pe, kv_out, 2 * c + bank - 5)
                            for k in range(C2):
                                mm = nc.tensor.matmul(ps[:, bank, 0:B * M], w[:, d, k, f * P:(f + 1) * P], feat20[:, k, :],
                                                      start=(k == 0), stop=(k == C2 - 1))
                            mm.then_inc(kv_mm, 1)
                    pe.wait_ge(ada_in, 16)
                    pe.wait_ge(silu_made, 1)
                    for j in range(6 * C2):
                        for k in range(C2):
                            mm = nc.tensor.matmul(ps[:, 6, j * B:(j + 1) * B], w_ada[:, k, j * P:(j + 1) * P], silu[:, k, :],
                                                  start=(k == 0), stop=(k == C2 - 1))
                    mm.then_inc(ada_mm, 1)

            graph_block(nc, graph, t, alloc, sems, ps, dict(
                x_res=x_res, ident=ident, ones=ones, head_of_row=head_of_row, w_x=w_x, w_q=w_q, b_self=b_self, b_q=b_q,
                b_out_sum=b_out_sum, w_label=w_label, b_label=b_label, q_cond=q_cond, k_all=k_all, v_all=v_all, xT=xT, adj=adj,
                xT_in=xT_in, adj_in=adj_in))

        with ExitStack() as attention:
            attention_block(nc, attention, t, alloc, sems, ps, dict(
                x_res=x_res, ident=ident, ident_b=ident_b, neg_half=neg_half, ln_eps=ln_eps, zero=zero, w_qkv=w_qkv, w_proj=w_proj, ada=ada,
                bias_qk=bias_qk, b_v=b_v, b_proj=b_proj, head_scale=head_scale, late_weights=late_weights, LATE=LATE))

        with ExitStack() as ffn:
            ffn_block(nc, ffn, t, alloc, sems, ps, dict(
                x_res=x_res, ident=ident, neg_half=neg_half, ln_eps=ln_eps, zero=zero, w_fc1=w_fc1, w_fc2=w_fc2, ada=ada, b_fc1=b_fc1, b_fc2=b_fc2))


def halves(ps, bank):
    return ps[:, bank, :].rearrange("p (a n) -> p a n", a=2)


def graph_block(nc, scope, t, alloc, sems, ps, g):
    x_res, ident, ones, head_of_row = g["x_res"], g["ident"], g["ones"], g["head_of_row"]
    w_x, w_q, b_self, b_q, b_out_sum = g["w_x"], g["w_q"], g["b_self"], g["b_q"], g["b_out_sum"]
    w_label, b_label, q_cond, k_all, v_all = g["w_label"], g["b_label"], g["q_cond"], g["k_all"], g["v_all"]
    E2 = T * 2 * M
    xT, adj, xT_in, adj_in = g["xT"], g["adj"], g["xT_in"], g["adj_in"]
    x_in = alloc(scope, "x_in", [P, 2, T, F])
    weighted = alloc(scope, "weighted", [P, E2 * L])
    count = alloc(scope, "count", [P, E2])
    no_edge = alloc(scope, "no_edge", [P, E2])
    label_bias = alloc(scope, "label_bias", [P, E2])
    edge_bias = alloc(scope, "edge_bias", [P, 2, T, 2, M])
    nz = alloc(scope, "nz", [P, N])
    cond = alloc(scope, "cond", [P, C2, N])
    qT = alloc(scope, "qT", [P, 2, 2, C2, N])
    k_blocks = alloc(scope, "k_blocks", [P, 2, 2 * C2, HT, M])
    v_masked = alloc(scope, "v_masked", [P, 2 * C2, HT, M])
    v_blocks = alloc(scope, "v_blocks", [G4, 2, H // 2, 64])
    scores = alloc(scope, "scores", [P, 2, 2, T, H, M])
    row_max = alloc(scope, "row_max", [P, 2, T, H])
    total = alloc(scope, "row_sum", [P, 2, T, H])
    inverse = alloc(scope, "row_inverse", [P, 2, T, H])
    weightT = alloc(scope, "weightT", [G4, 2, T, 4, P])
    outT = alloc(scope, "outT", [P, C2, N])
    x_arrived = sems(scope, "x_in_arrived_even", "x_in_arrived_odd")
    (sums_mm, nz_made, cond_made, feat_mm, feat_out, q_mm, q_out, kb_made, vm_made, vt_mm,
     vb_made, cnt_made, lab_w, lab_made, neg_made, edge_made, aff_mm, aff_out, max_made, shifted, exp_made,
     sum_made, rec_made, norm_made, wT_mm, wT_out, pv_mm, outT_made, out_mm, x_made) = sems(
        scope, "sums_mm", "nz_made_g", "cond_made", "feat_mm", "feat_out", "q_mm", "q_out",
        "kb_made", "vm_made", "vt_mm", "vb_made", "cnt_made", "lab_w", "lab_made", "neg_made", "edge_made",
        "aff_mm", "aff_out", "max_made", "shifted", "exp_made_g", "sum_made", "rec_made", "norm_made", "wT_mm", "wT_out",
        "pv_mm", "outT_made", "out_mm", "x_made")
    block = scope.enter_context(nc.Block())

    def feat_at(b):
        return x_res[:, bass.ds(b * T, T), :]

    @block.sync
    def _(sp):
        def turn(f, b, c, par):
            if f is not None and not (isinstance(f, int) and f == 0):
                ge(sp, feat_mm, f - 1)
                sp.dma_start(xT[:, par], t["xT"][:, bass.ds(f * N, N)].rearrange("(k p) n -> p k n", p=P)).then_inc(xT_in[par], 16)
                ge(sp, lab_w, f - 1)
                ge(sp, cnt_made, f - 1)
                sp.dma_start(adj[:, par].rearrange("p (t e) -> p t e", t=T),
                             t["adj"][bass.ds(f * N, N), :].rearrange("(t p) e -> p t e", p=P)).then_inc(adj_in[par], 16)
            if b is not None:
                ge(sp, x_made, b - 1)
                sp.dma_start(x_in[:, 1 - par], t["x"][bass.ds(b * N, N), :].rearrange("(t p) f -> p t f", p=P)
                             ).then_inc(x_arrived[1 - par], 16)

        turns(turn, sp, 3)

    @block.gpsimd
    def _(pool):
        own = head_of_row[:].unsqueeze(2).broadcast_to([P, HT, M])

        def shift(b, par, d):
            pool.wait_ge(max_made, 2 * b + d + 1)
            nc.gpsimd.tensor_tensor(scores[:, par, d], scores[:, par, d], row_max[:, d].unsqueeze(3).broadcast_to([P, T, H, M]),
                                    ALU.subtract).then_inc(shifted, 1)

        def normalise(b, par, d):
            pool.wait_ge(rec_made, 2 * b + d + 1)
            nc.gpsimd.tensor_tensor(scores[:, par, d], scores[:, par, d], inverse[:, d].unsqueeze(3).broadcast_to([P, T, H, M]),
                                    ALU.mult).then_inc(norm_made, 1)

        def turn(f, b, c, par):
            if b is not None:
                shift(b, 1 - par, 0)
            if f is not None:
                ge(pool, aff_mm, 2 * (f - 1))
                for k in range(2 * C2):
                    nc.gpsimd.tensor_tensor(k_blocks[:, par, k], k_all[:, k, bass.ds(f * M, M)].unsqueeze(1).broadcast_to([P, HT, M]),
                                            own, ALU.mult).then_inc(kb_made, 1)
            if b is not None:
                shift(b, 1 - par, 1)
            if f is not None:
                ge(pool, vt_mm, 2 * f)
                for k in range(2 * C2):
                    nc.gpsimd.tensor_tensor(v_masked[:, k], v_all[:, k, bass.ds(f * M, M)].unsqueeze(1).broadcast_to([P, HT, M]),
                                            own, ALU.mult).then_inc(vm_made, 1)
            if b is not None:
                normalise(b, 1 - par, 0)
                normalise(b, 1 - par, 1)

        turns(turn, pool, 3)

    @block.scalar
    def _(act):
        def exponentials(b, par, d):
            act.wait_ge(shifted, 2 * b + d + 1)
            nc.scalar.activation(scores[:, par, d], scores[:, par, d], ACT.Exp).then_inc(exp_made, 1)

        def take_queries(f, par, d):
            act.wait_ge(q_mm, 2 * f + d + 1)
            for k in range(C2):
                nc.scalar.activation(qT[:, par, d, k, :], halves(ps, 2 + d)[:, k, :], ACT.Identity,
                                     bias=b_q[:, d, k:k + 1], scale=float(HD) ** -0.5).then_inc(q_out, 1)

        def take_weights(c, d):
            act.wait_ge(wT_mm, 2 * c + d + 1)
            ge(act, pv_mm, c)
            nc.scalar.activation(weightT[:, d], ps[0:G4, 6:8, :].rearrange("p t (c n) -> p t c n", c=4),
                                 ACT.Copy).then_inc(wT_out, 1)

        def turn(f, b, c, par):
            if f is not None:
                act.wait_ge(nz_made, f + 1)
                ge(act, feat_out, f)
                for k in range(C2):
                    nc.scalar.activation(cond[:, k, :], nz[:], ACT.Identity, bias=b_self[:, k:k + 1],
                                         scale=q_cond[:, k, bass.ds(f, 1)]).then_inc(cond_made, 1)
            if c is not None:
                take_weights(c, 0)
                take_weights(c, 1)
            if f is not None:
                take_queries(f, par, 0)
            if b is not None:
                exponentials(b, 1 - par, 0)
                act.wait_ge(vt_mm, 2 * b + 2)
                ge(act, pv_mm, b - 1)
                nc.scalar.activation(v_blocks[:, 1 - par], ps[0:G4, 0, :].rearrange("p (c v) -> p c v", v=64),
                                     ACT.Copy).then_inc(vb_made, 1)
                exponentials(b, 1 - par, 1)
            if f is not None:
                ge(act, aff_mm, 2 * (f - 1))
                take_queries(f, par, 1)

        turns(turn, act, 3)

    @block.vector
    def _(dve):
        def raw_scores(b, par, d):
            dve.wait_ge(edge_made, b + 1)
            dve.wait_ge(aff_mm, 2 * b + d + 1)
            ge(dve, wT_mm, 2 * (b - 2) + d + 1)
            for tt in range(T):
                nc.vector.tensor_tensor(
                    scores[:, par, d, tt], ps[:, 4 + tt, 0:H * M].rearrange("p (h m) -> p h m", m=M),
                    edge_bias[:, par, tt, d, :].unsqueeze(1).broadcast_to([P, H, M]), ALU.add).then_inc(aff_out, 1)
            dve.wait_ge(aff_out, T * (2 * b + d + 1))
            nc.vector.tensor_reduce(row_max[:, d], scores[:, par, d], AX_X, ALU.max).then_inc(max_made, 1)

        def nonzero(f):
            dve.wait_ge(sums_mm, f + 1)
            ge(dve, cond_made, C2 * f)
            nc.vector.tensor_scalar(nz[:], halves(ps, 4)[:, 0, :], 0.0, None, ALU.not_equal).then_inc(nz_made, 1)

        def features(f):
            dve.wait_ge(feat_mm, f + 1)
            dve.wait_ge(cond_made, C2 * (f + 1))
            nc.vector.tensor_tensor(feat_at(f), halves(ps, 1), cond[:], ALU.add).then_inc(feat_out, 1)

        def label_products(f, par):
            dve.wait_ge(adj_in[par], loads(f, par))
            edges = adj[:, par].rearrange("p (e l) -> p e l", l=L)
            nc.vector.tensor_reduce(count[:], edges, AX_X, ALU.add).then_inc(cnt_made, 1)
            nc.vector.tensor_tensor(weighted[:].rearrange("p (e l) -> p e l", l=L), edges,
                                    w_label[:].unsqueeze(1).broadcast_to([P, E2, L]), ALU.mult).then_inc(lab_w, 1)

        def label_sums(f, par):
            dve.wait_ge(cnt_made, f + 1)
            nc.vector.tensor_scalar(no_edge[:], count[:], 0.0, NEG, ALU.is_le, ALU.mult).then_inc(neg_made, 1)
            dve.wait_ge(lab_w, f + 1)
            nc.vector.tensor_reduce(label_bias[:], weighted[:].rearrange("p (e l) -> p e l", l=L), AX_X,
                                    ALU.add).then_inc(lab_made, 1)

        def edge_biases(f, par):
            dve.wait_ge(neg_made, f + 1)
            dve.wait_ge(lab_made, f + 1)
            nc.vector.scalar_tensor_tensor(out=edge_bias[:, par].rearrange("p t d m -> p (t d m)"), in0=label_bias[:],
                                           scalar=b_label[:, 0:1], in1=no_edge[:], op0=ALU.add, op1=ALU.add).then_inc(edge_made, 1)

        def sums(b, par, d):
            dve.wait_ge(exp_made, 2 * b + d + 1)
            nc.vector.tensor_reduce(total[:, d], scores[:, par, d], AX_X, ALU.add).then_inc(sum_made, 1)
            dve.wait_ge(sum_made, 2 * b + d + 1)
            nc.vector.reciprocal(inverse[:, d], total[:, d]).then_inc(rec_made, 1)

        def take_output(c):
            dve.wait_ge(pv_mm, c + 1)
            ge(dve, out_mm, c)
            for k in range(C2):
                nc.vector.scalar_tensor_tensor(out=outT[:, k, :], in0=halves(ps, 1)[:, k, :], scalar=b_out_sum[:, k:k + 1],
                                               in1=feat_at(c)[:, k, :], op0=ALU.add, op1=ALU.add).then_inc(outT_made, 1)

        def residual(c, par):
            dve.wait_ge(out_mm, c + 1)
            dve.wait_ge(x_arrived[par], loads(c, par))
            dve.wait_ge(outT_made, C2 * (c + 1))
            nc.vector.scalar_tensor_tensor(
                out=x_res[:, bass.ds(c * T, T), :].rearrange("p t f -> p (t f)"), in0=ps[:, 0, :], scalar=0.0,
                in1=x_in[:, par].rearrange("p t f -> p (t f)"), op0=ALU.max, op1=ALU.add).then_inc(x_made, 1)

        def turn(f, b, c, par):
            if f is not None:
                nonzero(f)
                features(f)
            if b is not None:
                raw_scores(b, 1 - par, 0)
            if f is not None:
                label_products(f, par)
            if b is not None:
                raw_scores(b, 1 - par, 1)
            if c is not None:
                take_output(c)
            if b is not None:
                sums(b, 1 - par, 0)
            if f is not None:
                label_sums(f, par)
            if b is not None:
                sums(b, 1 - par, 1)
            if f is not None:
                edge_biases(f, par)
            if c is not None:
                residual(c, par)

        turns(turn, dve, 3)

    @block.tensor
    def _(pe):
        def raw_scores(b, par, d):
            pe.wait_ge(q_out, 4 * b + 2 * d + 2)
            pe.wait_ge(kb_made, 2 * C2 * (b + 1))
            ge(pe, aff_out, T * (2 * b + d))
            if d == 0:
                pe.wait_ge(nz_made, B if following(b) is None else b + 2)
                pe.wait_ge(vm_made, 2 * C2 * (b + 1))
                ge(pe, x_made, b - 1)
            else:
                pe.wait_ge(vt_mm, 2 * b + 1)
            for tt in range(T):
                for k in range(C2):
                    mm = nc.tensor.matmul(ps[:, 4 + tt, k * HT * M:(k + 1) * HT * M], qT[:, par, d, k, tt * P:(tt + 1) * P],
                                          k_blocks[:, par, C2 * d + k].rearrange("p h m -> p (h m)"), start=True, stop=True)
            mm.then_inc(aff_mm, 1)

        def row_sums(f, par):
            pe.wait_ge(xT_in[par], loads(f, par))
            ge(pe, aff_out, 2 * T * (f - 1))
            for k in range(C2):
                mm = nc.tensor.matmul(halves(ps, 4)[:, 0, :], ones[:], xT[:, par, k, :], start=(k == 0), stop=(k == C2 - 1))
            mm.then_inc(sums_mm, 1)

        def features(f, par):
            ge(pe, outT_made, C2 * (f - 2))
            for m in range(C2):
                for k in range(C2):
                    mm = nc.tensor.matmul(halves(ps, 1)[:, m, :], w_x[:, k, m * P:(m + 1) * P], xT[:, par, k, :],
                                          start=(k == 0), stop=(k == C2 - 1))
            mm.then_inc(feat_mm, 1)

        def queries(f, d):
            pe.wait_ge(feat_out, f + 1)
            ge(pe, q_out, 2 * C2 * f)
            for m in range(C2):
                for k in range(C2):
                    mm = nc.tensor.matmul(halves(ps, 2 + d)[:, m, :], w_q[:, d, k, m * P:(m + 1) * P], feat_at(f)[:, k, :],
                                          start=(k == 0), stop=(k == C2 - 1))
            mm.then_inc(q_mm, 1)

        def values_transposed(b, j):
            for k in range(2 * C2):
                o = (2 * k + j) * 64
                mm = nc.tensor.transpose(ps[0:G4, 0, o:o + 64],
                                         v_masked[64 * j:64 * j + 64, k, 4 * j:4 * j + 4].rearrange("p h m -> p (h m)"),
                                         ident[64 * j:64 * j + 64, 64 * j:64 * j + 64])
            mm.then_inc(vt_mm, 1)

        def weights_of(c, par, d):
            pe.wait_ge(norm_made, 2 * c + d + 1)
            ge(pe, wT_out, 2 * c + d)
            for tt in range(T):
                for k in range(4):
                    mm = nc.tensor.transpose(ps[0:G4, 6 + tt, k * P:(k + 1) * P],
                                             scores[:, par, d, tt, 4 * k:4 * k + 4].rearrange("p h m -> p (h m)"), ident[:])
            mm.then_inc(wT_mm, 1)

        def output_channels(c, par, fronts):
            pe.wait_ge(wT_out, 2 * c + 2)
            pe.wait_ge(feat_out, fronts)
            pe.wait_ge(vb_made, c + 1)
            for m in range(C2):
                for d in range(2):
                    for j in range(2):
                        mm = nc.tensor.matmul(halves(ps, 1)[64 * j:64 * j + 64, m, :], v_blocks[:, par, 2 * (C2 * d + m) + j, :],
                                              weightT[:, d, :, 2 * m + j, :], start=(d == 0), stop=(d == 1))
            mm.then_inc(pv_mm, 1)

        def output_tokens(c, backs):
            pe.wait_ge(outT_made, C2 * (c + 1))
            pe.wait_ge(vb_made, backs)
            for tt in range(T):
                for k in range(C2):
                    mm = nc.tensor.transpose(ps[:, 0, (C2 * tt + k) * P:(C2 * tt + k + 1) * P], outT[:, k, tt * P:(tt + 1) * P],
                                             ident[:])
            mm.then_inc(out_mm, 1)

        def turn(f, b, c, par):
            if f is not None:
                row_sums(f, par)
                features(f, par)
            if c is not None:
                weights_of(c, par, 0)
            if b is not None:
                raw_scores(b, 1 - par, 0)
                values_transposed(b, 0)
            if c is not None:
                weights_of(c, par, 1)
            if f is not None:
                queries(f, 0)
            if b is not None:
                raw_scores(b, 1 - par, 1)
                values_transposed(b, 1)
            if c is not None:
                output_channels(c, par, B if f is None else f + 1)
            if f is not None:
                queries(f, 1)
            if c is not None:
                output_tokens(c, B if b is None else b + 1)

        turns(turn, pe, 3)


def norm_stats(nc, x_res, b, stats, stats_made):
    for tt in range(T):
        nc.vector.bn_stats(stats[:, tt, :], x_res[:, bass.ds(b * T + tt, 1), :].rearrange("p a f -> p (a f)")).then_inc(stats_made, 1)


def norm_moments(nc, stats, mean_var, mv_made):
    for tt in range(T):
        nc.vector.bn_aggr(mean_var[:, tt, :], stats[:, tt, :]).then_inc(mv_made, 1)


def norm_root(pool, nc, b, mean_var, g, var_eps, rstd, mv_made, eps_made, rstd_made):
    pool.wait_ge(mv_made, T * (b + 1))
    nc.gpsimd.tensor_tensor(var_eps[:], mean_var[:, :, 1], g["ln_eps"][:], ALU.add).then_inc(eps_made, 1)
    pool.wait_ge(eps_made, b + 1)
    nc.gpsimd.tensor_tensor(rstd[:], var_eps[:], g["neg_half"][:], ALU.pow).then_inc(rstd_made, 1)


def attention_block(nc, scope, t, alloc, sems, ps, g):
    x_res, ident, ident_b = g["x_res"], g["ident"], g["ident_b"]
    w_qkv, w_proj, ada, bias_qk = g["w_qkv"], g["w_proj"], g["ada"], g["bias_qk"]
    b_v, b_proj, head_scale = g["b_v"], g["b_proj"], g["head_scale"]
    HH = T * 2 * H
    parts_dram = nc.dram_tensor("parts_dram", (2, HT, 3, HD, C2 * N), BF16, kind="Internal").ap()
    stats = alloc(scope, "stats", [P, T, 6])
    mean_var = alloc(scope, "mean_var", [P, T, 2])
    var_eps = alloc(scope, "var_eps", [P, T])
    rstd = alloc(scope, "rstd", [P, T])
    x_hat = alloc(scope, "x_hat", [P, T, F])
    x1T = alloc(scope, "x1T", [P, 2, C2, N])
    qk = alloc(scope, "qk", [P, T, 2 * F])
    squares = alloc(scope, "squares", [P, T, 2 * F])
    sum_sq = alloc(scope, "sum_sq", [P, HH])
    minus_half = alloc(scope, "minus_half", [P, HH])
    root = [alloc(scope, f"root{i}", [P, HH]) for i in range(2)]
    root_sq = alloc(scope, "root_sq", [P, HH])
    root_err = alloc(scope, "root_err", [P, HH])
    qkn = alloc(scope, "qkn", [P, T, 2 * F])
    parts = alloc(scope, "parts", [P, 2, 3, C2 * N], BF16)
    rest = alloc(scope, "rest", [P, 2, C2 * N])
    q_stack = alloc(scope, "q_stack", [KROWS + 1, 2, H, N], BF16)
    k_stack = alloc(scope, "k_stack", [KROWS + 1, 2, H, N], BF16)
    v_ones = alloc(scope, "v_ones", [P, 2, T, H, 2 * HD])
    neg_max = alloc(scope, "neg_max", [P, T, H], BF16)
    neg_maxT = alloc(scope, "neg_maxT", [HT, 2, N], BF16)
    probsT = alloc(scope, "probsT", [P, 4, 1024])
    o_sumsT = alloc(scope, "o_sumsT", [P, 2, 2 * N])
    denom = alloc(scope, "denom", [P, T, H])
    o_tok = alloc(scope, "o_tok", [P, T, F])
    oT = alloc(scope, "oT", [P, C2, N])
    projT = alloc(scope, "projT", [P, C2, N])
    b_gated = alloc(scope, "b_gated", [P, C2, B])
    (stats_made, mv_made, eps_made, rstd_made, xhat_made, xt_mm, x1_out, qk_mm, qk_out, v_mm, v_out, sq_made, ss_made,
     root_step, qkn_made, qkt_mm, high_made, rest_made, mid_made, low_made, parts_out, stack_in, s_mm, max_made, m_mm, m_out,
     m_low_in, m_high_in, st_mm, exp_made, pv_mm, os_out, otok_mm, den_made, otok_made, ot_mm, ot_out, proj_mm, proj_out,
     res_mm, res_made, ones_set, gated_bias) = sems(
        scope, "stats_made", "mv_made", "eps_made", "rstd_made", "xhat_made", "xt_mm", "x1_out", "qk_mm", "qk_out", "v_mm",
        "v_out", "sq_made", "ss_made", "root_step", "qkn_made", "qkt_mm", "high_made", "rest_made", "mid_made", "low_made",
        "parts_out", "stack_in", "s_mm", "max_made_a", "m_mm", "m_out", "m_low_in", "m_high_in", "st_mm", "exp_made_a",
        "pv_mm_a", "os_out", "otok_mm", "den_made", "otok_made", "ot_mm", "ot_out", "proj_mm", "proj_out", "res_mm",
        "res_made", "ones_set", "gated_bias")
    m_row_in = (m_low_in, m_high_in)
    block = scope.enter_context(nc.Block())
    SLOTS = 10
    ROW_GROUPS = 16
    FIRST = (0, 0, 0, 0, 0, 1, 3, 5, 8, 11, 14)
    LATE_FIRST = (14, 15, 16)

    VALUES = (3, 4, 6, 9)

    def groups(b, s):
        return () if b is None else range(FIRST[s], FIRST[s + 1])

    def late_groups(c, s):
        return range(LATE_FIRST[s], LATE_FIRST[s + 1]) if c is not None and s < 2 else ()

    def group_bank(n):
        return 3 + (n if n < 10 else n + 1) % 3

    def maxima_bank(i):
        return 3 + (10, 17)[i] % 3

    @block.sync
    def _(sp):
        def max_row(b, par, i):
            sp.wait_ge(m_out, 2 * b + i + 1)
            sp.dma_start(q_stack[KROWS:KROWS + 1, par, HT * i:HT * (i + 1)], neg_maxT[:, i, :]).then_inc(m_row_in[i], 16)

        def turn(f, b, c, d, par):
            if c is not None:
                max_row(c, par, 1)
            if f is not None:
                ge(sp, stack_in, f * (9 * 16))
                for part, made in enumerate((high_made, mid_made, low_made)):
                    for w in range(2):
                        sp.wait_ge(made, 2 * f + w + 1)
                        sp.dma_start(parts_dram[w, :, part], parts[:, w, part]).then_inc(parts_out, 16)
            if b is not None:
                max_row(b, 1 - par, 0)
            if f is not None:
                sp.wait_ge(parts_out, 6 * 16 * (f + 1))
                ge(sp, st_mm, f * 8 - 8)

                def rows(stack, at, n):
                    return stack[at * SLOT:(at + n) * SLOT, par].rearrange("p (h c) n -> p h (c n)", c=C2)

                def whole(w, part, n):
                    return parts_dram[w, :, part:part + n].rearrange("h a d x -> (a d) h x")

                for slot, part in enumerate(Q_PARTS):
                    sp.dma_start(rows(q_stack, slot, 1), whole(0, part, 1)).then_inc(stack_in, 16)
                for slot, n in ((0, 3), (3, 2), (5, 1)):
                    sp.dma_start(rows(k_stack, slot, n), whole(1, 0, n)).then_inc(stack_in, 16)
        turns(turn, sp, 4)

    @block.gpsimd
    def _(pool):
        norm_root(pool, nc, 0, mean_var, g, var_eps, rstd, mv_made, eps_made, rstd_made)

        def turn(f, b, c, d, par):
            ahead = following(f)
            if ahead is not None:
                norm_root(pool, nc, ahead, mean_var, g, var_eps, rstd, mv_made, eps_made, rstd_made)
            if f is not None:
                for w in range(2):
                    pool.wait_ge(mid_made, 2 * f + w + 1)
                    nc.gpsimd.tensor_tensor(parts[:, w, 2, :], rest[:, w, :], parts[:, w, 1, :], ALU.subtract).then_inc(low_made, 1)

        turns(turn, pool, 4)

    @block.scalar
    def _(act):
        def shift_scale(n, par):
            act.wait_ge(xt_mm, n + 1)
            ge(act, v_mm, n - 1)
            for k in range(C2):
                nc.scalar.activation(x1T[:, par, k, :], halves(ps, 1)[:, k, :], ACT.Identity,
                                     bias=ada[:, 4 * C2 + k, bass.ds(n, 1)],
                                     scale=ada[:, 2 * C2 + k, bass.ds(n, 1)]).then_inc(x1_out, 1)

        def square(f, tt):
            act.wait_ge(qk_out, T * f + tt + 1)
            ge(act, ss_made, T * f)
            nc.scalar.activation(squares[:, tt, :], qk[:, tt, :], ACT.Square).then_inc(sq_made, 1)

        def take_v(b, par):
            act.wait_ge(v_mm, b + 1)
            ge(act, pv_mm, 4 * (b - 1))
            if isinstance(b, int):
                ge(act, ones_set, 1)
            nc.scalar.activation(v_ones[:, par, :, :, 0:HD], halves(ps, 0).rearrange("p t (h d) -> p t h d", d=HD),
                                 ACT.Copy).then_inc(v_out, 1)

        def take_maxima(b, par, i):
            act.wait_ge(m_mm, 2 * b + i + 1)
            ge(act, m_row_in[i], 16 * b)
            nc.scalar.activation(neg_maxT[:, i, :], ps[0:HT, maxima_bank(i), 0:N // 2].bitcast(BF16), ACT.Copy).then_inc(m_out, 1)

        def probabilities(c, s):
            act.wait_ge(st_mm, 8 * c + s + 1)
            ge(act, pv_mm, 4 * c + s // 2 - 1)
            nc.scalar.activation(probsT[:, s % 4, :], ps[:, 6:8, :].rearrange("p a n -> p (a n)"),
                                 ACT.Exp).then_inc(exp_made, 1)

        def take_sums(c, i):
            act.wait_ge(pv_mm, 4 * c + 2 * i + 2)
            ge(act, otok_mm, c)
            nc.scalar.activation(o_sumsT[:, i, :], ps[:, 2, :], ACT.Copy).then_inc(os_out, 1)

        def add_bias_v(d):
            act.wait_ge(ot_mm, d + 1)
            ge(act, proj_mm, d)
            for k in range(C2):
                nc.scalar.activation(oT[:, k, :], halves(ps, 0)[:, k, :], ACT.Identity, bias=b_v[:, k:k + 1]).then_inc(ot_out, 1)

        def gate(d):
            act.wait_ge(proj_mm, d + 1)
            ge(act, res_mm, d)
            if isinstance(d, int):
                ge(act, gated_bias, C2)
            for k in range(C2):
                nc.scalar.activation(projT[:, k, :], halves(ps, 1)[:, k, :], ACT.Identity, bias=b_gated[:, k, bass.ds(d, 1)],
                                     scale=ada[:, k, bass.ds(d, 1)]).then_inc(proj_out, 1)

        def turn(f, b, c, d, par):
            for s in range(SLOTS):
                if c is not None and s < 8:
                    probabilities(c, s)
                if f is not None and s < 2:
                    square(f, s)
                if c is not None and s == 2:
                    take_maxima(c, par, 1)
                if b is not None and s == 2:
                    take_v(b, 1 - par)
                if d is not None and s == 4:
                    add_bias_v(d)
                if c is not None and s == 5:
                    take_sums(c, 0)
                if f is not None and s == 5:
                    ge(act, parts_out, 6 * 16 * f)
                    for w in range(2):
                        act.wait_ge(qkt_mm, 2 * f + w + 1)
                        nc.scalar.activation(parts[:, w, 0, :], ps[:, 1 - w, :], ACT.Copy).then_inc(high_made, 1)
                if f is not None and s == 6:
                    for w in range(2):
                        act.wait_ge(rest_made, 2 * f + w + 1)
                        nc.scalar.activation(parts[:, w, 1, :], rest[:, w, :], ACT.Copy).then_inc(mid_made, 1)
                if d is not None and s == 7:
                    gate(d)
                if b is not None and s == 8:
                    take_maxima(b, 1 - par, 0)
            if following(f) is not None:
                shift_scale(following(f), 1 - par)
            if c is not None:
                take_sums(c, 1)

        shift_scale(0, 0)
        turns(turn, act, 4)

    @block.vector
    def _(dve):
        def normalise(n):
            dve.wait_ge(rstd_made, n + 1)
            ge(dve, xt_mm, n)
            for tt in range(T):
                nc.vector.tensor_scalar(x_hat[:, tt, :], x_res[:, bass.ds(n * T + tt, 1), :].rearrange("p a f -> p (a f)"),
                                        mean_var[:, tt, 0:1], rstd[:, tt:tt + 1], ALU.subtract, ALU.mult).then_inc(xhat_made, 1)

        def take_qk(f, tt):
            dve.wait_ge(qk_mm, T * f + tt + 1)
            ge(dve, sq_made, T * f)
            nc.vector.tensor_tensor(qk[:, tt, :], ps[:, tt, :], bias_qk[:], ALU.add).then_inc(qk_out, 1)

        STEPS = 14

        def link(f, n, ins):
            ins.then_inc(root_step, 1)
            dve.wait_ge(root_step, f * STEPS + n)

        def sum_squares(f, tt):
            dve.wait_ge(sq_made, T * f + tt + 1)
            nc.vector.tensor_reduce(sum_sq[:, tt * 2 * H:(tt + 1) * 2 * H], squares[:, tt].rearrange("p (h d) -> p h d", d=HD), AX_X,
                                    ALU.add).then_inc(ss_made, 1)

        def first_guess(f):
            dve.wait_ge(ss_made, T * (f + 1))
            link(f, 1, nc.vector.tensor_scalar(sum_sq[:], sum_sq[:], NORM_EPS2, None, ALU.max))
            nc.vector.tensor_scalar(minus_half[:], sum_sq[:], -0.5, None, ALU.mult).then_inc(root_step, 1)
            link(f, 3, nc.vector.tensor_scalar(root[0][:].bitcast(I32), sum_sq[:].bitcast(I32), 1, None, ALU.arith_shift_right))
            link(f, 4, nc.vector.tensor_scalar(root[1][:].bitcast(I32), root[0][:].bitcast(I32), -1.0, SEED, ALU.mult, ALU.add))

        def newton(f, n):
            old, new = root[(n + 1) % 2], root[n % 2]
            link(f, 3 * n + 5, nc.vector.tensor_tensor(root_sq[:], old[:], old[:], ALU.mult))
            link(f, 3 * n + 6, nc.vector.tensor_tensor(root_err[:], root_sq[:], minus_half[:], ALU.mult))
            link(f, 3 * n + 7, nc.vector.scalar_tensor_tensor(out=new[:], in0=root_err[:], scalar=1.5, in1=old[:],
                                                              op0=ALU.add, op1=ALU.mult))

        def unit_qk(f):
            norm = root[0]
            by = norm[:].rearrange("p (t w h) -> p t w h", t=T, w=2)
            link(f, STEPS, nc.vector.tensor_tensor(by[:, :, 0, :], by[:, :, 0, :], head_scale[:].unsqueeze(1).broadcast_to([P, T, H]),
                                                   ALU.mult))
            ge(dve, qkt_mm, 2 * f)
            nc.vector.tensor_tensor(qkn[:].rearrange("p t (h d) -> p (t h) d", d=HD), qk[:].rearrange("p t (h d) -> p (t h) d", d=HD),
                                    norm[:].unsqueeze(2).broadcast_to([P, HH, HD]), ALU.mult).then_inc(qkn_made, 1)

        def maxima(b, n):
            if n == 0:
                ge(dve, m_mm, 2 * b)
            dve.wait_ge(s_mm, ROW_GROUPS * b + n + 1)
            pair, tt = n // 2, n % 2
            nc.vector.tensor_reduce(neg_max[:, tt, 2 * pair:2 * pair + 2], halves(ps, group_bank(n)), AX_X, ALU.max,
                                    negate=True).then_inc(max_made, 1)

        def rests(f):
            for w in range(2):
                dve.wait_ge(high_made, 2 * f + w + 1)
                ge(dve, low_made, 2 * f)
                nc.vector.tensor_tensor(rest[:, w, :], ps[:, 1 - w, :], parts[:, w, 0, :], ALU.subtract).then_inc(rest_made, 1)

        def divide(d):
            dve.wait_ge(otok_mm, d + 1)
            places = ps[:, 0:2, :].rearrange("p t (g d) -> p t g d", d=2 * HD)
            nc.vector.reciprocal(denom[:], places[:, :, :, HD]).then_inc(den_made, 1)
            dve.wait_ge(den_made, d + 1)
            ge(dve, ot_mm, d)
            for tt in range(T):
                nc.vector.tensor_tensor(o_tok[:, tt, :].rearrange("p (c h d) -> p h c d", c=C2, d=HD),
                                        places[:, tt, :, 0:HD].rearrange("p (h c) d -> p h c d", c=C2),
                                        denom[:, tt, :].rearrange("p (h c) -> p h c", c=C2).unsqueeze(3).broadcast_to([P, HT, C2, HD]),
                                        ALU.mult).then_inc(otok_made, 1)

        def residual(d):
            dve.wait_ge(res_mm, d + 1)
            x = x_res[:, bass.ds(d * T, T), :].rearrange("p t f -> p (t f)")
            nc.vector.tensor_tensor(x, ps[:, 0, :], x, ALU.add).then_inc(res_made, 1)

        norm_stats(nc, x_res, 0, stats, stats_made)
        dve.wait_ge(stats_made, T)
        norm_moments(nc, stats, mean_var, mv_made)
        normalise(0)
        nc.vector.memset(v_ones[:], 1.0).then_inc(ones_set, 1)
        nc.vector.memset(k_stack[KROWS:KROWS + 1], 1.0).then_inc(ones_set, 1)
        dve.wait_ge(g["late_weights"], g["LATE"])
        for k in range(C2):
            nc.vector.tensor_scalar(b_gated[:, k, :], ada[:, k, :], b_proj[:, k:k + 1], None, ALU.mult).then_inc(gated_bias, 1)

        def turn(f, b, c, d, par):
            ahead = following(f)
            for s in range(SLOTS):
                for n in late_groups(c, s):
                    maxima(c, n)
                if ahead is not None and s == 0:
                    norm_stats(nc, x_res, ahead, stats, stats_made)
                    dve.wait_ge(stats_made, T * (f + 2))
                if f is not None and s < 2:
                    take_qk(f, s)
                if ahead is not None and s == 0:
                    norm_moments(nc, stats, mean_var, mv_made)
                if f is not None and s == 1:
                    sum_squares(f, 0)
                if ahead is not None and s == 1:
                    normalise(ahead)
                if f is not None and s == 3:
                    newton(f, 0)
                    newton(f, 1)
                for n in groups(b, s):
                    maxima(b, n)
                if f is not None and s == 2:
                    sum_squares(f, 1)
                    first_guess(f)
                if d is not None and s == 3:
                    divide(d)
                if f is not None and s == 3:
                    newton(f, 2)
                    unit_qk(f)
                if f is not None and s == 5:
                    rests(f)
                if d is not None and s == 8:
                    residual(d)

        turns(turn, dve, 4)

    @block.tensor
    def _(pe):
        pe.wait_ge(g["late_weights"], g["LATE"])

        def norm_transposed(n, d):
            pe.wait_ge(xhat_made, T * (n + 1))
            if d is not None:
                pe.wait_ge(proj_out, C2 * (d + 1))
            else:
                ge(pe, rest_made, 2 * n - 1)
            for tt in range(T):
                for k in range(C2):
                    mm = nc.tensor.transpose(halves(ps, 1)[:, k, tt * P:(tt + 1) * P], x_hat[:, tt, k * P:(k + 1) * P], ident[:])
            mm.then_inc(xt_mm, 1)

        def make_qk(f, par, tt):
            pe.wait_ge(x1_out, C2 * (f + 1))
            if tt == 0:
                ge(pe, res_made, f - 3)
                if isinstance(f, int):
                    ge(pe, rest_made, 2 * f)
            for k in range(C2):
                mm = nc.tensor.matmul(ps[:, tt, :], x1T[:, par, k, tt * P:(tt + 1) * P], w_qkv[:, k, 0:2 * F],
                                      start=(k == 0), stop=(k == C2 - 1))
            mm.then_inc(qk_mm, 1)

        def make_v(b, par, f):
            if f is not None:
                pe.wait_ge(qk_out, T * f + 1)
            else:
                ge(pe, res_made, b - 2)
            for tt in range(T):
                for k in range(C2):
                    mm = nc.tensor.matmul(halves(ps, 0)[:, tt, :], x1T[:, par, k, tt * P:(tt + 1) * P], w_qkv[:, k, 2 * F:3 * F],
                                          start=(k == 0), stop=(k == C2 - 1))
            mm.then_inc(v_mm, 1)

        def row_scores(b, par, n):
            if n == 0:
                pe.wait_ge(stack_in, 9 * 16 * (b + 1))
            if n == 12:
                pe.wait_ge(m_out, 2 * b + 1)
            elif n == 2:
                ge(pe, m_out, 2 * b)
            else:
                ge(pe, max_made, ROW_GROUPS * b + n - (1 if n < 2 or 10 <= n <= 11 else 2))
            pair, tt = n // 2, n % 2
            for j in range(2):
                mm = nc.tensor.matmul(halves(ps, group_bank(n))[:, j, :],
                                      q_stack[0:KROWS, par, 2 * pair + j, tt * P:(tt + 1) * P], k_stack[0:KROWS, par, 2 * pair + j, :],
                                      start=True, stop=True)
            mm.then_inc(s_mm, 1)

        def max_transposed(b, i):
            pe.wait_ge(max_made, ROW_GROUPS * b + 8 * (i + 1))
            for tt in range(T):
                mm = nc.tensor.transpose(ps[0:HT, maxima_bank(i), tt * P // 2:(tt + 1) * P // 2].bitcast(BF16),
                                         neg_max[:, tt, HT * i:HT * (i + 1)], ident_b[:])
            mm.then_inc(m_mm, 1)

        def split_qk(f, d):
            pe.wait_ge(qkn_made, f + 1)
            for w in range(2):
                if w == 1:
                    ge(pe, v_out, f)
                    if d is not None:
                        pe.wait_ge(ot_out, C2 * (d + 1))
                for tt in range(T):
                    for k in range(C2):
                        mm = nc.tensor.transpose(halves(ps, 1 - w)[:, k, tt * P:(tt + 1) * P],
                                                 qkn[:, tt, w * F + k * P:w * F + (k + 1) * P], ident[:])
                mm.then_inc(qkt_mm, 1)

        def col_scores(c, par, s):
            if isinstance(c, int) and c == 0 and s == 0:
                pe.wait_ge(ones_set, 2)
            if s % 4 == 0:
                pe.wait_ge(m_row_in[s // 4], 16 * (c + 1))
            ge(pe, exp_made, 8 * c + s)
            for j in range(2):
                place = 2 * s + j
                for kt in range(T):
                    mm = nc.tensor.matmul(ps[:, 6 + j, kt * N:(kt + 1) * N], k_stack[:, par, place, kt * P:(kt + 1) * P],
                                          q_stack[:, par, place, :], start=True, stop=True)
            mm.then_inc(st_mm, 1)

        def values(c, par, hg):
            if hg % 2 == 0:
                ge(pe, os_out, 2 * c + hg // 2)
            pe.wait_ge(exp_made, 8 * c + 2 * hg + 2)
            for kt in range(T):
                for j in range(4):
                    place = 4 * hg + j
                    mm = nc.tensor.matmul(halves(ps, 2)[32 * j:32 * j + 32, hg % 2, :],
                                          v_ones[:, par, kt, HT * (place % 2) + place // 2, :],
                                          probsT[:, (2 * hg + j // 2) % 4, (j % 2) * 2 * N + kt * N:(j % 2) * 2 * N + (kt + 1) * N],
                                          start=(kt == 0), stop=(kt == T - 1))
            mm.then_inc(pv_mm, 1)

        def output_tokens(d, f):
            pe.wait_ge(os_out, 2 * (d + 1))
            pe.wait_ge(v_out, min(d + 3, B) if isinstance(d, int) else d + 3)
            if f is not None:
                pe.wait_ge(qk_out, T * (f + 1))
            else:
                pe.wait_ge(rest_made, 2 * B)
                ge(pe, res_made, d)
                ge(pe, proj_out, C2 * d)
            for tt in range(T):
                for hg in range(4):
                    o = (hg % 2) * N + tt * P
                    mm = nc.tensor.transpose(ps[:, tt, hg * P:(hg + 1) * P], o_sumsT[:, hg // 2, o:o + P], ident[:])
            mm.then_inc(otok_mm, 1)

        def output_channels(d):
            pe.wait_ge(otok_made, T * (d + 1))
            for tt in range(T):
                for k in range(C2):
                    mm = nc.tensor.transpose(halves(ps, 0)[:, k, tt * P:(tt + 1) * P], o_tok[:, tt, k * P:(k + 1) * P], ident[:])
            mm.then_inc(ot_mm, 1)

        def project(d, f):
            pe.wait_ge(ot_out, C2 * (d + 1))
            if f is not None:
                pe.wait_ge(rest_made, 2 * f + 1)
            for m in range(C2):
                for k in range(C2):
                    mm = nc.tensor.matmul(halves(ps, 1)[:, m, :], w_proj[:, k, m * P:(m + 1) * P], oT[:, k, :],
                                          start=(k == 0), stop=(k == C2 - 1))
            mm.then_inc(proj_mm, 1)

        def residual(d, f):
            pe.wait_ge(proj_out, C2 * (d + 1))
            if f is not None:
                pe.wait_ge(rest_made, 2 * (f + 1))
            for tt in range(T):
                for k in range(C2):
                    mm = nc.tensor.transpose(ps[:, 0, (C2 * tt + k) * P:(C2 * tt + k + 1) * P], projT[:, k, tt * P:(tt + 1) * P],
                                             ident[:])
            mm.then_inc(res_mm, 1)

        def turn(f, b, c, d, par):
            for s in range(SLOTS):
                if c is not None and s < 8:
                    col_scores(c, par, s)
                for n in late_groups(c, s):
                    row_scores(c, par, n)
                if c is not None and s == 2:
                    max_transposed(c, 1)
                for n in groups(b, s):
                    if n == 10:
                        max_transposed(b, 0)
                    row_scores(b, 1 - par, n)
                if f is not None and s < 2:
                    make_qk(f, par, s)
                if b is not None and s == 2:
                    make_v(b, 1 - par, f)
                if d is not None and s == 3:
                    output_tokens(d, f)
                if d is not None and s == 4:
                    output_channels(d)
                if f is not None and s == 5:
                    split_qk(f, d)
                if d is not None and s == 7:
                    project(d, f)
                if c is not None and s in VALUES:
                    values(c, par, VALUES.index(s))
                if d is not None and s == 8:
                    residual(d, f)
                if following(f) is not None and s == 8:
                    norm_transposed(following(f), d)
        norm_transposed(0, None)
        turns(turn, pe, 4)


def ffn_block(nc, scope, t, alloc, sems, ps, g):
    x_res, ident, ada = g["x_res"], g["ident"], g["ada"]
    w_fc1, w_fc2, b_fc1, b_fc2 = g["w_fc1"], g["w_fc2"], g["b_fc1"], g["b_fc2"]
    DT = DFF // P
    PAIRS = DT // 2
    stats = alloc(scope, "stats_f", [P, T, 6])
    mean_var = alloc(scope, "mean_var_f", [P, T, 2])
    var_eps = alloc(scope, "var_eps_f", [P, T])
    rstd = alloc(scope, "rstd_f", [P, T])
    x_hat = alloc(scope, "x_hat_f", [P, T, F])
    w1_parts = [alloc(scope, f"w1_{n}", [P, C2, DFF], F32R) for n in ("high", "low")]
    w2_parts = [alloc(scope, f"w2_{n}", [P, DT, F], F32R) for n in ("high", "low")]
    cleared_w = alloc(scope, "cleared_w", [P, 2, DT * F])
    x2T = alloc(scope, "x2T", [P, C2, N])
    x2_cleared = alloc(scope, "x2_cleared", [P, C2, N])
    x2_parts = [alloc(scope, f"x2_{n}", [P, C2, N], F32R) for n in ("high", "low")]
    hidden = alloc(scope, "hidden", [P, DT, N])
    hidden_cleared = alloc(scope, "hidden_cleared", [P, DT, N])
    hidden_parts = [alloc(scope, f"hidden_{n}", [P, 2, DT, N], F32R) for n in ("high", "low")]
    outT = alloc(scope, "outT_f", [P, C2, N])
    result = alloc(scope, "result", [P, 2, T * F])
    (stats_made, mv_made, eps_made, rstd_made, xhat_made, xt_mm, x2_out, x2_clear, x2_high, x2_low, fc1_mm, gelu_made,
     h_clear, h_high, h_low, fc2_mm, outT_made, out_mm, result_made, w_clear, w_high, w_low) = sems(
        scope, "stats_made_f", "mv_made_f", "eps_made_f", "rstd_made_f", "xhat_made_f", "xt_mm_f", "x2_out", "x2_clear",
        "x2_high", "x2_low", "fc1_mm", "gelu_made", "h_clear", "h_high", "h_low", "fc2_mm", "outT_made_f", "out_mm_f",
        "result_made", "w_clear", "w_high", "w_low")
    stored = sems(scope, "stored_even", "stored_odd")
    weights = [(w_fc1[:].rearrange("p k n -> p (k n)"), [w[:].rearrange("p k n -> p (k n)") for w in w1_parts]),
               (w_fc2[:].rearrange("p k n -> p (k n)"), [w[:].rearrange("p k n -> p (k n)") for w in w2_parts])]
    block = scope.enter_context(nc.Block())

    def clear_low_bits(out, in_):
        return nc.vector.tensor_scalar(out.bitcast(I32), in_.bitcast(I32), LOW_BITS, LOW_BITS, ALU.logical_shift_right,
                                       ALU.logical_shift_left)

    @block.sync
    def _(sp):
        def turn(f, b, c, par):
            if c is not None:
                sp.wait_ge(result_made, c + 1)
                sp.dma_start(t["out"][bass.ds(c * N, N), :].rearrange("(t p) f -> p t f", p=P),
                             result[:, par, :].rearrange("p (t f) -> p t f", t=T)).then_inc(stored[par], 16)

        turns(turn, sp, 3)
        for par in range(2):
            sp.wait_ge(stored[par], 16 * (B // 2))

    @block.gpsimd
    def _(pool):
        norm_root(pool, nc, 0, mean_var, g, var_eps, rstd, mv_made, eps_made, rstd_made)

        def turn(f, b, c, par):
            if following(f) is not None:
                norm_root(pool, nc, following(f), mean_var, g, var_eps, rstd, mv_made, eps_made, rstd_made)

        turns(turn, pool, 3)

    @block.scalar
    def _(act):
        def weights_high(i):
            act.wait_ge(w_clear, i + 1)
            nc.scalar.activation(weights[i][1][0], cleared_w[:, i, :], ACT.Copy).then_inc(w_high, 1)

        def shift_scale(n):
            act.wait_ge(xt_mm, n + 1)
            ge(act, x2_low, n)
            for k in range(C2):
                nc.scalar.activation(x2T[:, k, :], halves(ps, 0)[:, k, :], ACT.Identity, bias=ada[:, 5 * C2 + k, bass.ds(n, 1)],
                                     scale=ada[:, 3 * C2 + k, bass.ds(n, 1)]).then_inc(x2_out, 1)
            act.wait_ge(x2_clear, n + 1)
            ge(act, fc1_mm, PAIRS * n)
            nc.scalar.activation(x2_parts[0][:], x2_cleared[:], ACT.Copy).then_inc(x2_high, 1)

        def hidden_high(f, par, q):
            act.wait_ge(h_clear, PAIRS * f + q + 1)
            nc.scalar.activation(hidden_parts[0][:, par, 2 * q:2 * q + 2, :], hidden_cleared[:, 2 * q:2 * q + 2, :],
                                 ACT.Copy).then_inc(h_high, 1)

        def turn(f, b, c, par):
            if f is None:
                return
            ge(act, fc2_mm, f - 1)
            for q in range(PAIRS):
                ge(act, h_low, PAIRS * (f - 1) + q + 1)
                act.wait_ge(fc1_mm, PAIRS * f + q + 1)
                for m in (2 * q, 2 * q + 1):
                    nc.scalar.activation(hidden[:, m, :], halves(ps, 1 + q)[:, m % 2, :], ACT.Gelu,
                                         bias=b_fc1[:, m:m + 1]).then_inc(gelu_made, 1)
                if q > 0:
                    hidden_high(f, par, q - 1)
            hidden_high(f, par, PAIRS - 1)
            if following(f) is not None:
                shift_scale(following(f))

        weights_high(0)
        shift_scale(0)
        weights_high(1)
        turns(turn, act, 3)

    @block.vector
    def _(dve):
        def clear_weights(i):
            clear_low_bits(cleared_w[:, i, :], weights[i][0]).then_inc(w_clear, 1)

        def weights_low(i):
            dve.wait_ge(w_clear, i + 1)
            nc.vector.tensor_tensor(weights[i][1][1], weights[i][0], cleared_w[:, i, :], ALU.subtract).then_inc(w_low, 1)

        def normalise(n):
            dve.wait_ge(rstd_made, n + 1)
            ge(dve, xt_mm, n)
            for tt in range(T):
                nc.vector.tensor_scalar(x_hat[:, tt, :], x_res[:, bass.ds(n * T + tt, 1), :].rearrange("p a f -> p (a f)"),
                                        mean_var[:, tt, 0:1], rstd[:, tt:tt + 1], ALU.subtract, ALU.mult).then_inc(xhat_made, 1)

        def split_x2(n):
            dve.wait_ge(x2_out, C2 * (n + 1))
            ge(dve, x2_high, n)
            clear_low_bits(x2_cleared[:], x2T[:]).then_inc(x2_clear, 1)
            dve.wait_ge(x2_clear, n + 1)
            ge(dve, fc1_mm, PAIRS * n)
            nc.vector.tensor_tensor(x2_parts[1][:], x2T[:], x2_cleared[:], ALU.subtract).then_inc(x2_low, 1)

        def split_hidden(f, par, q):
            pair = slice(2 * q, 2 * q + 2)
            dve.wait_ge(gelu_made, DT * f + 2 * q + 2)
            ge(dve, h_high, PAIRS * (f - 1) + q + 1)
            clear_low_bits(hidden_cleared[:, pair, :], hidden[:, pair, :]).then_inc(h_clear, 1)
            dve.wait_ge(h_clear, PAIRS * f + q + 1)
            ge(dve, fc2_mm, f - 1)
            nc.vector.tensor_tensor(hidden_parts[1][:, par, pair, :], hidden[:, pair, :], hidden_cleared[:, pair, :],
                                    ALU.subtract).then_inc(h_low, 1)

        def turn(f, b, c, par):
            ahead = following(f)
            if ahead is not None:
                norm_stats(nc, x_res, ahead, stats, stats_made)
                dve.wait_ge(stats_made, T * (f + 2))
            if c is not None:
                dve.wait_ge(fc2_mm, c + 1)
                ge(dve, out_mm, c)
                for k in range(C2):
                    nc.vector.tensor_scalar(outT[:, k, :], halves(ps, 5)[:, k, :], b_fc2[:, k:k + 1],
                                            ada[:, C2 + k, bass.ds(c, 1)], ALU.add, ALU.mult).then_inc(outT_made, 1)
            if ahead is not None:
                norm_moments(nc, stats, mean_var, mv_made)
            if f is not None:
                split_hidden(f, par, 0)
            if c is not None:
                dve.wait_ge(out_mm, c + 1)
                ge(dve, stored[par], loads(c, par) - 16)
                nc.vector.tensor_tensor(result[:, par, :], ps[:, 6, :],
                                        x_res[:, bass.ds(c * T, T), :].rearrange("p t f -> p (t f)"), ALU.add).then_inc(result_made, 1)
            if ahead is not None:
                normalise(ahead)
            for q in (range(1, PAIRS) if f is not None else ()):
                split_hidden(f, par, q)
            if ahead is not None:
                split_x2(ahead)

        norm_stats(nc, x_res, 0, stats, stats_made)
        clear_weights(0)
        dve.wait_ge(stats_made, T)
        norm_moments(nc, stats, mean_var, mv_made)
        weights_low(0)
        normalise(0)
        clear_weights(1)
        split_x2(0)
        weights_low(1)
        turns(turn, dve, 3)

    @block.tensor
    def _(pe):
        PASSES = ((0, 0), (0, 1), (1, 0))

        def norm_transposed(n):
            pe.wait_ge(xhat_made, T * (n + 1))
            ge(pe, x2_out, C2 * n)
            for tt in range(T):
                for k in range(C2):
                    mm = nc.tensor.transpose(halves(ps, 0)[:, k, tt * P:(tt + 1) * P], x_hat[:, tt, k * P:(k + 1) * P], ident[:])
            mm.then_inc(xt_mm, 1)

        def hidden_of(f, m):
            if m == 0:
                pe.wait_ge(x2_high, f + 1)
                pe.wait_ge(x2_low, f + 1)
            if m % 2 == 0:
                ge(pe, gelu_made, DT * (f - 1) + m + 2)
            for k in range(C2):
                for i, j in PASSES:
                    mm = nc.tensor.matmul(halves(ps, 1 + m // 2)[:, m % 2, :], w1_parts[i][:, k, m * P:(m + 1) * P],
                                          x2_parts[j][:, k, :], start=(k == 0 and i + j == 0), stop=(k == C2 - 1 and i == 1))
            if m % 2 == 1:
                mm.then_inc(fc1_mm, 1)

        def output(b, par):
            if isinstance(b, int) and b == 0:
                pe.wait_ge(w_high, 2)
                pe.wait_ge(w_low, 2)
            pe.wait_ge(h_high, PAIRS * (b + 1))
            pe.wait_ge(h_low, PAIRS * (b + 1))
            ge(pe, outT_made, C2 * b)
            for k in range(C2):
                for m in range(DT):
                    for i, j in PASSES:
                        mm = nc.tensor.matmul(halves(ps, 5)[:, k, :], w2_parts[i][:, m, k * P:(k + 1) * P],
                                              hidden_parts[j][:, par, m, :], start=(m == 0 and i + j == 0),
                                              stop=(m == DT - 1 and i == 1))
            mm.then_inc(fc2_mm, 1)

        def back_to_tokens(c):
            pe.wait_ge(outT_made, C2 * (c + 1))
            ge(pe, result_made, c)
            for tt in range(T):
                for k in range(C2):
                    mm = nc.tensor.transpose(ps[:, 6, (C2 * tt + k) * P:(C2 * tt + k + 1) * P], outT[:, k, tt * P:(tt + 1) * P],
                                             ident[:])
            mm.then_inc(out_mm, 1)

        def turn(f, b, c, par):
            for m in range(DT):
                if f is not None:
                    hidden_of(f, m)
                if c is not None and m == 3:
                    back_to_tokens(c)
            if following(f) is not None:
                norm_transposed(following(f))
            if b is not None:
                output(b, 1 - par)

        norm_transposed(0)
        pe.wait_ge(w_high, 1)
        pe.wait_ge(w_low, 1)
        turns(turn, pe, 3)


def kernel(x, cond_1024, mask_BxSxSx11_ik0, L0_cond_W_self, L0_cond_b_self, L0_cond_w_bias, L0_cond_b_bias, L0_cond_Wq,
           L0_cond_bq, L0_cond_Wk, L0_cond_bk, L0_cond_Wout, L0_cond_bout, L1_cond_mat_qkv_w, L1_cond_q_bias,
           L1_cond_v_bias, L1_cond_scale_mul, L1_cond_proj_w, L1_cond_proj_b, L1_cond_ada_w, L1_cond_ada_b, L1_cond_fc1_w,
           L1_cond_fc1_b, L1_cond_fc2_w, L1_cond_fc2_b):
    import numpy as np
    import concourse.bacc as bacc
    from concourse.bass_utils import run_bass_kernel_spmd

    def columns(a):
        a = np.asarray(a)
        return np.moveaxis(a.reshape(*a.shape[:-1], a.shape[-1] // P, P), -1, 0)

    flat = np.asarray(x).reshape(B * N, F)
    mask = np.asarray(mask_BxSxSx11_ik0)
    adj = np.stack([mask[:, :, :M, :], np.swapaxes(mask[:, :M, :, :], 1, 2)], axis=2)
    arrays = {
        "x": flat, "xT": flat.T, "adj": adj.reshape(B * N, 2 * M * L), "condT": np.asarray(cond_1024).T,
        "w_selfT": np.asarray(L0_cond_W_self).T, "b_self": columns(L0_cond_b_self),
        "w_label": L0_cond_w_bias, "b_label": np.asarray(L0_cond_b_bias).reshape(1),
        "w_qT": np.swapaxes(L0_cond_Wq, 1, 2), "b_q": columns(L0_cond_bq), "w_kT": np.swapaxes(L0_cond_Wk, 1, 2), "b_k": columns(L0_cond_bk),
        "w_oT": np.swapaxes(np.asarray(L0_cond_Wout).reshape(2, F, F), 1, 2), "b_out": columns(L0_cond_bout),
        "w_qkvT": np.asarray(L1_cond_mat_qkv_w).T, "b_qkv_q": L1_cond_q_bias, "b_v": columns(L1_cond_v_bias),
        "scale_mul": np.asarray(L1_cond_scale_mul).reshape(H), "w_projT": np.asarray(L1_cond_proj_w).T,
        "b_proj": columns(L1_cond_proj_b), "w_adaT": np.asarray(L1_cond_ada_w).T, "b_ada": columns(L1_cond_ada_b),
        "w_fc1T": np.asarray(L1_cond_fc1_w).T, "b_fc1": columns(L1_cond_fc1_b), "w_fc2T": np.asarray(L1_cond_fc2_w).T,
        "b_fc2": columns(L1_cond_fc2_b),
    }
    nc = bacc.Bacc("TRN2", target_bir_lowering=False, num_devices=1)
    sent, tensors = {}, {}
    for name, a in arrays.items():
        a = np.ascontiguousarray(a)
        sent[f"in_{name}"] = a
        tensors[name] = nc.dram_tensor(f"in_{name}", a.shape, mybir.dt.from_np(a.dtype), kind="ExternalInput").ap()
    tensors["out"] = nc.dram_tensor("out_x", (B * N, F), F32, kind="ExternalOutput").ap()
    build(nc, tensors)
    ran = run_bass_kernel_spmd(nc, [sent], core_ids=[0])
    return ran.results[0]["out_x"].reshape(B, N, F)
```
